# Optimizing a Trainium2 kernel written in Bass

```python
import numpy as np
import jax
import jax.numpy as jnp

def _softmax(x, axis=-1):
    return jax.nn.softmax(x, axis=axis)

def _gelu(x):
    return jax.nn.gelu(x, approximate=True)

def _silu(x):
    return jax.nn.silu(x)

def _sigmoid(x):
    return jax.nn.sigmoid(x)

def _layernorm(x, axis=-1, eps=1e-05):
    m = jnp.mean(x, axis=axis, keepdims=True)
    v = jnp.var(x, axis=axis, keepdims=True)
    return (x - m) / jnp.sqrt(v + eps)

def _scatter_add(tgt, idx, src, axis=0):
    return tgt.at[idx].add(src)

def _segment_sum(src, seg, n):
    return jax.ops.segment_sum(src, seg, n)
kernel_name = 'mk_gnn_preln_d4_gnn_r32_8bf77c'

def setup_inputs(seed: int=0):
    np.random.seed(seed)
    _w = jnp.asarray

    def _rec_inputs():
        import jax
        import jax.numpy as jnp
        _gk = jax.random.key(seed)
        x = -0.000202 + 1 * jax.random.normal(jax.random.fold_in(_gk, 1), (3125, 64), jnp.float32)
        _s = jax.random.randint(jax.random.fold_in(_gk, 2), (50000,), 0, 3125, jnp.int32)
        _d = jax.random.randint(jax.random.fold_in(_gk, 3), (50000,), 0, 3125, jnp.int32)
        _loop = jnp.arange(3125, dtype=jnp.int32)
        src = jnp.concatenate([_s, _d, _loop])
        dst = jnp.concatenate([_d, _s, _loop])
        _o = jnp.argsort(dst, stable=True)
        src = src[_o]
        dst = dst[_o]
        edge_type_4 = jax.random.randint(jax.random.fold_in(_gk, 12), (103125,), 0, 4, jnp.int32)
        edge_type_8 = jax.random.randint(jax.random.fold_in(_gk, 13), (103125,), 0, 8, jnp.int32)
        return (x, src, dst, edge_type_4, edge_type_8)
    x, src, dst, edge_type_4, edge_type_8 = _rec_inputs()

    def _L0_gnn_setup():
        import jax, jax.numpy as jnp
        import numpy as np
        N_NODES = 3125
        N_EDGES = 25000
        D = 64
        BN_EPS = 1e-05

        def _gin_aggregate(x, src, dst):
            msgs = x[src]
            agg = jax.ops.segment_sum(msgs, dst, num_segments=N_NODES)
            return x + agg

        def _batchnorm(h, gamma, beta):
            mean = jnp.mean(h, axis=0)
            var = jnp.var(h, axis=0)
            return (h - mean) * jax.lax.rsqrt(var + BN_EPS) * gamma + beta
        key = jax.random.key(seed)
        ks = jax.random.split(key, 8)
        x = jax.random.normal(ks[0], (N_NODES, D), dtype=jnp.float32)
        edge_index = jax.random.randint(ks[1], (2, N_EDGES), 0, N_NODES, dtype=jnp.int32)
        s = 1.0 / np.sqrt(D)
        W1 = jax.random.uniform(ks[2], (D, D), jnp.float32, -s, s)
        b1 = jnp.zeros((D,), jnp.float32)
        gamma1 = jnp.ones((D,), jnp.float32)
        beta1 = jnp.zeros((D,), jnp.float32)
        W2 = jax.random.uniform(ks[3], (D, D), jnp.float32, -s, s)
        b2 = jnp.zeros((D,), jnp.float32)
        return {'x': x, 'edge_index': edge_index, 'W1': W1, 'b1': b1, 'gamma1': gamma1, 'beta1': beta1, 'W2': W2, 'b2': b2}
    _L0_gnn_all = _L0_gnn_setup()
    _L0_gnn_in = {k: v for k, v in _L0_gnn_all.items() if k in ('W1', 'b1', 'gamma1', 'beta1', 'W2', 'b2')}
    del _L0_gnn_all

    def _L1_gnn_setup():
        import jax, jax.numpy as jnp
        import numpy as np
        N_NODES = 3125
        N_EDGES = 31250
        D_IN = 64
        D_OUT = 64
        R = 4

        def rgcn_conv(x, W, root, b, src, dst, etype):
            H = jnp.einsum('nd,rde->rne', x, W)
            msg = H[etype, src]
            seg = etype * N_NODES + dst
            deg = jax.ops.segment_sum(jnp.ones((src.shape[0],), x.dtype), seg, num_segments=R * N_NODES)
            norm = jnp.where(deg > 0, 1.0 / jnp.maximum(deg, 1.0), 0.0)
            msg = msg * norm[seg][:, None]
            agg = jax.ops.segment_sum(msg, dst, num_segments=N_NODES)
            return agg + x @ root + b
        key = jax.random.key(seed)
        ks = jax.random.split(key, 9)
        x = jax.random.normal(ks[0], (N_NODES, D_IN), dtype=jnp.float32)
        edge_index = jax.random.randint(ks[1], (2, N_EDGES), 0, N_NODES, dtype=jnp.int64)
        edge_type = jax.random.randint(ks[2], (N_EDGES,), 0, R, dtype=jnp.int64)
        s1 = 1.0 / np.sqrt(D_IN)
        s2 = 1.0 / np.sqrt(D_OUT)
        W1 = jax.random.uniform(ks[3], (R, D_IN, D_OUT), jnp.float32, -s1, s1)
        root1 = jax.random.uniform(ks[4], (D_IN, D_OUT), jnp.float32, -s1, s1)
        b1 = jnp.zeros((D_OUT,), jnp.float32)
        W2 = jax.random.uniform(ks[5], (R, D_OUT, D_OUT), jnp.float32, -s2, s2)
        root2 = jax.random.uniform(ks[6], (D_OUT, D_OUT), jnp.float32, -s2, s2)
        b2 = jnp.zeros((D_OUT,), jnp.float32)
        return {'x': x, 'W1': W1, 'root1': root1, 'b1': b1, 'W2': W2, 'root2': root2, 'b2': b2, 'edge_index': edge_index, 'edge_type': edge_type}
    _L1_gnn_all = _L1_gnn_setup()
    _L1_gnn_in = {k: v for k, v in _L1_gnn_all.items() if k in ('W1', 'root1', 'b1', 'W2', 'root2', 'b2')}
    del _L1_gnn_all

    def _L2_gnn_setup():
        import jax, jax.numpy as jnp
        import numpy as np
        N_NODES = 50000
        N_EDGES = 25000
        IN_DIM = 64
        OUT_DIM = 64
        N_REL = 8
        N_RULES = 32
        N_ACTIVE = 4
        LN_EPS = 1e-05

        def _seg_softmax(scores, seg, num_segments):
            m = jax.ops.segment_max(scores, seg, num_segments=num_segments)
            e = jnp.exp(scores - m[seg])
            d = jax.ops.segment_sum(e, seg, num_segments=num_segments)
            return e / d[seg]
        key = jax.random.key(seed)
        ks = jax.random.split(key, 12)
        x = jax.random.normal(ks[0], (N_NODES, IN_DIM), dtype=jnp.float32)
        edge_index = jax.random.randint(ks[1], (2, N_EDGES), 0, N_NODES, dtype=jnp.int64)
        edge_type = jax.random.randint(ks[2], (N_EDGES,), 0, N_REL, dtype=jnp.int64)
        rule_ids = jax.random.randint(ks[3], (N_ACTIVE,), 0, N_RULES, dtype=jnp.int64)
        W_r = jax.random.normal(ks[4], (N_REL, IN_DIM, OUT_DIM), dtype=jnp.float32) * (2.0 / (IN_DIM + OUT_DIM)) ** 0.5
        Wq_w = jax.random.normal(ks[5], (IN_DIM, OUT_DIM), dtype=jnp.float32) * (1.0 / IN_DIM) ** 0.5
        Wq_bias = jnp.zeros((OUT_DIM,), dtype=jnp.float32)
        Wk_w = jax.random.normal(ks[6], (3 * IN_DIM, OUT_DIM), dtype=jnp.float32) * (1.0 / (3 * IN_DIM)) ** 0.5
        Wk_bias = jnp.zeros((OUT_DIM,), dtype=jnp.float32)
        rule_emb = jax.random.normal(ks[7], (N_RULES, IN_DIM), dtype=jnp.float32) * (2.0 / (N_RULES + IN_DIM)) ** 0.5
        bias = jnp.zeros((OUT_DIM,), dtype=jnp.float32)
        ln_g = jnp.ones((OUT_DIM,), dtype=jnp.float32)
        ln_b = jnp.zeros((OUT_DIM,), dtype=jnp.float32)
        return {'x': x, 'edge_index': edge_index, 'edge_type': edge_type, 'rule_ids': rule_ids, 'W_r': W_r, 'Wq_w': Wq_w, 'Wq_bias': Wq_bias, 'Wk_w': Wk_w, 'Wk_bias': Wk_bias, 'rule_emb': rule_emb, 'bias': bias, 'ln_g': ln_g, 'ln_b': ln_b}
    _L2_gnn_all = _L2_gnn_setup()
    _L2_gnn_in = {k: v for k, v in _L2_gnn_all.items() if k in ('rule_ids', 'W_r', 'Wq_w', 'Wq_bias', 'Wk_w', 'Wk_bias', 'rule_emb', 'bias', 'ln_g', 'ln_b')}
    del _L2_gnn_all

    def _L3_gnn_setup():
        import jax, jax.numpy as jnp
        import numpy as np
        N_NODES = 3125
        N_EDGES = 50000
        D = 64
        H = 64
        key = jax.random.key(seed)
        k1, k2, k3, k4, k5, k6 = jax.random.split(key, 6)
        x = jax.random.normal(k1, (N_NODES, D), dtype=jnp.float32)
        edge_index = jax.random.randint(k2, (2, N_EDGES), 0, N_NODES, dtype=jnp.int64)
        s1 = 1.0 / np.sqrt(2 * D)
        s2 = 1.0 / np.sqrt(H)
        W1 = jax.random.uniform(k3, (H, 2 * D), dtype=jnp.float32, minval=-s1, maxval=s1)
        b1 = jax.random.uniform(k4, (H,), dtype=jnp.float32, minval=-s1, maxval=s1)
        W2 = jax.random.uniform(k5, (D, H), dtype=jnp.float32, minval=-s2, maxval=s2)
        b2 = jax.random.uniform(k6, (D,), dtype=jnp.float32, minval=-s2, maxval=s2)
        return {'x': x, 'W1': W1, 'b1': b1, 'W2': W2, 'b2': b2, 'edge_index': edge_index}
    _L3_gnn_all = _L3_gnn_setup()
    _L3_gnn_in = {k: v for k, v in _L3_gnn_all.items() if k in ('W1', 'b1', 'W2', 'b2')}
    del _L3_gnn_all
    return {'x': x, 'src': src, 'dst': dst, 'edge_type_4': edge_type_4, 'edge_type_8': edge_type_8, 'L0_gnn_W1': _L0_gnn_in['W1'], 'L0_gnn_b1': _L0_gnn_in['b1'], 'L0_gnn_gamma1': _L0_gnn_in['gamma1'], 'L0_gnn_beta1': _L0_gnn_in['beta1'], 'L0_gnn_W2': _L0_gnn_in['W2'], 'L0_gnn_b2': _L0_gnn_in['b2'], 'L1_gnn_W1': _L1_gnn_in['W1'], 'L1_gnn_root1': _L1_gnn_in['root1'], 'L1_gnn_b1': _L1_gnn_in['b1'], 'L1_gnn_W2': _L1_gnn_in['W2'], 'L1_gnn_root2': _L1_gnn_in['root2'], 'L1_gnn_b2': _L1_gnn_in['b2'], 'L2_gnn_rule_ids': _L2_gnn_in['rule_ids'], 'L2_gnn_W_r': _L2_gnn_in['W_r'], 'L2_gnn_Wq_w': _L2_gnn_in['Wq_w'], 'L2_gnn_Wq_bias': _L2_gnn_in['Wq_bias'], 'L2_gnn_Wk_w': _L2_gnn_in['Wk_w'], 'L2_gnn_Wk_bias': _L2_gnn_in['Wk_bias'], 'L2_gnn_rule_emb': _L2_gnn_in['rule_emb'], 'L2_gnn_bias': _L2_gnn_in['bias'], 'L2_gnn_ln_g': _L2_gnn_in['ln_g'], 'L2_gnn_ln_b': _L2_gnn_in['ln_b'], 'L3_gnn_W1': _L3_gnn_in['W1'], 'L3_gnn_b1': _L3_gnn_in['b1'], 'L3_gnn_W2': _L3_gnn_in['W2'], 'L3_gnn_b2': _L3_gnn_in['b2']}

def reference(x, src, dst, edge_type_4, edge_type_8, L0_gnn_W1, L0_gnn_b1, L0_gnn_gamma1, L0_gnn_beta1, L0_gnn_W2, L0_gnn_b2, L1_gnn_W1, L1_gnn_root1, L1_gnn_b1, L1_gnn_W2, L1_gnn_root2, L1_gnn_b2, L2_gnn_rule_ids, L2_gnn_W_r, L2_gnn_Wq_w, L2_gnn_Wq_bias, L2_gnn_Wk_w, L2_gnn_Wk_bias, L2_gnn_rule_emb, L2_gnn_bias, L2_gnn_ln_g, L2_gnn_ln_b, L3_gnn_W1, L3_gnn_b1, L3_gnn_W2, L3_gnn_b2):
    import jax
    import jax.numpy as jnp

    def _L0_gnn_ref(x, edge_index, W1, b1, gamma1, beta1, W2, b2):
        import jax, jax.numpy as jnp
        import numpy as np
        N_NODES = 3125
        N_EDGES = 25000
        D = 64
        BN_EPS = 1e-05

        def _gin_aggregate(x, src, dst):
            msgs = x[src]
            agg = jax.ops.segment_sum(msgs, dst, num_segments=N_NODES)
            return x + agg

        def _batchnorm(h, gamma, beta):
            mean = jnp.mean(h, axis=0)
            var = jnp.var(h, axis=0)
            return (h - mean) * jax.lax.rsqrt(var + BN_EPS) * gamma + beta
        src = edge_index[0]
        dst = edge_index[1]
        h = _gin_aggregate(x, src, dst) @ W1 + b1
        h = jax.nn.relu(_batchnorm(h, gamma1, beta1))
        out = _gin_aggregate(h, src, dst) @ W2 + b2
        return out

    def _L1_gnn_ref(x, W1, root1, b1, W2, root2, b2, edge_index, edge_type):
        import jax, jax.numpy as jnp
        import numpy as np
        N_NODES = 3125
        N_EDGES = 31250
        D_IN = 64
        D_OUT = 64
        R = 4

        def rgcn_conv(x, W, root, b, src, dst, etype):
            H = jnp.einsum('nd,rde->rne', x, W)
            msg = H[etype, src]
            seg = etype * N_NODES + dst
            deg = jax.ops.segment_sum(jnp.ones((src.shape[0],), x.dtype), seg, num_segments=R * N_NODES)
            norm = jnp.where(deg > 0, 1.0 / jnp.maximum(deg, 1.0), 0.0)
            msg = msg * norm[seg][:, None]
            agg = jax.ops.segment_sum(msg, dst, num_segments=N_NODES)
            return agg + x @ root + b
        src, dst = (edge_index[0], edge_index[1])
        h = rgcn_conv(x, W1, root1, b1, src, dst, edge_type)
        h = jax.nn.relu(h)
        out = rgcn_conv(h, W2, root2, b2, src, dst, edge_type)
        return out

    def _L2_gnn_ref(x, edge_index, edge_type, rule_ids, W_r, Wq_w, Wq_bias, Wk_w, Wk_bias, rule_emb, bias, ln_g, ln_b):
        import jax, jax.numpy as jnp
        import numpy as np
        N_NODES = 50000
        N_EDGES = 25000
        IN_DIM = 64
        OUT_DIM = 64
        N_REL = 8
        N_RULES = 32
        N_ACTIVE = 4
        LN_EPS = 1e-05

        def _seg_softmax(scores, seg, num_segments):
            m = jax.ops.segment_max(scores, seg, num_segments=num_segments)
            e = jnp.exp(scores - m[seg])
            d = jax.ops.segment_sum(e, seg, num_segments=num_segments)
            return e / d[seg]
        src, dst = (edge_index[0], edge_index[1])
        num_nodes, in_dim = x.shape
        num_rel, _, out_dim = W_r.shape
        x_src = x[src]
        q = x[dst] @ Wq_w + Wq_bias
        rel_emb = W_r.mean(axis=-1)[edge_type]
        Wk1, Wk2, Wk3 = (Wk_w[:in_dim], Wk_w[in_dim:2 * in_dim], Wk_w[2 * in_dim:])
        key_base = x_src @ Wk1 + rel_emb @ Wk2 + Wk_bias
        h_R = rule_emb[rule_ids]
        key_rule = h_R @ Wk3
        scale = 1.0 / out_dim ** 0.5
        score_base = jnp.einsum('eo,eo->e', q, key_base)
        score_rule = jnp.einsum('eo,ro->er', q, key_rule)
        scores = (score_base[:, None] + score_rule) * scale
        attn = jax.vmap(lambda s: _seg_softmax(s, dst, num_nodes), in_axes=1, out_axes=1)(scores)
        mean_attn = attn.mean(axis=1)
        msg = jnp.zeros((x_src.shape[0], out_dim), dtype=x.dtype)
        for r in range(num_rel):
            msg = jnp.where((edge_type == r)[:, None], x_src @ W_r[r], msg)
        out = jax.ops.segment_sum(msg * mean_attn[:, None], dst, num_segments=num_nodes)
        out = out + bias
        mu = out.mean(axis=-1, keepdims=True)
        var = ((out - mu) ** 2).mean(axis=-1, keepdims=True)
        out = (out - mu) * jax.lax.rsqrt(var + LN_EPS) * ln_g + ln_b
        return jax.nn.relu(out)

    def _L3_gnn_ref(x, W1, b1, W2, b2, edge_index):
        import jax, jax.numpy as jnp
        import numpy as np
        N_NODES = 3125
        N_EDGES = 50000
        D = 64
        H = 64
        src = edge_index[0]
        dst = edge_index[1]
        xi = x[dst]
        xj = x[src]
        m = jnp.concatenate([xi, xj - xi], axis=-1)
        h = jax.nn.relu(m @ W1.T + b1)
        e = h @ W2.T + b2
        agg = jax.ops.segment_max(e, dst, num_segments=x.shape[0])
        return jnp.where(jnp.isneginf(agg), jnp.float32(0.0), agg)
    edge_index = jnp.stack([src, dst])
    h = jnp.maximum(_layernorm(x, axis=-1), 0.0)
    x = x + _L0_gnn_ref(h, edge_index, L0_gnn_W1, L0_gnn_b1, L0_gnn_gamma1, L0_gnn_beta1, L0_gnn_W2, L0_gnn_b2)
    h = jnp.maximum(_layernorm(x, axis=-1), 0.0)
    x = x + _L1_gnn_ref(h, L1_gnn_W1, L1_gnn_root1, L1_gnn_b1, L1_gnn_W2, L1_gnn_root2, L1_gnn_b2, edge_index, edge_type_4)
    h = jnp.maximum(_layernorm(x, axis=-1), 0.0)
    x = x + _L2_gnn_ref(h, edge_index, edge_type_8, L2_gnn_rule_ids, L2_gnn_W_r, L2_gnn_Wq_w, L2_gnn_Wq_bias, L2_gnn_Wk_w, L2_gnn_Wk_bias, L2_gnn_rule_emb, L2_gnn_bias, L2_gnn_ln_g, L2_gnn_ln_b)
    h = jnp.maximum(_layernorm(x, axis=-1), 0.0)
    x = x + _L3_gnn_ref(h, L3_gnn_W1, L3_gnn_b1, L3_gnn_W2, L3_gnn_b2, edge_index)
    return x

_drawn_inputs = setup_inputs


def setup_inputs(seed=0):
    import zlib

    import numpy as np

    out = dict(_drawn_inputs(seed))
    spreads = {'L0_gnn_b1': (0.0, 2.0),
     'L0_gnn_gamma1': (1.0, 0.2),
     'L0_gnn_beta1': (0.0, 0.1),
     'L0_gnn_b2': (0.0, 0.8),
     'L1_gnn_b1': (0.0, 0.8),
     'L1_gnn_b2': (0.0, 0.664),
     'L2_gnn_Wq_bias': (0.0, 2.0),
     'L2_gnn_Wk_bias': (0.0, 2.0),
     'L2_gnn_bias': (0.0, 0.358),
     'L2_gnn_ln_g': (1.0, 0.6),
     'L2_gnn_ln_b': (0.0, 0.8)}
    factors = {'L2_gnn_Wq_w': 8.0,
     'L2_gnn_Wk_w': 8.0,
     'L2_gnn_rule_emb': 200.0,
     'L3_gnn_W1': 6.481,
     'L3_gnn_b1': 8.0,
     'L3_gnn_W2': 4.834,
     'L3_gnn_b2': 6.636}
    for name, (base, spread) in spreads.items():
        noise = np.random.default_rng([zlib.crc32(name.encode()), seed]).standard_normal(out[name].shape)
        drawn = base * np.exp(spread * noise) if base else spread * noise
        out[name] = jnp.asarray(drawn.astype(out[name].dtype))
    for name, factor in factors.items():
        out[name] = (out[name] * factor).astype(out[name].dtype)
    return out
```

```python
from contextlib import ExitStack

import concourse.bass as bass
from concourse import mybir

F32 = mybir.dt.float32
BF16 = mybir.dt.bfloat16
I32 = mybir.dt.int32
ALU = mybir.AluOpType
ACT = mybir.ActivationFunctionType
AX = mybir.AxisListType

N = 3125
D = 64
NP = 125
NK = N // NP
E = 103125
BLK = 512
CPB = BLK // 128
BODY = 12
TURNS = -(-E // (BLK * BODY))
NB = TURNS * BODY
EP = NB * BLK
GRP = 4
NG = NB // GRP
GC = GRP * CPB
PCS = TURNS
PL = EP // PCS
PQ = 4 * PCS
R4, R8 = 4, 8
RW = D + R8 + 4
ZROW = EP
BIG = 3.3e38
HEADS = EP // 128
EPS = 1e-5
CH = 500
CHUNKS = [(a, min(CH, N - a)) for a in range(0, N, CH)]


def build(nc, A, out, dbg=None):
    with ExitStack() as ctx:
        def sb(name, shape, dt=F32):
            return ctx.enter_context(nc.sbuf_tensor(name, shape, dt))

        def dram(name, shape, dt=F32):
            return nc.dram_tensor(name, shape, dt, kind="ExternalOutput" if dbg else "Internal").ap()

        def sem(name):
            return ctx.enter_context(nc.semaphore(name))

        hold_d = dram("hold_d", [EP], BF16)
        cap_d = dram("cap_d", [EP], BF16)
        ends_d = dram("ends_d", [N + 1], F32)
        idx4_d = dram("idx4_d", [NG, 128, GC], I32)
        idx8_d = dram("idx8_d", [NG, 128, GC], I32)
        norm_d = dram("norm_d", [NG, 128, GC])
        att_d = dram("att_d", [NG, 128, GC])
        scan_d = dram("scan_d", [EP + 1, D])
        tab_d = dram("tab_d", [N, D])
        tab4_d = dram("tab4_d", [R4 * N, D])
        tab8_d = dram("tab8_d", [R8 * N, 2 * D])
        spread_d = dram("spread_d", [EP + N, RW])
        msg_d = dram("msg_d", [EP + 1, D])
        score_d = dram("score_d", [4, EP])

        PA = sb("PA", [128, 6400])
        PB = sb("PB", [128, 6400])
        PC = sb("PC", [128, 6400])
        same_prev = sb("same_prev", [PQ, PL], BF16)
        same_next = sb("same_next", [PQ, PL], BF16)
        last_of_run = sb("last_of_run", [PQ, PL], BF16)
        ident = sb("ident", [128, 128])
        iota8 = sb("iota8", [128, R8])
        ones = sb("ones", [128, 4])
        end_idx = sb("end_idx", [NP, NK], I32)
        start_idx = sb("start_idx", [NP, NK], I32)
        nonempty = sb("nonempty", [NP, NK])
        xn = sb("xn", [NP, NK, D])
        hn = sb("hn", [NP, NK, D])
        rn = sb("rn", [NP, NK, D])
        gn = sb("gn", [NP, NK, D])
        small = sb("small", [128, 8, 32])
        fold = sb("fold", [PQ, PCS])
        srow = sb("srow", [1, 4, PQ + 1])
        scol = sb("scol", [PQ, 4])
        G = sb("G", [128, 4, CPB, 2 * D + RW - D])
        GS = sb("GS", [128, 2, CPB, D])
        EX = sb("EX", [128, 3, CPB, RW])
        idx = sb("idx", [128, 3, GC], I32)
        aux = sb("aux", [128, 3, GC])
        auxi = sb("auxi", [128, 3, GC], I32)
        hold = sb("hold", [RW, 3, BLK], BF16)
        cap = sb("cap", [D, 3, BLK], BF16)
        held = sb("held", [RW, 2, BLK])
        prod = sb("prod", [RW, 2, BLK])
        act_sb = sb("act_sb", [D, 2, BLK])
        run = sb("run", [D, 2, BLK])
        O = sb("O", [128, 4, CPB, D])
        sc_sb = sb("sc_sb", [4, 4, BLK])
        w0a = sb("w0a", [D, D]); w0b = sb("w0b", [D, D])
        w1a = sb("w1a", [D, R4 + 1, D]); w1b = sb("w1b", [D, R4 + 1, D])
        w2r = sb("w2r", [D, R8, D])
        wq = sb("wq", [D, D]); wk = sb("wk", [D, 3, D]); m2 = sb("m2", [D, RW])
        w3 = sb("w3", [D, 2 * D]); w3t = sb("w3t", [D, 2, D]); w3b = sb("w3b", [D, D]); w3bt = sb("w3bt", [D, D])
        emb = sb("emb", [4, D]); embT = sb("embT", [D, 4]); relT = sb("relT", [D, R8]); rid = sb("rid", [4, 1], I32)
        cols = sb("cols", [D, 8])
        rows = sb("rows", [NP, 8, D])
        w4 = sb("w4", [RW, 4])
        zero_row = sb("zero_row", [1, D])
        bn = sb("bn", [D, len(CHUNKS), 6]); bnm = sb("bnm", [D, 2]); bnc = sb("bnc", [D, 4])

        ps = [ctx.enter_context(nc.psum_tensor(f"ps{i}", [128, 512], F32)) for i in range(8)]

        armed = sem("armed")

        class Line:
            def __init__(self, name):
                self.s, self.n = sem(name), 0

            def step(self, eng, ins, by=1):
                self.n += by
                ins.then_inc(self.s, by)
                eng.wait_ge(self.s, self.n)

        dve_line, pool_line, act_line, sp_line, pe_line = (
            Line(n) for n in ("dve_line", "pool_line", "act_line", "sp_line", "pe_line"))

        def bcast(ap, n):
            return ap.unsqueeze(len(ap.shape)).to_broadcast(list(ap.shape) + [n])

        def row_bcast(v, parts, n):
            return bass.AP(tensor=v.tensor, offset=v.offset, ap=[[0, parts], [1, n]])

        node = lambda d: d.rearrange("(p k) f -> p k f", p=NP)
        P_ = lambda t: t[:, :]

        loaded = sem("loaded")
        n_loads = [0]
        iot = sem("iot")
        with nc.Block() as block:
            @block.sync
            def _(sp):
                def ld(dst, src):
                    sp.dma_start(dst, src).then_inc(loaded, 16)
                    n_loads[0] += 16
                ld(xn[:, :, :], node(A["x"]))
                ld(P_(w0a), A["L0_gnn_W1"]); ld(P_(w0b), A["L0_gnn_W2"])
                for w, nm, rt in ((w1a, "L1_gnn_W1", "L1_gnn_root1"), (w1b, "L1_gnn_W2", "L1_gnn_root2")):
                    ld(w[:, 0:R4, :], A[nm].rearrange("r d e -> d r e"))
                    ld(w[:, R4, :], A[rt])
                ld(w2r[:, :, :], A["L2_gnn_W_r"].rearrange("r d e -> d r e"))
                ld(P_(wq), A["L2_gnn_Wq_w"])
                ld(wk[:, :, :], A["L2_gnn_Wk_w"].rearrange("(a d) e -> d a e", a=3))
                ld(P_(w3), A["L3_gnn_W1"]); ld(P_(w3b), A["L3_gnn_W2"])
                ld(P_(rid), A["rule_ids"])
                for j, nm in enumerate(("L0_gnn_b1", "L0_gnn_gamma1", "L0_gnn_beta1", "L2_gnn_Wq_bias", "L2_gnn_Wk_bias")):
                    ld(cols[:, j:j + 1], A[nm])
                for j, nm in enumerate(("L0_gnn_b2", "L1_gnn_b1", "L1_gnn_b2", "L2_gnn_bias", "L2_gnn_ln_g", "L2_gnn_ln_b", "L3_gnn_b1", "L3_gnn_b2")):
                    ld(rows[:, j, :], row_bcast(A[nm], NP, D))
                sp.wait_ge(loaded, n_loads[0])

            @block.gpsimd
            def _(g):
                L = pool_line
                L.step(g, g.iota(PA[:, 0:128].bitcast(I32), [[1, 128]], base=0, channel_multiplier=0))
                L.step(g, g.iota(PA[:, 128:129].bitcast(I32), [[0, 1]], base=0, channel_multiplier=1))
                L.step(g, g.iota(PA[0:NP, 256:256 + NK].bitcast(I32), [[1, NK]], base=0, channel_multiplier=NK))
                g.sem_inc(iot, 1)

            @block.vector
            def _(v):
                L = dve_line
                v.wait_ge(iot, 1)
                L.step(v, v.tensor_copy(PB[:, 0:129], PA[:, 0:129].bitcast(I32)))
                L.step(v, v.tensor_scalar(ident[:, :], PB[:, 0:128], PB[:, 128:129], None, ALU.is_equal))
                L.step(v, v.tensor_copy(P_(iota8), PB[:, 0:R8]))
                L.step(v, v.memset(P_(ones), 1.0))
                L.step(v, v.memset(P_(zero_row), 0.0))
                L.step(v, v.tensor_copy(fold[:, :], ident[0:PQ, 0:PCS]))
                for t in range(1, 4):
                    L.step(v, v.tensor_tensor(fold[:, :], fold[:, :], ident[0:PQ, t * PCS:(t + 1) * PCS], ALU.add))
                L.step(v, v.memset(G[:, :, :, 2 * D + R8:], 1.0))
                L.step(v, v.memset(run[:, :, :], 0.0))
                L.step(v, v.memset(held[:, :, :], 0.0))
                L.step(v, v.memset(PC[:, :], 0.0))
                L.step(v, v.memset(w4[0:D, :], 1.0))
                L.step(v, v.tensor_copy(w4[D:RW, :], ident[D:RW, D + R8:RW]))
                L.step(v, v.tensor_scalar(small[:, 0, 0:4], ident[:, D:D + 4], 0.0, None, ALU.mult))
            @block.scalar
            def _(a):
                a.sem_inc(armed, 1)

        zfill = sem("zfill")
        with nc.Block() as block:
            @block.sync
            def _(sp):
                flat = spread_d.rearrange("a b -> (a b)")
                total = (EP + N) * RW
                step = 128 * 6400
                n = 0
                for a in range(0, total - step + 1, step):
                    sp.dma_start(flat[a:a + step].rearrange("(p f) -> p f", p=128), PC[:, :]).then_inc(zfill, 16)
                    n += 16
                rest = total % step
                if rest:
                    a = total - rest
                    w = rest // 128
                    sp.dma_start(flat[a:a + 128 * w].rearrange("(p f) -> p f", p=128), PC[:, 0:w]).then_inc(zfill, 16)
                    n += 16
                    r2 = rest - 128 * w
                    if r2:
                        sp.dma_start(flat[total - r2:total].rearrange("(p f) -> p f", p=1), PC[0:1, 0:r2]).then_inc(zfill, 16)
                        n += 16
                sp.dma_start(ends_d[0:1].rearrange("(p f) -> p f", p=1), PC[0:1, 0:1]).then_inc(zfill, 16)
                n += 16
                sp.wait_ge(zfill, n)
            @block.vector
            def _(v):
                L = dve_line
                L.step(v, v.memset(w4[0:D, :], 1.0))
                L.step(v, v.tensor_reduce(small[D:RW, 1, 0:1], ident[D:RW, D:D + R8], AX.X, ALU.add))
                L.step(v, v.tensor_tensor(w4[D:RW, :], w4[D:RW, :],
                                          small[D:RW, 1, 0:1].to_broadcast([RW - D, 4]), ALU.add))

        cur = PA[:, 0:816].bitcast(I32)
        prv = PA[:, 816:1632].bitcast(I32)
        srcs = PA[:, 1632:2448].bitcast(I32)
        t4s = PA[:, 2448:3264].bitcast(I32)
        t8s = PA[:, 3264:4080].bitcast(I32)
        heads_i = PA[:, 4080:4896].bitcast(I32)
        edge_in = sem("edge_in"); flags_up = sem("flags_up"); rows_at = sem("rows_at"); rows_in = sem("rows_in")
        ends_up = sem("ends_up"); ends_out = sem("ends_out"); ends_in = sem("ends_in"); flags_out = sem("flags_out")
        assert EP // 128 == 816
        em = lambda d: d.rearrange("g p c -> p g c")
        em3 = lambda t: t.rearrange("p (g c) -> p g c", c=GC)
        dst_rows = A["dst_rows"]
        with nc.Block() as block:
            @block.sync
            def _(sp):
                dx = A["dst_ext"]
                sp.dma_start(cur, dx[1:EP + 1].rearrange("(p f) -> p f", p=128)).then_inc(edge_in, 16)
                sp.dma_start(prv, dx[0:EP].rearrange("(p f) -> p f", p=128)).then_inc(edge_in, 16)
                sp.dma_start(em3(srcs), em(A["src_it"])).then_inc(edge_in, 16)
                sp.dma_start(em3(t4s), em(A["t4_it"])).then_inc(edge_in, 16)
                sp.dma_start(em3(t8s), em(A["t8_it"])).then_inc(edge_in, 16)
                sp.dma_start(heads_i[0:NP, :], row_bcast(A["dst_heads"], NP, HEADS)).then_inc(edge_in, 16)
                sp.wait_ge(flags_up, 1)
                hb = PB[:, 0:408].bitcast(BF16)
                cb = PB[:, 408:816].bitcast(BF16)
                sp.dma_start(hold_d.rearrange("(p f) -> p f", p=128), hb).then_inc(flags_out, 16)
                sp.dma_start(cap_d.rearrange("(p f) -> p f", p=128), cb).then_inc(flags_out, 16)
                sp.dma_start(em(idx4_d), em3(t4s)).then_inc(flags_out, 16)
                sp.dma_start(em(idx8_d), em3(t8s)).then_inc(flags_out, 16)
                sp.wait_ge(ends_up, 1)
                sp.dma_start(ends_d[1:N + 1].rearrange("(p k) -> p k", p=NP), small[0:NP, 3, 0:NK]).then_inc(ends_out, 16)
                sp.wait_ge(ends_out, 16)
                sp.dma_start(small[0:NP, 4, 0:NK], ends_d[0:N].rearrange("(p k) -> p k", p=NP)).then_inc(ends_in, 16)
                sp.wait_ge(flags_out, 64)

            @block.vector
            def _(v):
                L = dve_line
                v.wait_ge(edge_in, 96)
                hf = PB[:, 816:1632]
                L.step(v, v.tensor_tensor(hf, cur, prv, ALU.is_equal))
                L.step(v, v.tensor_copy(PB[:, 0:408].bitcast(BF16), hf))
                L.step(v, v.tensor_scalar(hf, hf, 0.5, 2.0, ALU.subtract, ALU.mult))
                L.step(v, v.tensor_scalar(PB[:, 408:816].bitcast(BF16), hf, BIG, None, ALU.mult))
                for t in (t4s, t8s):
                    L.step(v, v.tensor_scalar(PB[:, 816:1632], t, float(N), None, ALU.mult))
                    L.step(v, v.tensor_tensor(t, PB[:, 816:1632], srcs, ALU.add))
                v.sem_inc(flags_up, 1)
                nid = small[0:NP, 0, 0:NK]
                v.wait_ge(iot, 2)
                L.step(v, v.tensor_copy(nid, PA[0:NP, 5000:5000 + NK].bitcast(I32)))
                heads = PB[0:NP, 816:1632]
                L.step(v, v.tensor_copy(heads, heads_i[0:NP, :]))
                cnt = small[0:NP, 1, 0:NK]
                for k in range(NK):
                    L.step(v, v.tensor_scalar(PB[0:NP, 1632:2448], heads, nid[:, k:k + 1], 0.0, ALU.is_le, ALU.add,
                                              accum_out=cnt[:, k:k + 1]))
                rowc = small[0:NP, 2, 0:NK]
                L.step(v, v.tensor_scalar(rowc, cnt, -1.0, 0.0, ALU.add, ALU.max))
                L.step(v, v.tensor_copy(small[0:NP, 5, 0:NK].bitcast(I32), rowc))
                v.sem_inc(rows_at, 1)
                v.wait_ge(rows_in, 16 * NK)
                drows = PC[0:NP, 0:NK * 128].bitcast(I32).rearrange("p (k c) -> p k c", c=128)
                le = PB[0:NP, 2448:2448 + NK * 128].rearrange("p (k c) -> p k c", c=128)
                L.step(v, v.tensor_tensor(le, drows, bcast(nid, 128), ALU.is_le))
                L.step(v, v.tensor_reduce(cnt, le, AX.X, ALU.add))
                end = small[0:NP, 3, 0:NK]
                L.step(v, v.scalar_tensor_tensor(end, rowc, 128.0, cnt, ALU.mult, ALU.add))
                v.sem_inc(ends_up, 1)
                v.wait_ge(ends_in, 16)
                start = small[0:NP, 4, 0:NK]
                tmp = small[0:NP, 6, 0:NK]
                L.step(v, v.tensor_tensor(nonempty[:, :], end, start, ALU.is_gt))
                L.step(v, v.tensor_scalar(tmp, end, -1.0 - ZROW, None, ALU.add))
                L.step(v, v.tensor_tensor(tmp, tmp, nonempty[:, :], ALU.mult))
                L.step(v, v.tensor_scalar(tmp, tmp, float(ZROW), None, ALU.add))
                L.step(v, v.tensor_copy(end_idx[:, :], tmp))
                L.step(v, v.tensor_scalar(tmp, nid, float(EP), None, ALU.add))
                L.step(v, v.tensor_tensor(start, start, tmp, ALU.subtract))
                L.step(v, v.tensor_tensor(start, start, nonempty[:, :], ALU.mult))
                L.step(v, v.tensor_tensor(start, start, tmp, ALU.add))
                L.step(v, v.tensor_copy(start_idx[:, :], start))

            @block.gpsimd
            def _(g):
                L = pool_line
                L.step(g, g.iota(PA[0:NP, 5000:5000 + NK].bitcast(I32), [[1, NK]], base=0, channel_multiplier=NK))
                g.sem_inc(iot, 1)
                g.wait_ge(rows_at, 1)
                for k in range(NK):
                    g.indirect_dma_start(PC[0:NP, k * 128:(k + 1) * 128].bitcast(I32), None, dst_rows,
                                         bass.IndirectOffsetOnAxis(ap=small[0:NP, 5, k:k + 1].bitcast(I32), axis=0)
                                         ).then_inc(rows_in, 16)
                g.wait_ge(rows_in, 16 * NK)

        tp = sem("tp"); tpn = [0]

        def flip(v, pe_todo, col, row, back=False):
            pass

        carry_req = sem("carry_req"); carry_row = sem("carry_row"); carry_back = sem("carry_back"); carry_col = sem("carry_col")
        carries = [0]

        def scan_pieces(v, dst, flag, flag_min, val, op0, op1, rest, back):
            L = dve_line
            w = slice(None, None, -1) if back else slice(None)
            far = 0 if back else PL - 1
            L.step(v, v.tensor_tensor_scan(dst[:, w], flag[:, w], val[:, w], rest, op0, op1))
            L.step(v, v.tensor_copy(scol[:, 0:1], dst[:, far:far + 1]))
            L.step(v, v.tensor_copy(scol[:, 1:2], flag_min))
            c = carries[0] = carries[0] + 1
            v.sem_inc(carry_req, 1)
            v.wait_ge(carry_row, c)
            L.step(v, v.tensor_copy(srow[:, 0, 0:PQ], ps[6][0:1, 0:PQ]))
            L.step(v, v.tensor_copy(srow[:, 1, 0:PQ], ps[6][0:1, PQ:2 * PQ]))
            L.step(v, v.memset(srow[:, 2, :], rest))
            if back:
                L.step(v, v.tensor_tensor_scan(srow[:, 2, 0:PQ][:, ::-1], srow[:, 1, 0:PQ][:, ::-1],
                                               srow[:, 0, 0:PQ][:, ::-1], rest, op0, op1))
            else:
                L.step(v, v.tensor_tensor_scan(srow[:, 2, 1:PQ + 1], srow[:, 1, 0:PQ], srow[:, 0, 0:PQ],
                                               rest, op0, op1))
            v.sem_inc(carry_back, 1)
            v.wait_ge(carry_col, c)
            L.step(v, v.tensor_copy(scol[:, 2:3], ps[7][0:PQ, 0:1]))
            L.step(v, v.tensor_tensor_scan(dst[:, w], flag[:, w], val[:, w], scol[:, 2:3], op0, op1))

        def carry_pe(pe, first, backs):
            for j, back in enumerate(backs):
                c = first + j + 1
                pe.wait_ge(carry_req, c)
                pe.matmul(ps[6][0:1, 0:PQ], scol[:, 0:1], ident[0:PQ, 0:PQ], start=True, stop=True)
                pe.matmul(ps[6][0:1, PQ:2 * PQ], scol[:, 1:2], ident[0:PQ, 0:PQ], start=True, stop=True).then_inc(carry_row, 1)
                pe.wait_ge(carry_back, c)
                init = srow[:, 2, 1:PQ + 1] if back else srow[:, 2, 0:PQ]
                pe.matmul(ps[7][0:PQ, 0:1], init, ones[0:1, 0:1], start=True, stop=True).then_inc(carry_col, 1)

        folded = sem("folded"); fold_out = sem("fold_out"); turned = sem("turned"); fold_n = [0]; emt = sem("emt")

        def fold_pe(pe, wt, src, half_ready, rowt, base):
            nchunk = PL // 512
            pe.wait_ge(half_ready, base + 1)
            for j in range(nchunk):
                if j >= 4:
                    pe.wait_ge(fold_out, base * nchunk + j - 3)
                pe.matmul(ps[j % 4][0:PCS, :], wt, src[:, 512 * j:512 * (j + 1)], start=True, stop=True).then_inc(folded, 1)
            pe.wait_ge(fold_out, (base + 1) * nchunk)
            for j in range(PL // 128):
                b, c = divmod(j, CPB)
                last = pe.transpose(ps[4 + j // 24][:, (j % 24) * PCS:(j % 24 + 1) * PCS],
                                    rowt[:, 512 * b + c:512 * (b + 1):CPB], ident[0:PCS, 0:PCS])
            last.then_inc(turned, 1)

        def fold_act(a, rowt, base):
            nchunk = PL // 512
            for j in range(nchunk):
                a.wait_ge(folded, base * nchunk + j + 1)
                a.copy(rowt[:, 512 * j:512 * (j + 1)], ps[j % 4][0:PCS, :]).then_inc(fold_out, 1)

        pin = sem("pin"); oh_in = sem("oh_in"); cnt_up = sem("cnt_up"); norm_out = sem("norm_out"); emu = sem("emu")
        with nc.Block() as block:
            @block.sync
            def _(sp):
                dx = A["dst_ext"]
                for t in range(4):
                    q = slice(t * PCS, (t + 1) * PCS)
                    for j, tile in ((1, PA), (0, PB), (2, PC)):
                        sp.dma_start(tile[q, 0:PL].bitcast(I32), dx[j:j + EP].rearrange("(i f) -> i f", i=PCS)).then_inc(pin, 16)
                sp.wait_ge(oh_in, 1)
                for t in range(4):
                    q = slice(t * PCS, (t + 1) * PCS)
                    sp.dma_start(PB[q, 0:PL].bitcast(I32), A["t4_nat"].rearrange("(i f) -> i f", i=PCS)).then_inc(oh_in, 16)
                sp.wait_ge(emu, 1)
                sp.dma_start(em(norm_d), em3(PC[:, 0:816])).then_inc(norm_out, 16)
                sp.wait_ge(norm_out, 16)

            @block.gpsimd
            def _(g):
                pass

            @block.vector
            def _(v):
                L = dve_line
                a, b, c = (t[0:PQ, 0:PL] for t in (PA, PB, PC))
                v.wait_ge(pin, 16 * 12)
                L.step(v, v.tensor_tensor(same_prev[:, :], a.bitcast(I32), b.bitcast(I32), ALU.is_equal))
                L.step(v, v.tensor_tensor(same_next[:, :], a.bitcast(I32), c.bitcast(I32), ALU.is_equal))
                L.step(v, v.tensor_scalar(last_of_run[:, :], same_next[:, :], -1.0, 1.0, ALU.mult, ALU.add))
                L.step(v, v.tensor_reduce(small[0:PQ, 6, 0:1], same_prev[:, :], AX.X, ALU.min))
                L.step(v, v.tensor_reduce(small[0:PQ, 6, 1:2], same_next[:, :], AX.X, ALU.min))
                L.step(v, v.tensor_scalar(small[0:PQ, 6, 3:4], small[0:PQ, 6, 0:1], 0.5, 2.0, ALU.subtract, ALU.mult))
                L.step(v, v.tensor_reduce(small[0:PQ, 7, 0:4], ident[0:PQ, 0:PQ].rearrange("q (t i) -> q t i", i=PCS),
                                          AX.X, ALU.add))
                L.step(v, v.tensor_tensor(small[0:PQ, 7, 4:8], small[0:PQ, 7, 0:4], iota8[0:PQ, 0:4], ALU.mult))
                L.step(v, v.tensor_reduce(small[0:PQ, 6, 2:3], small[0:PQ, 7, 4:8], AX.X, ALU.add))
                v.sem_inc(oh_in, 1)
                v.wait_ge(oh_in, 1 + 64)
                L.step(v, v.tensor_scalar(a, b.bitcast(I32), small[0:PQ, 6, 2:3], None, ALU.is_equal))
                scan_pieces(v, b, same_prev, small[0:PQ, 6, 0:1], a, ALU.mult, ALU.add, 0.0, False)
                L.step(v, v.tensor_tensor(b, b, last_of_run[:, :], ALU.mult))
                scan_pieces(v, c, same_next, small[0:PQ, 6, 1:2], b, ALU.mult, ALU.add, 0.0, True)
                L.step(v, v.tensor_tensor(c, c, a, ALU.mult))
                v.sem_inc(cnt_up, 1)
                v.wait_ge(turned, 1)
                L.step(v, v.tensor_copy(PB[:, 0:816].rearrange("p (i j) -> p j i", i=PCS)[:, 0:24, :],
                                        ps[4][:, 0:24 * PCS].rearrange("p (j i) -> p j i", i=PCS)))
                L.step(v, v.tensor_copy(PB[:, 0:816].rearrange("p (i j) -> p j i", i=PCS)[:, 24:48, :],
                                        ps[5][:, 0:24 * PCS].rearrange("p (j i) -> p j i", i=PCS)))
                L.step(v, v.tensor_scalar(PB[:, 0:816], PB[:, 0:816], 1.0, None, ALU.max))
                L.step(v, v.reciprocal(PC[:, 0:816], PB[:, 0:816]))
                v.sem_inc(emu, 1)

            @block.tensor
            def _(pe):
                carry_pe(pe, 0, [False, True])
                fold_pe(pe, fold[:, :], PC[0:PQ, 0:PL], cnt_up, PA[0:PCS, 0:PL], 0)

            @block.scalar
            def _(a):
                fold_act(a, PA[0:PCS, 0:PL], 0)

        def layer_norm(v, a, src, dst, sqrt_req, sqrt_done, n, tile, affine=None):
            L = dve_line
            m, s = small[0:NP, 0, 0:NK], small[0:NP, 1, 0:NK]
            L.step(v, v.tensor_reduce(m, src, AX.X, ALU.add))
            L.step(v, v.tensor_scalar(m, m, 1.0 / D, None, ALU.mult))
            L.step(v, v.tensor_tensor(dst, src, bcast(m, D), ALU.subtract))
            L.step(v, v.tensor_tensor(tile, dst, dst, ALU.mult))
            L.step(v, v.tensor_reduce(s, tile, AX.X, ALU.add))
            L.step(v, v.tensor_scalar(s, s, 1.0 / D, EPS, ALU.mult, ALU.add))
            v.sem_inc(sqrt_req, 1)
            v.wait_ge(sqrt_done, n)
            L.step(v, v.reciprocal(s, small[0:NP, 2, 0:NK]))
            L.step(v, v.tensor_tensor(dst, dst, bcast(s, D), ALU.mult))

        sqrt_req = sem("sqrt_req"); sqrt_done = sem("sqrt_done"); sqrts = [0]

        def sqrt_act(a, n, width=NP):
            a.wait_ge(sqrt_req, n)
            a.activation(small[0:NP, 2, 0:NK], small[0:NP, 1, 0:NK], ACT.Sqrt).then_inc(sqrt_done, 1)

        hT = PA[0:D, 0:N]
        zT = PB[0:D, 0:N]
        scratch = PC[0:NP, 0:NK * D].rearrange("p (k f) -> p k f", f=D)
        turn_in = sem("turn_in"); turn_pe = sem("turn_pe"); turn_act = sem("turn_act"); turns = [0]
        mm_pe = sem("mm_pe"); mm_out = sem("mm_out"); mms = [0]

        def turn_nodes(pe, src, t):
            pe.wait_ge(turn_in, t + 1)
            for g in range(7):
                if g >= 2:
                    pe.wait_ge(turn_act, 7 * t + g - 1)
                for k in range(4 * g, min(4 * g + 4, NK)):
                    last = pe.transpose(ps[g % 2][0:D, (k % 4) * NP:(k % 4 + 1) * NP], src[:, k, :], ident[0:NP, 0:NP])
                last.then_inc(turn_pe, 1)

        def turn_copy(a, t):
            for g in range(7):
                w = (min(4 * g + 4, NK) - 4 * g) * NP
                a.wait_ge(turn_pe, 7 * t + g + 1)
                a.copy(hT[:, 4 * g * NP:4 * g * NP + w], ps[g % 2][0:D, 0:w]).then_inc(turn_act, 1)

        ends_rows = sem("ends_rows"); ends_cnt = [0]

        def gather_ends(g):
            for k in range(NK):
                g.indirect_dma_start(gn[:, k, :], None, scan_d[:, :],
                                     bass.IndirectOffsetOnAxis(ap=end_idx[:, k:k + 1], axis=0)).then_inc(ends_rows, 16)
                ends_cnt[0] += 16
            g.wait_ge(ends_rows, ends_cnt[0])

        tab_up = sem("tab_up"); tab_out = sem("tab_out"); tabs = [0]
        gat = sem("gat")

        sw_names = ("loaded_g", "t_done", "scan_done", "back_done", "copy_done", "scaled")

        idx_in = [sem(f"idx_in{j}") for j in range(3)]
        flag_in = [sem(f"flag_in{j}") for j in range(3)]
        rows_in_ = [sem(f"gathered{j}") for j in range(4)]
        spread_in = [sem(f"spread_in{j}") for j in range(3)]
        msg_in = [sem(f"msg_in{j}") for j in range(4)]
        stored = [sem(f"stored{j}") for j in range(4)]
        msg_out = [sem(f"msg_out{j}") for j in range(4)]
        turned_ = sem("turned_blocks")
        scaled = sem("scaled")
        scanned = sem("scanned")
        heldt = sem("spread_turned")
        held_up = sem("held_up")
        mid = sem("joined")
        relued = sem("relued")
        mixed = sem("mixed")
        backt = sem("turned_back")
        copied = sem("copied")
        sent = {s.num: 0 for s in (*idx_in, *msg_in, *flag_in, *rows_in_, *spread_in, *stored, *msg_out, turned_, scaled,
                                   scanned, heldt, held_up, mid, relued, mixed, backt, copied)}

        def sweep(kind, table, idx_dram, aux_dram, aux_int=False):

            gath = kind in ("sum", "score", "max")
            spread = kind in ("score", "max")
            scale = aux_dram is not None and kind in ("sum", "att")
            first = sweeps[0] == 0
            sweeps[0] += 1
            W = RW if kind == "score" else D
            arrived = rows_in_ if gath else msg_in
            per_rows = 16 * (CPB if gath else 1)
            read = mid if spread else scanned
            flags_read = held_up if kind == "score" else scanned

            def at(s, i, off):
                return i * BODY + (sent[s.num] + off + BODY)

            def fills(s, i, u, n, by=16):
                return i * (BODY // n * by) + (sent[s.num] + (u // n + 1) * by)

            def used(s, i, u, n, by=16):
                return i * (BODY // n * by) + (sent[s.num] + (u // n + 1) * by)

            cols_in = slice(D, 2 * D + RW - D) if kind == "score" else slice(0, D)
            with nc.Block() as block:
                @block.sync
                def _(sp):
                    with sp.Fori(0, TURNS) as i:
                        for u in range(BODY):
                            if u % GRP == 0:
                                j = u // GRP
                                sp.wait_ge(turned_, at(turned_, i, u - 2 * GRP))
                                sp.sem_inc(armed, 1)
                                g = i * (BODY // GRP) + j
                                n = 0
                                if gath:
                                    sp.dma_start(idx[:, j, :], idx_dram[g]).then_inc(idx_in[j], 16)
                                if aux_dram is not None:
                                    dst = auxi if aux_int else aux
                                    sp.dma_start(dst[:, j, :], aux_dram[g]).then_inc(idx_in[j], 16)
                            b = i * BODY + u
                            sp.wait_ge(flags_read, at(flags_read, i, u - 2))
                            sp.sem_inc(armed, 1)
                            sp.dma_start(hold[0:W, u % 3, :], seg_bcast(hold_d, b, W)).then_inc(flag_in[u % 3], 16)
                            if kind == "max":
                                sp.dma_start(cap[:, u % 3, :], seg_bcast(cap_d, b, D)).then_inc(flag_in[u % 3], 16)
                            if spread:
                                sp.wait_ge(heldt, at(heldt, i, u - 2))
                                sp.sem_inc(armed, 1)
                                sp.dma_start(EX[:, u % 3, :, :], blk(spread_d[0:EP, :])[b]).then_inc(spread_in[u % 3], 16)
                            if kind == "att":
                                sp.wait_ge(scaled, at(scaled, i, u - 3))
                                sp.sem_inc(armed, 1)
                                sp.dma_start(G[:, u % 4, :, 0:D], blk(msg_d[0:EP, :])[b]).then_inc(msg_in[u % 4], 16)
                    for s in stored:
                        sp.wait_ge(s, sent[s.num] + 16 * (NB // 4 + 1))
                    for s in msg_out:
                        sp.wait_ge(s, sent[s.num] + 16 * (NB // 4 * (kind == "score") + 1))

                if gath:
                    @block.gpsimd
                    def _(g):
                        with g.Fori(0, TURNS) as i:
                            for u in range(BODY):
                                if u % GRP == 0:
                                    n_in = 16 * (1 + (aux_dram is not None))
                                    g.wait_ge(idx_in[u // GRP], sent[idx_in[u // GRP].num] + i * n_in + n_in)
                                    g.sem_inc(armed, 1)
                                g.wait_ge(turned_, at(turned_, i, u - 3))
                                g.sem_inc(armed, 1)
                                if kind == "score":
                                    g.wait_ge(msg_out[u % 4], used(msg_out[u % 4], i, u, 4))
                                    g.sem_inc(armed, 1)
                                for c in range(CPB):
                                    q = (u % GRP) * CPB + c
                                    g.indirect_dma_start(G[:, u % 4, c, 0:table.shape[1]], None, table,
                                                         bass.IndirectOffsetOnAxis(ap=idx[:, u // GRP, q:q + 1], axis=0)
                                                         ).then_inc(rows_in_[u % 4], 16)

                @block.tensor
                def _(pe):
                    for s in (turned_, heldt, mixed, backt) * first:
                        pe.sem_inc(s, BODY)
                    with pe.Fori(0, TURNS) as i:
                        for u in range(BODY):
                            if spread:
                                pe.wait_ge(spread_in[u % 3], fills(spread_in[u % 3], i, u, 3))
                                pe.wait_ge(held_up, at(held_up, i, u - 1))
                                pe.sem_inc(armed, 1)
                                for c in range(CPB):
                                    last = pe.transpose(ps[2 + u % 2][0:W, c:BLK:CPB], EX[:, u % 3, c, 0:W], ident[:, :])
                                last.then_inc(heldt, 1)
                            pe.wait_ge(arrived[u % 4], fills(arrived[u % 4], i, u, 4, per_rows))
                            if scale or kind == "score":
                                pe.wait_ge(scaled, at(scaled, i, u + 1))
                            pe.wait_ge(read, at(read, i, u - 1))
                            pe.sem_inc(armed, 1)
                            src = GS[:, u % 2] if scale else G[:, u % 4]
                            cc = slice(0, D) if scale else cols_in
                            for c in range(CPB):
                                last = pe.transpose(ps[u % 2][0:W, c:BLK:CPB], src[:, c, cc], ident[:, :])
                            last.then_inc(turned_, 1)
                            if kind == "score":
                                pe.wait_ge(mid, at(mid, i, u + 1))
                                pe.wait_ge(copied, at(copied, i, u - 1))
                                pe.matmul(ps[4 + u % 2][0:4, :], w4[:, :], prod[:, u % 2, :], start=True, stop=True
                                          ).then_inc(mixed, 1)
                            if kind == "max":
                                pe.wait_ge(relued, at(relued, i, u + 1))
                                pe.wait_ge(scanned, at(scanned, i, u - 1))
                                pe.sem_inc(armed, 1)
                                pe.matmul(ps[4 + u % 2][0:D, :], w3bt[:, :], act_sb[:, u % 2, :], start=True, stop=True
                                          ).then_inc(mixed, 1)
                            if kind != "score":
                                pe.wait_ge(scanned, at(scanned, i, u + 1))
                                pe.wait_ge(copied, at(copied, i, u - 1))
                                pe.sem_inc(armed, 1)
                                for c in range(CPB):
                                    last = pe.transpose(ps[6 + u % 2][:, c * D:(c + 1) * D], run[:, u % 2, c:BLK:CPB],
                                                        ident[0:D, 0:D])
                                last.then_inc(backt, 1)

                @block.vector
                def _(v):
                    for s in (scaled, scanned, held_up, mid) * first:
                        v.sem_inc(s, BODY)
                    with v.Fori(0, TURNS) as i:
                        for u in range(BODY):
                            j, q = u // GRP, (u % GRP) * CPB
                            n_in = 16 * (gath + (aux_dram is not None))
                            if spread:
                                v.wait_ge(flag_in[u % 3], fills(flag_in[u % 3], i, u, 3, 32 if kind == "max" else 16))
                                v.wait_ge(heldt, at(heldt, i, u + 1))
                                v.wait_ge(held_up, at(held_up, i, u))
                                v.wait_ge(mid, at(mid, i, u - 1))
                                v.tensor_tensor_scan(held[0:W, u % 2, :], hold[0:W, u % 3, :], ps[2 + u % 2][0:W, :],
                                                     held[0:W, (u + 1) % 2, BLK - 1:BLK], ALU.mult, ALU.add).then_inc(held_up, 1)
                            if kind == "score":
                                v.wait_ge(idx_in[j], sent[idx_in[j].num] + i * n_in + n_in)
                                v.wait_ge(turned_, at(turned_, i, u - 3))
                                v.tensor_tensor(G[:, u % 4, :, 2 * D:2 * D + R8], bcast(auxi[:, j, q:q + CPB], R8),
                                                iota8[:, :].unsqueeze(1).to_broadcast([128, CPB, R8]),
                                                ALU.is_equal).then_inc(scaled, 1)
                            if scale:
                                v.wait_ge(idx_in[j], sent[idx_in[j].num] + i * n_in + n_in)
                                v.wait_ge(arrived[u % 4], fills(arrived[u % 4], i, u, 4, per_rows))
                                v.wait_ge(turned_, at(turned_, i, u - 1))
                                v.tensor_tensor(GS[:, u % 2], G[:, u % 4, :, 0:D], bcast(aux[:, j, q:q + CPB], D),
                                                ALU.mult).then_inc(scaled, 1)
                            v.wait_ge(turned_, at(turned_, i, u + 1))
                            if kind == "score":
                                v.wait_ge(held_up, at(held_up, i, u + 1))
                                v.wait_ge(mixed, at(mixed, i, u - 1))
                                v.tensor_tensor(prod[:, u % 2, :], ps[u % 2][0:W, :], held[:, u % 2, :], ALU.mult).then_inc(mid, 1)
                                continue
                            if kind == "max":
                                v.wait_ge(held_up, at(held_up, i, u + 1))
                                v.wait_ge(relued, at(relued, i, u - 1))
                                v.tensor_tensor(prod[0:D, u % 2, :], ps[u % 2][0:D, :], held[0:D, u % 2, :], ALU.add).then_inc(mid, 1)
                                v.wait_ge(mixed, at(mixed, i, u + 1))
                                flag, val, ops = cap[:, u % 3, :], ps[4 + u % 2][0:D, :], (ALU.min, ALU.max)
                            else:
                                v.wait_ge(flag_in[u % 3], fills(flag_in[u % 3], i, u, 3))
                                flag, val, ops = hold[0:D, u % 3, :], ps[u % 2][0:D, :], (ALU.mult, ALU.add)
                            v.wait_ge(scanned, at(scanned, i, u))
                            v.wait_ge(backt, at(backt, i, u - 1))
                            v.tensor_tensor_scan(run[:, u % 2, :], flag, val, run[:, (u + 1) % 2, BLK - 1:BLK],
                                                 *ops).then_inc(scanned, 1)

                @block.scalar
                def _(a):
                    for s in (copied, relued) * first:
                        a.sem_inc(s, BODY)
                    for j in range(4 * first):
                        part = slice(j * D // 4, (j + 1) * D // 4)
                        a.dma_start(scan_d[ZROW:ZROW + 1, part], zero_row[0:1, part]).then_inc(stored[j], 16)
                        a.dma_start(msg_d[EP:EP + 1, part], zero_row[0:1, part]).then_inc(msg_out[j], 16)
                    with a.Fori(0, TURNS) as i:
                        for u in range(BODY):
                            b = i * BODY + u
                            if kind == "max":
                                a.wait_ge(mid, at(mid, i, u + 1))
                                a.wait_ge(mixed, at(mixed, i, u - 1))
                                a.activation(act_sb[:, u % 2, :], prod[0:D, u % 2, :], ACT.Relu).then_inc(relued, 1)
                            if kind == "score":
                                a.wait_ge(arrived[u % 4], fills(arrived[u % 4], i, u, 4, per_rows))
                                a.sem_inc(armed, 1)
                                a.dma_start(blk(msg_d[0:EP, :])[b], G[:, u % 4, :, 0:D]).then_inc(msg_out[u % 4], 16)
                                a.wait_ge(mixed, at(mixed, i, u + 1))
                                a.wait_ge(stored[u % 4], used(stored[u % 4], i, u, 4))
                                a.activation(sc_sb[:, u % 4, :], ps[4 + u % 2][0:4, :], ACT.Copy, scale=D ** -0.5
                                             ).then_inc(copied, 1)
                                a.wait_ge(copied, at(copied, i, u + 1))
                                a.sem_inc(armed, 1)
                                a.dma_start(score_d.rearrange("r (b e) -> b r e", e=BLK)[b], sc_sb[:, u % 4, :]
                                            ).then_inc(stored[u % 4], 16)
                                continue
                            a.wait_ge(backt, at(backt, i, u + 1))
                            a.wait_ge(stored[u % 4], used(stored[u % 4], i, u, 4))
                            a.activation(O[:, u % 4].rearrange("p c f -> p (c f)"), ps[6 + u % 2][:, 0:CPB * D], ACT.Copy
                                         ).then_inc(copied, 1)
                            a.wait_ge(copied, at(copied, i, u + 1))
                            a.sem_inc(armed, 1)
                            a.dma_start(blk(scan_d[0:EP, :])[b], O[:, u % 4, :, :]).then_inc(stored[u % 4], 16)

            for s, on in ((turned_, True), (scaled, scale or kind == "score"), (scanned, kind != "score"),
                          (heldt, spread), (held_up, spread), (mid, spread), (relued, kind == "max"),
                          (mixed, spread), (backt, kind != "score"), (copied, True)):
                sent[s.num] += NB * on
            for s in idx_in:
                sent[s.num] += TURNS * 16 * (gath + (aux_dram is not None))
            for s in flag_in:
                sent[s.num] += NB // 3 * (32 if kind == "max" else 16)
            for s in spread_in:
                sent[s.num] += NB // 3 * 16 * spread
            for s in arrived:
                sent[s.num] += NB // 4 * per_rows
            for s in stored:
                sent[s.num] += NB // 4 * 16
            for s in msg_out:
                sent[s.num] += NB // 4 * 16 * (kind == "score")

        sweeps = [0]

        def blk(d):
            return d.rearrange("(b p c) f -> b p c f", p=128, c=CPB)

        def seg_bcast(d, b, parts):
            return d.rearrange("(b e) -> b e", e=BLK)[b].unsqueeze(0).to_broadcast([parts, BLK])

        def norm_phase():
            sqrts[0] += 1
            n = sqrts[0]
            with nc.Block() as block:
                @block.vector
                def _(v):
                    layer_norm(v, None, xn[:, :, :], hn[:, :, :], sqrt_req, sqrt_done, n, scratch)
                    dve_line.step(v, v.tensor_scalar(hn[:, :, :], hn[:, :, :], 0.0, None, ALU.max))

                @block.scalar
                def _(a):
                    sqrt_act(a, n)

        def store_table(dst_d):
            with nc.Block() as block:
                @block.sync
                def _(sp):
                    sp_line.step(sp, sp.dma_start(node(dst_d), hn[:, :, :]), 16)

        norm_phase()
        store_table(tab_d)
        sweep("sum", tab_d, A["src_it"], None)

        zin = sem("zin"); zup = sem("zup"); zcp = sem("zcp"); bnr = sem("bnr"); h1b = sem("h1b"); h1c = sem("h1c")
        with nc.Block() as block:
            @block.gpsimd
            def _(g):
                gather_ends(g)

            @block.vector
            def _(v):
                L = dve_line
                v.wait_ge(ends_rows, 16 * NK)
                L.step(v, v.tensor_tensor(gn[:, :, :], gn[:, :, :], hn[:, :, :], ALU.add))
                v.sem_inc(turn_in, 1)
                for c, (a0, w) in enumerate(CHUNKS):
                    v.wait_ge(zcp, c + 1)
                    L.step(v, v.bn_stats(bn[:, c, :], zT[:, a0:a0 + w]))
                L.step(v, v.bn_aggr(bnm[:, :], bn[:, :, :]))
                L.step(v, v.tensor_scalar(bnc[:, 0:1], bnm[:, 1:2], EPS, None, ALU.add))
                v.sem_inc(bnr, 1)
                v.wait_ge(bnr, 2)
                L.step(v, v.reciprocal(bnc[:, 2:3], bnc[:, 1:2]))
                L.step(v, v.tensor_tensor(bnc[:, 2:3], bnc[:, 2:3], cols[:, 1:2], ALU.mult))
                L.step(v, v.tensor_tensor(bnc[:, 3:4], bnm[:, 0:1], bnc[:, 2:3], ALU.mult))
                L.step(v, v.tensor_tensor(bnc[:, 3:4], cols[:, 2:3], bnc[:, 3:4], ALU.subtract))
                v.sem_inc(bnr, 1)

            @block.tensor
            def _(pe):
                turn_nodes(pe, gn, 0)
                pe.wait_ge(turn_act, 7)
                for c, (a0, w) in enumerate(CHUNKS):
                    if c >= 2:
                        pe.wait_ge(zcp, c - 1)
                    pe.matmul(ps[2 + c % 2][0:D, 0:w], w0a[:, :], hT[:, a0:a0 + w], start=True, stop=True).then_inc(zup, 1)
                pe.wait_ge(h1b, 1)
                for k in range(NK):
                    if k and k % 8 == 0:
                        pe.wait_ge(h1c, (k // 8) - 1) if k >= 16 else None
                    last = pe.transpose(ps[4 + (k // 8) % 2][0:NP, (k % 8) * D:(k % 8 + 1) * D], zT[:, k * NP:(k + 1) * NP],
                                        ident[0:D, 0:D])
                    if k % 8 == 7 or k == NK - 1:
                        last.then_inc(h1b, 1)

            @block.scalar
            def _(a):
                turn_copy(a, 0)
                for c, (a0, w) in enumerate(CHUNKS):
                    a.wait_ge(zup, c + 1)
                    a.activation(zT[:, a0:a0 + w], ps[2 + c % 2][0:D, 0:w], ACT.Identity, bias=cols[:, 0:1]).then_inc(zcp, 1)
                a.wait_ge(bnr, 1)
                a.activation(bnc[:, 1:2], bnc[:, 0:1], ACT.Sqrt).then_inc(bnr, 1)
                a.wait_ge(bnr, 3)
                a.activation(zT, zT, ACT.Relu, bias=bnc[:, 3:4], scale=bnc[:, 2:3]).then_inc(h1b, 1)
                for gidx in range(4):
                    w = min(8, NK - 8 * gidx)
                    a.wait_ge(h1b, gidx + 2)
                    a.copy(hn[:, 8 * gidx:8 * gidx + w, :].rearrange("p k f -> p (k f)"), ps[4 + gidx % 2][0:NP, 0:w * D]).then_inc(h1c, 1)

        store_table(tab_d)
        sweep("sum", tab_d, A["src_it"], None)
        turns[0] = 1

        def node_matmul(pe, rhs, width, lhs=None):
            lhs = hT if lhs is None else lhs
            base = mms[0]
            for k in range(NK):
                if k >= 2:
                    pe.wait_ge(mm_out, base + k - 1)
                pe.matmul(ps[2 + k % 2][0:NP, 0:width], lhs[:, k * NP:(k + 1) * NP], rhs, start=True, stop=True).then_inc(mm_pe, 1)

        def add_ends(v, other):
            v.wait_ge(ends_rows, ends_total[0])
            dve_line.step(v, v.tensor_tensor(gn[:, :, :], gn[:, :, :], other, ALU.add))

        ends_total = [16 * NK]

        ends_total[0] += 16 * NK
        with nc.Block() as block:
            @block.gpsimd
            def _(g):
                gather_ends(g)

            @block.vector
            def _(v):
                add_ends(v, hn[:, :, :])
                v.sem_inc(turn_in, 1)
                dve_line.step(v, v.tensor_tensor(xn[:, :, :], xn[:, :, :],
                                                 rows[:, 0, :].unsqueeze(1).to_broadcast([NP, NK, D]), ALU.add))
                for k in range(NK):
                    v.wait_ge(mm_pe, k + 1)
                    v.tensor_tensor(xn[:, k, :], xn[:, k, :], ps[2 + k % 2][0:NP, 0:D], ALU.add).then_inc(mm_out, 1)
                v.wait_ge(mm_out, NK)

            @block.tensor
            def _(pe):
                turn_nodes(pe, gn, 1)
                pe.wait_ge(turn_act, 14)
                node_matmul(pe, w0b[:, :], D)

            @block.scalar
            def _(a):
                turn_copy(a, 1)
        mms[0] += NK
        turns[0] = 2
        if dbg == 1:
            with nc.Block() as block:
                @block.sync
                def _(sp):
                    sp_line.step(sp, sp.dma_start(node(out), xn[:, :, :]), 16)
            return

        def conv_tables(w, b_row):
            t = turns[0]
            turns[0] += 1
            base = mms[0]
            H4 = [PB[0:NP, :], PC[0:NP, :]]
            v4 = lambda t_: H4[t_ // 2][:, (t_ % 2) * NK * D:(t_ % 2 + 1) * NK * D].rearrange("p (k f) -> p k f", f=D)
            with nc.Block() as block:
                @block.vector
                def _(v):
                    v.sem_inc(turn_in, 1)
                    for k in range(NK):
                        v.wait_ge(mm_pe, base + k + 1)
                        p = ps[2 + k % 2]
                        for h in range(2):
                            o = H4[h][:, 0:2 * NK * D].rearrange("p (t k f) -> p t k f", t=2, f=D)[:, :, k, :]
                            v.tensor_copy(o, p[0:NP, 2 * h * D:2 * (h + 1) * D].rearrange("p (t f) -> p t f", t=2))
                        v.tensor_tensor(rn[:, k, :], p[0:NP, R4 * D:(R4 + 1) * D], rows[:, b_row, :], ALU.add).then_inc(mm_out, 1)
                    v.wait_ge(mm_out, base + NK)
                    v.sem_inc(tab_up, 1)

                @block.tensor
                def _(pe):
                    turn_nodes(pe, hn, t)
                    pe.wait_ge(turn_act, 7 * (t + 1))
                    node_matmul(pe, w[:, :, :].rearrange("d r e -> d (r e)"), (R4 + 1) * D)

                @block.scalar
                def _(a):
                    turn_copy(a, t)

                @block.sync
                def _(sp):
                    tabs[0] += 1
                    sp.wait_ge(tab_up, tabs[0])
                    for t_ in range(R4):
                        sp.dma_start(node(tab4_d[t_ * N:(t_ + 1) * N, :]), v4(t_)).then_inc(tab_out, 16)
                    sp.wait_ge(tab_out, 16 * R4 * tabs[0])
            mms[0] += NK

        def ends_phase(finish):
            ends_total[0] += 16 * NK
            with nc.Block() as block:
                @block.gpsimd
                def _(g):
                    gather_ends(g)

                @block.vector
                def _(v):
                    add_ends(v, rn[:, :, :])
                    finish(v, dve_line)

        norm_phase()
        conv_tables(w1a, 1)
        sweep("sum", tab4_d, idx4_d, norm_d)
        ends_phase(lambda v, L: L.step(v, v.tensor_scalar(hn[:, :, :], gn[:, :, :], 0.0, None, ALU.max)))
        conv_tables(w1b, 2)
        sweep("sum", tab4_d, idx4_d, norm_d)
        ends_phase(lambda v, L: L.step(v, v.tensor_tensor(xn[:, :, :], xn[:, :, :], gn[:, :, :], ALU.add)))
        norm_phase()
        if dbg == 2:
            with nc.Block() as block:
                @block.sync
                def _(sp):
                    sp_line.step(sp, sp.dma_start(node(out), xn[:, :, :]), 16)
            return

        w_rel = sem("w_rel"); w_tr = sem("w_tr"); w_cp = sem("w_cp"); emb_in = sem("emb_in"); q_pe = sem("q_pe"); q_cp = sem("q_cp")
        with nc.Block() as block:
            @block.gpsimd
            def _(g):
                g.indirect_dma_start(emb[:, :], None, A["L2_gnn_rule_emb"],
                                     bass.IndirectOffsetOnAxis(ap=rid[:, 0:1], axis=0)).then_inc(emb_in, 16)
                g.wait_ge(emb_in, 16)

            @block.vector
            def _(v):
                L = dve_line
                L.step(v, v.tensor_reduce(relT[:, :], w2r[:, :, :], AX.X, ALU.add))
                L.step(v, v.tensor_scalar(relT[:, :], relT[:, :], 1.0 / D, None, ALU.mult))
                v.sem_inc(w_rel, 1)
                v.wait_ge(w_tr, 1)
                L.step(v, v.tensor_copy(m2[:, 0:D], ps[0][0:D, 0:D]))
                L.step(v, v.tensor_copy(embT[:, :], ps[0][0:D, D:D + 4]))
                L.step(v, v.tensor_copy(w3t[:, 0, :], ps[0][0:D, 2 * D:3 * D]))
                L.step(v, v.tensor_tensor(w3t[:, 1, :], ps[0][0:D, 3 * D:4 * D], w3t[:, 0, :], ALU.subtract))
                L.step(v, v.tensor_copy(w3bt[:, :], ps[0][0:D, 4 * D:5 * D]))
                v.sem_inc(w_cp, 1)
                v.wait_ge(w_tr, 2)
                L.step(v, v.tensor_scalar(m2[:, D:D + R8], ps[1][0:D, 0:R8], cols[:, 4:5], None, ALU.add))
                L.step(v, v.tensor_copy(m2[:, D + R8:RW], ps[1][0:D, R8:R8 + 4]))

            @block.tensor
            def _(pe):
                pe.wait_ge(emb_in, 16)
                pe.transpose(ps[0][0:D, 0:D], wk[:, 0, :], ident[0:D, 0:D])
                pe.transpose(ps[0][0:D, D:D + 4], emb[:, :], ident[0:4, 0:4])
                pe.transpose(ps[0][0:D, 2 * D:3 * D], w3[:, D:2 * D], ident[0:D, 0:D])
                pe.transpose(ps[0][0:D, 3 * D:4 * D], w3[:, 0:D], ident[0:D, 0:D])
                pe.transpose(ps[0][0:D, 4 * D:5 * D], w3b[:, :], ident[0:D, 0:D]).then_inc(w_tr, 1)
                pe.wait_ge(w_rel, 1)
                pe.wait_ge(w_cp, 1)
                pe.matmul(ps[1][0:D, 0:R8], wk[:, 1, :], relT[:, :], start=True, stop=True)
                pe.matmul(ps[1][0:D, R8:R8 + 4], wk[:, 2, :], embT[:, :], start=True, stop=True).then_inc(w_tr, 1)

        t = turns[0]
        turns[0] += 1
        base = mms[0]
        R_nm = rn
        rrows = PC[0:NP, 0:NK * RW].rearrange("p (k f) -> p k f", f=RW)
        T8 = PC[0:NP, NK * RW:NK * RW + 4 * R8 * 2 * D // 4 * 1]
        t8buf = [PC[0:NP, 2048 + 1024 * s:2048 + 1024 * (s + 1)].rearrange("p (t f) -> p t f", t=R8) for s in range(4)]
        t8_out = [sem(f"t8_out{s}") for s in range(4)]
        spread_out = sem("spread_out"); rr_up = sem("rr_up"); t8_up = sem("t8_up")
        qT = zT

        def scatter_rows(g, n):
            for k in range(NK):
                g.indirect_dma_start(spread_d, bass.IndirectOffsetOnAxis(ap=start_idx[:, k:k + 1], axis=0),
                                     rrows[:, k, :], None).then_inc(spread_out, 16)
            g.wait_ge(spread_out, n)

        with nc.Block() as block:
            @block.vector
            def _(v):
                L = dve_line
                v.sem_inc(turn_in, 1)
                for k in range(NK):
                    v.wait_ge(mm_pe, base + k + 1)
                    v.tensor_copy(rrows[:, k, :], ps[2 + k % 2][0:NP, 0:RW]).then_inc(mm_out, 1)
                v.wait_ge(mm_out, base + NK)
                v.sem_inc(rr_up, 1)
                for k in range(NK):
                    v.wait_ge(mm_pe, base + NK + k + 1)
                    if k >= 4:
                        v.wait_ge(t8_out[k % 4], 16 * (k // 4))
                    v.tensor_copy(t8buf[k % 4][:, :, D:2 * D], hn[:, k, :].unsqueeze(1).to_broadcast([NP, R8, D]))
                    v.tensor_copy(t8buf[k % 4][:, :, 0:D], ps[2 + k % 2][0:NP, :].rearrange("p (t f) -> p t f", t=R8)
                                  ).then_inc(mm_out, 1)

            @block.tensor
            def _(pe):
                turn_nodes(pe, hn, t)
                pe.wait_ge(turn_act, 7 * (t + 1))
                for c, (a0, w) in enumerate(CHUNKS):
                    if c >= 2:
                        pe.wait_ge(q_cp, c - 1)
                    pe.matmul(ps[4 + c % 2][0:D, 0:w], wq[:, :], hT[:, a0:a0 + w], start=True, stop=True).then_inc(q_pe, 1)
                pe.wait_ge(q_cp, len(CHUNKS))
                node_matmul(pe, m2[:, :], RW, qT)
                mms[0] += NK
                pe.wait_ge(mm_out, mms[0])
                node_matmul(pe, w2r[:, :, :].rearrange("d r e -> d (r e)"), R8 * D)
                mms[0] += NK

            @block.scalar
            def _(a):
                turn_copy(a, t)
                for c, (a0, w) in enumerate(CHUNKS):
                    a.wait_ge(q_pe, c + 1)
                    a.activation(qT[:, a0:a0 + w], ps[4 + c % 2][0:D, 0:w], ACT.Identity, bias=cols[:, 3:4]).then_inc(q_cp, 1)

            @block.gpsimd
            def _(g):
                g.wait_ge(rr_up, 1)
                scatter_rows(g, 16 * NK)

            @block.sync
            def _(sp):
                tv = tab8_d.rearrange("(t p k) f -> k p t f", t=R8, k=NK)
                for k in range(NK):
                    sp.wait_ge(mm_out, base + NK + k + 1)
                    sp.dma_start(tv[k], t8buf[k % 4]).then_inc(t8_out[k % 4], 16)
                for s in range(4):
                    sp.wait_ge(t8_out[s], 16 * len(range(s, NK, 4)))

        sweep("score", tab8_d, idx8_d, A["t8_it"], aux_int=True)

        s_in = sem("s_in"); exp_req = sem("exp_req"); exp_done = sem("exp_done"); att_out = sem("att_out"); att_up = sem("att_up")
        sumw = sem("sumw")
        with nc.Block() as block:
            a_, b_, c_ = (t_[0:PQ, 0:PL] for t_ in (PA, PB, PC))
            capp = c_[:, 0:PL // 2].bitcast(BF16)
            attrow = PB[0:PCS, 0:PL]

            @block.sync
            def _(sp):
                for r in range(4):
                    sp.dma_start(PA[r * PCS:(r + 1) * PCS, 0:PL], score_d[r].rearrange("(i f) -> i f", i=PCS)).then_inc(s_in, 16)
                sp.wait_ge(att_up, 1)
                sp.dma_start(em(att_d), em3(PC[:, 0:816])).then_inc(att_out, 16)
                sp.wait_ge(att_out, 16)

            @block.vector
            def _(v):
                L = dve_line
                v.wait_ge(s_in, 64)
                L.step(v, v.tensor_scalar(b_, same_prev[:, :], 0.5, 2.0, ALU.subtract, ALU.mult))
                L.step(v, v.tensor_scalar(capp, b_, BIG, None, ALU.mult))
                L.step(v, v.tensor_scalar(small[0:PQ, 7, 0:1], small[0:PQ, 6, 3:4], BIG, None, ALU.mult))
                scan_pieces(v, b_, capp, small[0:PQ, 7, 0:1], a_, ALU.min, ALU.max, -BIG, False)
                L.step(v, v.tensor_tensor(b_, b_, last_of_run[:, :], ALU.mult))
                scan_pieces(v, c_, same_next, small[0:PQ, 6, 1:2], b_, ALU.mult, ALU.add, 0.0, True)
                L.step(v, v.tensor_tensor(a_, a_, c_, ALU.subtract))
                v.sem_inc(exp_req, 1)
                v.wait_ge(exp_done, 1)
                scan_pieces(v, b_, same_prev, small[0:PQ, 6, 0:1], a_, ALU.mult, ALU.add, 0.0, False)
                L.step(v, v.tensor_tensor(b_, b_, last_of_run[:, :], ALU.mult))
                scan_pieces(v, c_, same_next, small[0:PQ, 6, 1:2], b_, ALU.mult, ALU.add, 0.0, True)
                L.step(v, v.reciprocal(b_, c_))
                L.step(v, v.tensor_tensor(a_, a_, b_, ALU.mult))
                L.step(v, v.tensor_scalar(a_, a_, 0.25, None, ALU.mult))
                v.sem_inc(cnt_up, 1)
                v.wait_ge(turned, 2)
                for h in range(2):
                    L.step(v, v.tensor_copy(PC[:, 0:816].rearrange("p (i j) -> p j i", i=PCS)[:, 24 * h:24 * h + 24, :],
                                            ps[4 + h][:, 0:24 * PCS].rearrange("p (j i) -> p j i", i=PCS)))
                v.sem_inc(att_up, 1)

            @block.tensor
            def _(pe):
                carry_pe(pe, 2, [False, True, False, True])
                fold_pe(pe, fold[:, :], PA[0:PQ, 0:PL], cnt_up, attrow, 1)

            @block.scalar
            def _(a):
                a.wait_ge(exp_req, 1)
                a.activation(a_, a_, ACT.Exp).then_inc(exp_done, 1)
                fold_act(a, attrow, 1)

        sweep("att", None, None, att_d)

        sqrts[0] += 1
        n_sq = sqrts[0]
        ends_total[0] += 16 * NK
        rb = lambda j: rows[:, j, :].unsqueeze(1).to_broadcast([NP, NK, D])
        with nc.Block() as block:
            @block.gpsimd
            def _(g):
                gather_ends(g)

            @block.vector
            def _(v):
                L = dve_line
                add_ends(v, rb(3))
                layer_norm(v, None, gn[:, :, :], rn[:, :, :], sqrt_req, sqrt_done, n_sq, scratch)
                L.step(v, v.tensor_tensor(rn[:, :, :], rn[:, :, :], rb(4), ALU.mult))
                L.step(v, v.tensor_tensor(rn[:, :, :], rn[:, :, :], rb(5), ALU.add))
                L.step(v, v.tensor_scalar(rn[:, :, :], rn[:, :, :], 0.0, None, ALU.max))
                L.step(v, v.tensor_tensor(xn[:, :, :], xn[:, :, :], rn[:, :, :], ALU.add))

            @block.scalar
            def _(a):
                sqrt_act(a, n_sq)
        norm_phase()
        if dbg == 3:
            with nc.Block() as block:
                @block.sync
                def _(sp):
                    sp_line.step(sp, sp.dma_start(node(out), xn[:, :, :]), 16)
            return

        t = turns[0]
        turns[0] += 1
        base = mms[0]
        s3_out = sem("s3_out")
        with nc.Block() as block:
            @block.vector
            def _(v):
                L = dve_line
                v.sem_inc(turn_in, 1)
                L.step(v, v.memset(rrows[:, :, D:RW], 0.0))
                for k in range(NK):
                    v.wait_ge(mm_pe, base + k + 1)
                    v.tensor_copy(rn[:, k, :], ps[2 + k % 2][0:NP, 0:D])
                    v.tensor_tensor(rrows[:, k, 0:D], ps[2 + k % 2][0:NP, D:2 * D], rows[:, 6, :], ALU.add).then_inc(mm_out, 1)
                v.wait_ge(mm_out, base + NK)
                v.sem_inc(rr_up, 1)

            @block.tensor
            def _(pe):
                turn_nodes(pe, hn, t)
                pe.wait_ge(turn_act, 7 * (t + 1))
                node_matmul(pe, w3t[:, :, :].rearrange("d r e -> d (r e)"), 2 * D)

            @block.scalar
            def _(a):
                turn_copy(a, t)

            @block.gpsimd
            def _(g):
                g.wait_ge(rr_up, 2)
                scatter_rows(g, 32 * NK)

            @block.sync
            def _(sp):
                sp.wait_ge(rr_up, 2)
                sp.dma_start(node(tab_d), rn[:, :, :]).then_inc(s3_out, 16)
                sp.wait_ge(s3_out, 16)

        sweep("max", tab_d, A["src_it"], None)

        fin = sem("fin"); fin_out = sem("fin_out")
        with nc.Block() as block:
            @block.gpsimd
            def _(g):
                gather_ends(g)

            @block.vector
            def _(v):
                L = dve_line
                L.step(v, v.tensor_tensor(rn[:, :, :], rb(7), bcast(nonempty[:, :], D), ALU.mult))
                ends_total[0] += 16 * NK
                add_ends(v, rn[:, :, :])
                L.step(v, v.tensor_tensor(xn[:, :, :], xn[:, :, :], gn[:, :, :], ALU.add))
                v.sem_inc(fin, 1)

            @block.sync
            def _(sp):
                sp.wait_ge(fin, 1)
                sp.dma_start(node(out), xn[:, :, :]).then_inc(fin_out, 16)
                sp.wait_ge(fin_out, 16)


_FLOATS = ['x', 'L0_gnn_W1', 'L0_gnn_b1', 'L0_gnn_gamma1', 'L0_gnn_beta1', 'L0_gnn_W2', 'L0_gnn_b2', 'L1_gnn_W1',
           'L1_gnn_root1', 'L1_gnn_b1', 'L1_gnn_W2', 'L1_gnn_root2', 'L1_gnn_b2', 'L2_gnn_W_r', 'L2_gnn_Wq_w',
           'L2_gnn_Wq_bias', 'L2_gnn_Wk_w', 'L2_gnn_Wk_bias', 'L2_gnn_rule_emb', 'L2_gnn_bias', 'L2_gnn_ln_g',
           'L2_gnn_ln_b', 'L3_gnn_W1', 'L3_gnn_b1', 'L3_gnn_W2', 'L3_gnn_b2']
_COLUMNS = ['L0_gnn_b1', 'L0_gnn_gamma1', 'L0_gnn_beta1', 'L2_gnn_Wq_bias', 'L2_gnn_Wk_bias']
DBG = 0


def kernel(**inputs):
    import numpy as _np
    import concourse.bacc as _bacc
    from concourse import mybir as _mybir
    from concourse.bass_utils import run_bass_kernel_spmd as _run

    def padded(name, fill):
        a = _np.asarray(inputs[name])
        return _np.concatenate([a, _np.full(EP - E, fill, a.dtype)])

    def by_group(a):
        return _np.ascontiguousarray(a.reshape(NG, GRP, 128, CPB).transpose(0, 2, 1, 3).reshape(NG, 128, GC))

    host = {n: _np.ascontiguousarray(inputs[n]) for n in _FLOATS}
    for n in _COLUMNS:
        host[n] = host[n].reshape(D, 1)
    dst = padded("dst", N)
    none = _np.full(1, -1, dst.dtype)
    host["dst_ext"] = _np.concatenate([none, dst, none])
    host["dst_rows"] = dst.reshape(HEADS, 128)
    host["dst_heads"] = _np.ascontiguousarray(dst[::128])
    host["src_it"] = by_group(padded("src", 0))
    t4, t8 = padded("edge_type_4", 0), padded("edge_type_8", 0)
    host["t4_nat"] = t4
    host["t4_it"] = by_group(t4)
    host["t8_it"] = by_group(t8)
    host["rule_ids"] = _np.asarray(inputs["L2_gnn_rule_ids"]).reshape(4, 1)

    nc = _bacc.Bacc("TRN2", target_bir_lowering=False, num_devices=1)
    arrays = {f"in_{n}": a for n, a in host.items()}
    A = {n: nc.dram_tensor(f"in_{n}", a.shape, _mybir.dt.from_np(a.dtype), kind="ExternalInput").ap()
         for n, a in host.items()}
    out = nc.dram_tensor("out", (N, D), F32, kind="ExternalOutput").ap()
    build(nc, A, out, DBG)
    r = _run(nc, [arrays], core_ids=[0])
    return r.results[0]["out"]
```

```python
from contextlib import ExitStack

import concourse.bass as bass
from concourse import mybir

F32 = mybir.dt.float32
BF16 = mybir.dt.bfloat16
I32 = mybir.dt.int32
ALU = mybir.AluOpType
ACT = mybir.ActivationFunctionType
AX = mybir.AxisListType

N = 3125
D = 64
NP = 125
NK = N // NP
E = 103125
BLK = 512
CPB = BLK // 128
BODY = 12
NBP = -(-E // BLK)
NBP += NBP % 2
TURNS, TAIL = divmod(NBP, BODY)
BPP = 8
PCS = -(-NBP // BPP)
NB = PCS * BPP
EP = NB * BLK
FLAGS = 6
RING = BODY
GRP = 4
NG = NB // GRP
GC = GRP * CPB
PL = EP // PCS
PQ = 4 * PCS
R4, R8 = 4, 8
RW = D + R8 + 4
ZROW = EP
BIG = 3.3e38
HEADS = EP // 128
HALF = NBP // 2
EPS = 1e-5
CH = 500
CHUNKS = [(a, min(CH, N - a)) for a in range(0, N, CH)]


def build(nc, A, out, dbg=None):
    with ExitStack() as ctx:
        def sb(name, shape, dt=F32):
            return ctx.enter_context(nc.sbuf_tensor(name, shape, dt))

        def dram(name, shape, dt=F32):
            return nc.dram_tensor(name, shape, dt, kind="ExternalOutput" if dbg else "Internal").ap()

        def sem(name):
            return ctx.enter_context(nc.semaphore(name))

        hold_d = dram("hold_d", [EP], BF16)
        cap_d = dram("cap_d", [EP], BF16)
        ends_d = dram("ends_d", [N + 1], F32)
        idx4_d = dram("idx4_d", [NG, 128, GC], I32)
        idx8_d = dram("idx8_d", [NG, 128, GC], I32)
        scan_d = dram("scan_d", [EP + 1, D])
        tab_d = dram("tab_d", [N, D])
        tab4_d = dram("tab4_d", [R4 * N, D])
        tab8_d = dram("tab8_d", [R8 * N, 2 * D])
        spread_d = dram("spread_d", [EP + N, RW])
        msg_d = dram("msg_d", [EP, D])
        score_d = dram("score_d", [4, EP])

        PA = sb("PA", [128, 4096])
        PB = sb("PB", [128, 4096])
        PC = sb("PC", [128, 6400])
        same_prev = sb("same_prev", [PQ, PL], BF16)
        same_next = sb("same_next", [PQ, PL], BF16)
        last_of_run = sb("last_of_run", [PQ, PL], BF16)
        ident = sb("ident", [128, 128])
        iota8 = sb("iota8", [128, R8])
        ones = sb("ones", [128, 4])
        end_idx = sb("end_idx", [NP, NK], I32)
        start_idx = sb("start_idx", [NP, NK], I32)
        nonempty = sb("nonempty", [NP, NK])
        xn = sb("xn", [NP, NK, D])
        hn = sb("hn", [NP, NK, D])
        rn = sb("rn", [NP, NK, D])
        gn = sb("gn", [NP, NK, D])
        small = sb("small", [128, 8, 32])
        straddle = sb("straddle", [NP, NK])
        fold = sb("fold", [PQ, PCS])
        srow = sb("srow", [1, 4, PQ + 1])
        scol = sb("scol", [PQ, 4])
        G = sb("G", [128, RING, CPB, D + RW])
        GS = sb("GS", [128, 2, CPB, 2 * D])
        EX = sb("EX", [128, 3, CPB, RW])
        idx = sb("idx", [128, 3, GC], I32)
        scal = sb("scal", [128, NB * CPB])
        G2 = G[:, :, :, :].rearrange("p r c w -> p (r c w)")[:, 0:4 * CPB * 2 * D].rearrange(
            "p (s h c f) -> p s h c f", s=4, c=CPB, h=2)
        GS2 = GS[:, :, :, :].rearrange("p s c (h f) -> p s c h f", h=2)
        hold = sb("hold", [128, FLAGS, BLK], BF16)
        cap = sb("cap", [D, FLAGS, BLK], BF16)
        held = sb("held", [RW, 2, BLK])
        prod = sb("prod", [RW, 2, BLK])
        act_sb = sb("act_sb", [D, 2, BLK])
        run = sb("run", [128, 2, BLK])
        O = sb("O", [128, 4, 2, CPB, D])
        sc_sb = O[0:4].rearrange("r s h c f -> r s (h c f)")
        w0a = sb("w0a", [D, D]); w0b = sb("w0b", [D, D])
        w1a = sb("w1a", [D, R4 + 1, D]); w1b = sb("w1b", [D, R4 + 1, D])
        w2r = sb("w2r", [D, R8, D])
        wq = sb("wq", [D, D]); wk = sb("wk", [D, 3, D]); m2 = sb("m2", [D, RW])
        w3 = sb("w3", [D, 2 * D]); w3t = sb("w3t", [D, 2, D]); w3b = sb("w3b", [D, D]); w3bt = sb("w3bt", [D, D])
        emb = sb("emb", [4, D]); embT = sb("embT", [D, 4]); relT = sb("relT", [D, R8]); rid = sb("rid", [4, 1], I32)
        cols = sb("cols", [D, 8])
        rows = sb("rows", [NP, 8, D])
        w4 = sb("w4", [RW, 4])
        bn = sb("bn", [D, len(CHUNKS), 6]); bnm = sb("bnm", [D, 2]); bnc = sb("bnc", [D, 4])

        ps = [ctx.enter_context(nc.psum_tensor(f"ps{i}", [128, 512], F32)) for i in range(8)]

        armed = sem("armed")

        class Line:
            def __init__(self, name):
                self.s, self.n = sem(name), 0

            def step(self, eng, ins, by=1):
                self.n += by
                ins.then_inc(self.s, by)
                eng.wait_ge(self.s, self.n)

        dve_line, pool_line, act_line, sp_line, pe_line = (
            Line(n) for n in ("dve_line", "pool_line", "act_line", "sp_line", "pe_line"))

        def bcast(ap, n):
            return ap.unsqueeze(len(ap.shape)).to_broadcast(list(ap.shape) + [n])

        def row_bcast(v, parts, n):
            return bass.AP(tensor=v.tensor, offset=v.offset, ap=[[0, parts], [1, n]])

        node = lambda d: d.rearrange("(p k) f -> p k f", p=NP)
        P_ = lambda t: t[:, :]

        loaded = sem("loaded")
        n_loads = [0]
        iot = sem("iot")
        with nc.Block() as block:
            @block.sync
            def _(sp):
                def ld(dst, src):
                    sp.dma_start(dst, src).then_inc(loaded, 16)
                    n_loads[0] += 16
                ld(xn[:, :, :], node(A["x"]))
                ld(P_(w0a), A["L0_gnn_W1"]); ld(P_(w0b), A["L0_gnn_W2"])
                for w, nm, rt in ((w1a, "L1_gnn_W1", "L1_gnn_root1"), (w1b, "L1_gnn_W2", "L1_gnn_root2")):
                    ld(w[:, 0:R4, :], A[nm].rearrange("r d e -> d r e"))
                    ld(w[:, R4, :], A[rt])
                ld(w2r[:, :, :], A["L2_gnn_W_r"].rearrange("r d e -> d r e"))
                ld(P_(wq), A["L2_gnn_Wq_w"])
                ld(wk[:, :, :], A["L2_gnn_Wk_w"].rearrange("(a d) e -> d a e", a=3))
                ld(P_(w3), A["L3_gnn_W1"]); ld(P_(w3b), A["L3_gnn_W2"])
                ld(P_(rid), A["rule_ids"])
                for j, nm in enumerate(("L0_gnn_b1", "L0_gnn_gamma1", "L0_gnn_beta1", "L2_gnn_Wq_bias", "L2_gnn_Wk_bias")):
                    ld(cols[:, j:j + 1], A[nm])
                for j, nm in enumerate(("L0_gnn_b2", "L1_gnn_b1", "L1_gnn_b2", "L2_gnn_bias", "L2_gnn_ln_g", "L2_gnn_ln_b", "L3_gnn_b1", "L3_gnn_b2")):
                    ld(rows[:, j, :], row_bcast(A[nm], NP, D))
                sp.wait_ge(loaded, n_loads[0])

            @block.gpsimd
            def _(g):
                L = pool_line
                L.step(g, g.iota(PA[:, 0:128].bitcast(I32), [[1, 128]], base=0, channel_multiplier=0))
                L.step(g, g.iota(PA[:, 128:129].bitcast(I32), [[0, 1]], base=0, channel_multiplier=1))
                L.step(g, g.iota(PA[0:NP, 256:256 + NK].bitcast(I32), [[1, NK]], base=0, channel_multiplier=NK))
                g.sem_inc(iot, 1)

            @block.vector
            def _(v):
                L = dve_line
                v.wait_ge(iot, 1)
                L.step(v, v.tensor_copy(PB[:, 0:129], PA[:, 0:129].bitcast(I32)))
                L.step(v, v.tensor_scalar(ident[:, :], PB[:, 0:128], PB[:, 128:129], None, ALU.is_equal))
                L.step(v, v.tensor_copy(P_(iota8), PB[:, 0:R8]))
                L.step(v, v.memset(P_(ones), 1.0))
                L.step(v, v.tensor_copy(fold[:, :], ident[0:PQ, 0:PCS]))
                for t in range(1, 4):
                    L.step(v, v.tensor_tensor(fold[:, :], fold[:, :], ident[0:PQ, t * PCS:(t + 1) * PCS], ALU.add))
                L.step(v, v.memset(G[:, :, :, 2 * D + R8:], 1.0))
                L.step(v, v.memset(run[:, :, :], 0.0))
                L.step(v, v.memset(held[:, :, :], 0.0))
        with nc.Block() as block:
            @block.vector
            def _(v):
                L = dve_line
                L.step(v, v.memset(w4[0:D, :], 1.0))
                L.step(v, v.tensor_copy(w4[D:RW, :], ident[D:RW, D + R8:RW]))
                L.step(v, v.tensor_reduce(small[D:RW, 1, 0:1], ident[D:RW, D:D + R8], AX.X, ALU.add))
                L.step(v, v.tensor_tensor(w4[D:RW, :], w4[D:RW, :],
                                          small[D:RW, 1, 0:1].to_broadcast([RW - D, 4]), ALU.add))

        cur = PA[:, 0:HEADS].bitcast(I32)
        prv = PA[:, HEADS:2 * HEADS].bitcast(I32)
        edge_in = sem("edge_in"); flags_up = sem("flags_up"); flags_out = sem("flags_out")
        zeros = PC[:, PL:]
        with nc.Block() as block:
            @block.sync
            def _(sp):
                dx = A["dst_ext"]
                sp.dma_start(cur, dx[1:EP + 1].rearrange("(p f) -> p f", p=128)).then_inc(edge_in, 16)
                sp.dma_start(prv, dx[0:EP].rearrange("(p f) -> p f", p=128)).then_inc(edge_in, 16)
                sp.wait_ge(flags_up, 1)
                sp.dma_start(hold_d.rearrange("(p f) -> p f", p=128), PB[:, 0:HEADS // 2].bitcast(BF16)).then_inc(flags_out, 16)
                sp.dma_start(cap_d.rearrange("(p f) -> p f", p=128), PB[:, HEADS // 2:HEADS].bitcast(BF16)).then_inc(flags_out, 16)
                sp.wait_ge(flags_out, 32)

            @block.vector
            def _(v):
                L = dve_line
                v.wait_ge(edge_in, 32)
                hf = PB[:, HEADS:2 * HEADS]
                L.step(v, v.tensor_tensor(hf, cur, prv, ALU.is_equal))
                L.step(v, v.tensor_copy(PB[:, 0:HEADS // 2].bitcast(BF16), hf))
                L.step(v, v.tensor_scalar(hf, hf, 0.5, 2.0, ALU.subtract, ALU.mult))
                L.step(v, v.tensor_scalar(PB[:, HEADS // 2:HEADS].bitcast(BF16), hf, BIG, None, ALU.mult))
                v.sem_inc(flags_up, 1)
                L.step(v, v.memset(zeros, 0.0))

        carry_req = sem("carry_req"); carry_row = sem("carry_row"); carry_back = sem("carry_back"); carry_col = sem("carry_col")
        carries = [0]

        def scan_pieces(v, dst, flag, flag_min, val, op0, op1, rest, back):
            L = dve_line
            w = slice(None, None, -1) if back else slice(None)
            far = 0 if back else PL - 1
            L.step(v, v.tensor_tensor_scan(dst[:, w], flag[:, w], val[:, w], rest, op0, op1))
            L.step(v, v.tensor_copy(scol[:, 0:1], dst[:, far:far + 1]))
            L.step(v, v.tensor_copy(scol[:, 1:2], flag_min))
            c = carries[0] = carries[0] + 1
            v.sem_inc(carry_req, 1)
            v.wait_ge(carry_row, c)
            L.step(v, v.tensor_copy(srow[:, 0, 0:PQ], ps[2][0:1, 0:PQ]))
            L.step(v, v.tensor_copy(srow[:, 1, 0:PQ], ps[2][0:1, PQ:2 * PQ]))
            L.step(v, v.memset(srow[:, 2, :], rest))
            if back:
                L.step(v, v.tensor_tensor_scan(srow[:, 2, 0:PQ][:, ::-1], srow[:, 1, 0:PQ][:, ::-1],
                                               srow[:, 0, 0:PQ][:, ::-1], rest, op0, op1))
            else:
                L.step(v, v.tensor_tensor_scan(srow[:, 2, 1:PQ + 1], srow[:, 1, 0:PQ], srow[:, 0, 0:PQ],
                                               rest, op0, op1))
            v.sem_inc(carry_back, 1)
            v.wait_ge(carry_col, c)
            L.step(v, v.tensor_copy(scol[:, 2:3], ps[3][0:PQ, 0:1]))
            L.step(v, v.tensor_tensor_scan(dst[:, w], flag[:, w], val[:, w], scol[:, 2:3], op0, op1))

        def carry_pe(pe, c, back):
            pe.wait_ge(carry_req, c)
            pe.matmul(ps[2][0:1, 0:PQ], scol[:, 0:1], ident[0:PQ, 0:PQ], start=True, stop=True)
            pe.matmul(ps[2][0:1, PQ:2 * PQ], scol[:, 1:2], ident[0:PQ, 0:PQ], start=True, stop=True).then_inc(carry_row, 1)
            pe.wait_ge(carry_back, c)
            init = srow[:, 2, 1:PQ + 1] if back else srow[:, 2, 0:PQ]
            pe.matmul(ps[3][0:PQ, 0:1], init, ones[0:1, 0:1], start=True, stop=True).then_inc(carry_col, 1)

        kinds_up = sem("kinds_up"); folded = sem("folded"); fold_out = sem("fold_out"); edge_major = sem("edge_major")
        FC = PL // 512
        TB = BPP * CPB // 2

        def fold_pe(pe, src, rowt, n):
            pe.wait_ge(kinds_up, n)
            for j in range(FC):
                if j >= 2:
                    pe.wait_ge(fold_out, (n - 1) * FC + j - 1)
                pe.matmul(ps[2 + j % 2][0:PCS, :], fold[:, :], src[:, 512 * j:512 * (j + 1)], start=True, stop=True
                          ).then_inc(folded, 1)
            pe.wait_ge(fold_out, n * FC)
            for j in range(2 * TB):
                b, c = divmod(j, CPB)
                last = pe.transpose(ps[4 + j // TB][:, (j % TB) * PCS:(j % TB + 1) * PCS],
                                    rowt[:, 512 * b + c:512 * (b + 1):CPB], ident[0:PCS, 0:PCS])
            last.then_inc(edge_major, 1)

        def fold_act(a, rowt, n):
            for j in range(FC):
                a.wait_ge(folded, (n - 1) * FC + j + 1)
                a.copy(rowt[:, 512 * j:512 * (j + 1)], ps[2 + j % 2][0:PCS, :]).then_inc(fold_out, 1)

        def edge_major_out(v, dst, n):
            v.wait_ge(edge_major, n)
            for h in range(2):
                dve_line.step(v, v.tensor_copy(dst.rearrange("p (i j) -> p j i", i=PCS)[:, TB * h:TB * h + TB, :],
                                               ps[4 + h][:, 0:TB * PCS].rearrange("p (j i) -> p j i", i=PCS)))

        srcs = PA[:, 0:HEADS].bitcast(I32)
        t4s = PA[:, HEADS:2 * HEADS].bitcast(I32)
        t8s = PA[:, 2 * HEADS:3 * HEADS].bitcast(I32)
        heads_i = PA[0:NP, 3 * HEADS:4 * HEADS].bitcast(I32)
        nid_i = PA[0:NP, 4 * HEADS:4 * HEADS + NK].bitcast(I32)
        em = lambda d: d.rearrange("g p c -> p g c")
        em3 = lambda t: t.rearrange("p (g c) -> p g c", c=GC)
        types_in = sem("types_in"); idx_up = sem("idx_up"); idx_out = sem("idx_out"); nid_up = sem("nid_up")
        rows_at = sem("rows_at"); rows_in = sem("rows_in"); ends_up = sem("ends_up"); ends_out = sem("ends_out")
        ends_in = sem("ends_in"); pieces_in = sem("pieces_in"); onehot_at = sem("onehot_at"); kinds_in = sem("kinds_in")
        zfill = sem("zfill")
        nid, cnt, rowc, end, start, tmp = (small[0:NP, j, 0:NK] for j in (0, 1, 2, 3, 4, 6))
        rowc_i = small[0:NP, 5, 0:NK].bitcast(I32)
        drows = PC[0:NP, 0:NK * 128].bitcast(I32).rearrange("p (k c) -> p k c", c=128)
        pa, pb, pc = (t[0:PQ, 0:PL] for t in (PA, PB, PC))

        def load_types(sp):
            for dst, src in ((em3(srcs), em(A["src_it"])), (em3(t4s), em(A["t4_it"])), (em3(t8s), em(A["t8_it"])),
                             (heads_i, row_bcast(A["dst_heads"], NP, HEADS))):
                sp.dma_start(dst, src).then_inc(types_in, 16)

        wide = 6400 - PL
        whole, rest = divmod((EP + N) * RW, 128 * wide)
        cuts = [(j * 128 * wide, 128, wide) for j in range(whole)]
        cuts += [(whole * 128 * wide, 128, rest // 128), ((EP + N) * RW - rest % 128, 1, rest % 128)]
        cuts = [c for c in cuts if c[2]]
        FILL = -(-len(cuts) // (TURNS - 1))
        n_zfill = 16 * (len(cuts) + 3 + NB - NBP)

        def zero_fill(turn):
            def fill(a):
                flat = spread_d.rearrange("a b -> (a b)")
                for at_, p, w in cuts[(turn - 1) * FILL:turn * FILL]:
                    a.dma_start(flat[at_:at_ + p * w].rearrange("(p f) -> p f", p=p), zeros[0:p, 0:w]).then_inc(zfill, 16)
                if turn > 1:
                    return
                a.dma_start(ends_d[0:1].rearrange("(p f) -> p f", p=1), zeros[0:1, 0:1]).then_inc(zfill, 16)
                a.dma_start(scan_d[ZROW:ZROW + 1, :], zeros[0:1, 0:D]).then_inc(zfill, 16)
                a.dma_start(scan_d[NBP * BLK:EP, :].rearrange("(p r) f -> p (r f)", p=128),
                            zeros[:, 0:(NB - NBP) * CPB * D]).then_inc(zfill, 16)
                for b in range(NBP, NB):
                    a.dma_start(score_d[:, b * BLK:(b + 1) * BLK], zeros[0:4, 0:BLK]).then_inc(zfill, 16)
            return fill

        def node_numbers(g):
            pool_line.step(g, g.iota(nid_i, [[1, NK]], base=0, channel_multiplier=NK))
            g.sem_inc(nid_up, 1)

        def count_rows(v):
            L = dve_line
            v.wait_ge(types_in, 64)
            for t in (t4s, t8s):
                L.step(v, v.tensor_scalar(PB[:, 0:HEADS], t, float(N), None, ALU.mult))
                L.step(v, v.tensor_tensor(t, PB[:, 0:HEADS], srcs, ALU.add))
            v.sem_inc(idx_up, 1)
            v.wait_ge(nid_up, 1)
            L.step(v, v.tensor_copy(nid, nid_i))
            heads = PB[0:NP, HEADS:2 * HEADS]
            L.step(v, v.tensor_copy(heads, heads_i))
            for k in range(NK):
                L.step(v, v.tensor_scalar(PB[0:NP, 0:HEADS], heads, nid[:, k:k + 1], 0.0, ALU.is_le, ALU.add,
                                          accum_out=cnt[:, k:k + 1]))
            L.step(v, v.tensor_scalar(rowc, cnt, -1.0, 0.0, ALU.add, ALU.max))
            L.step(v, v.tensor_copy(rowc_i, rowc))
            v.sem_inc(rows_at, 1)

        def store_indices(sp):
            sp.wait_ge(idx_up, 1)
            sp.dma_start(em(idx4_d), em3(t4s)).then_inc(idx_out, 16)
            sp.dma_start(em(idx8_d), em3(t8s)).then_inc(idx_out, 16)

        def gather_rows(g):
            g.wait_ge(rows_at, 1)
            for k in range(NK):
                g.indirect_dma_start(drows[:, k, :], None, A["dst_rows"],
                                     bass.IndirectOffsetOnAxis(ap=rowc_i[:, k:k + 1], axis=0)).then_inc(rows_in, 16)

        def find_ends(v):
            L = dve_line
            v.wait_ge(rows_in, 16 * NK)
            le = PB[0:NP, 0:NK * 128].rearrange("p (k c) -> p k c", c=128)
            L.step(v, v.tensor_tensor(le, drows, bcast(nid, 128), ALU.is_le))
            L.step(v, v.tensor_reduce(cnt, le, AX.X, ALU.add))
            L.step(v, v.scalar_tensor_tensor(end, rowc, 128.0, cnt, ALU.mult, ALU.add))
            v.sem_inc(ends_up, 1)

        def exchange_ends(sp):
            sp.wait_ge(ends_up, 1)
            sp.wait_ge(idx_out, 32)
            sp.dma_start(ends_d[1:N + 1].rearrange("(p k) -> p k", p=NP), end).then_inc(ends_out, 16)
            dx = A["dst_ext"]
            for t in range(4):
                q = slice(t * PCS, (t + 1) * PCS)
                for j, tile in ((1, PA), (0, PB), (2, PC)):
                    sp.dma_start(tile[q, 0:PL].bitcast(I32), dx[j:j + EP].rearrange("(i f) -> i f", i=PCS)
                                 ).then_inc(pieces_in, 16)
            sp.wait_ge(ends_out, 16)
            sp.dma_start(start, ends_d[0:N].rearrange("(p k) -> p k", p=NP)).then_inc(ends_in, 16)

        def index_runs(v):
            L = dve_line
            v.wait_ge(ends_in, 16)
            L.step(v, v.tensor_tensor(nonempty[:, :], end, start, ALU.is_gt))
            L.step(v, v.tensor_scalar(straddle[:, :], start, float(HALF * BLK), None, ALU.is_lt))
            L.step(v, v.tensor_scalar(tmp, end, float(HALF * BLK), None, ALU.is_gt))
            L.step(v, v.tensor_tensor(straddle[:, :], straddle[:, :], tmp, ALU.mult))
            L.step(v, v.tensor_scalar(tmp, end, -1.0 - ZROW, None, ALU.add))
            L.step(v, v.tensor_tensor(tmp, tmp, nonempty[:, :], ALU.mult))
            L.step(v, v.tensor_scalar(tmp, tmp, float(ZROW), None, ALU.add))
            L.step(v, v.tensor_copy(end_idx[:, :], tmp))
            L.step(v, v.tensor_scalar(tmp, nid, float(EP), None, ALU.add))
            L.step(v, v.tensor_tensor(start, start, tmp, ALU.subtract))
            L.step(v, v.tensor_tensor(start, start, nonempty[:, :], ALU.mult))
            L.step(v, v.tensor_tensor(start, start, tmp, ALU.add))
            L.step(v, v.tensor_copy(start_idx[:, :], start))

        def piece_flags(v):
            L = dve_line
            v.wait_ge(pieces_in, 16 * 12)
            L.step(v, v.tensor_tensor(same_prev[:, :], pa.bitcast(I32), pb.bitcast(I32), ALU.is_equal))
            v.sem_inc(onehot_at, 1)
            L.step(v, v.tensor_tensor(same_next[:, :], pa.bitcast(I32), pc.bitcast(I32), ALU.is_equal))
            L.step(v, v.tensor_scalar(last_of_run[:, :], same_next[:, :], -1.0, 1.0, ALU.mult, ALU.add))
            L.step(v, v.tensor_reduce(small[0:PQ, 6, 0:1], same_prev[:, :], AX.X, ALU.min))
            L.step(v, v.tensor_reduce(small[0:PQ, 6, 1:2], same_next[:, :], AX.X, ALU.min))
            L.step(v, v.tensor_scalar(small[0:PQ, 6, 3:4], small[0:PQ, 6, 0:1], 0.5, 2.0, ALU.subtract, ALU.mult))
            L.step(v, v.tensor_reduce(small[0:PQ, 7, 0:4], ident[0:PQ, 0:PQ].rearrange("q (t i) -> q t i", i=PCS),
                                      AX.X, ALU.add))
            L.step(v, v.tensor_tensor(small[0:PQ, 7, 4:8], small[0:PQ, 7, 0:4], iota8[0:PQ, 0:4], ALU.mult))
            L.step(v, v.tensor_reduce(small[0:PQ, 6, 2:3], small[0:PQ, 7, 4:8], AX.X, ALU.add))

        def load_kinds(sp):
            sp.wait_ge(onehot_at, 1)
            for t in range(4):
                q = slice(t * PCS, (t + 1) * PCS)
                sp.dma_start(PB[q, 0:PL].bitcast(I32), A["t4_nat"].rearrange("(i f) -> i f", i=PCS)).then_inc(kinds_in, 16)

        def count_kinds(v):
            v.wait_ge(kinds_in, 64)
            dve_line.step(v, v.tensor_scalar(pa, pb.bitcast(I32), small[0:PQ, 6, 2:3], None, ALU.is_equal))
            scan_pieces(v, pb, same_prev, small[0:PQ, 6, 0:1], pa, ALU.mult, ALU.add, 0.0, False)

        def spread_counts(v):
            L = dve_line
            L.step(v, v.tensor_tensor(pb, pb, last_of_run[:, :], ALU.mult))
            scan_pieces(v, pc, same_next, small[0:PQ, 6, 1:2], pb, ALU.mult, ALU.add, 0.0, True)
            L.step(v, v.tensor_tensor(pc, pc, pa, ALU.mult))
            v.sem_inc(kinds_up, 1)

        def norms(v):
            L = dve_line
            edge_major_out(v, PB[:, 0:HEADS], 1)
            L.step(v, v.tensor_scalar(PB[:, 0:HEADS], PB[:, 0:HEADS], 1.0, None, ALU.max))
            L.step(v, v.reciprocal(scal[:, :], PB[:, 0:HEADS]))

        first_side = {
            "sync": {1: load_types, 4: store_indices, 7: exchange_ends, 9: load_kinds},
            "scalar": {t: zero_fill(t) for t in range(1, TURNS)} | {
                14: lambda a: (zero_fill(14)(a), fold_act(a, PA[0:PCS, 0:PL], 1))},
            "gpsimd": {1: node_numbers, 4: gather_rows},
            "tensor": {10: lambda pe: carry_pe(pe, 1, False), 12: lambda pe: carry_pe(pe, 2, True),
                       14: lambda pe: fold_pe(pe, pc, PA[0:PCS, 0:PL], 1)},
            "vector": {2: count_rows, 6: find_ends, 8: lambda v: (index_runs(v), piece_flags(v)), 10: count_kinds,
                       12: spread_counts, 15: norms},
        }

        def layer_norm(v, a, src, dst, sqrt_req, sqrt_done, n, tile, affine=None):
            L = dve_line
            m, s = small[0:NP, 0, 0:NK], small[0:NP, 1, 0:NK]
            L.step(v, v.tensor_reduce(m, src, AX.X, ALU.add))
            L.step(v, v.tensor_scalar(m, m, 1.0 / D, None, ALU.mult))
            L.step(v, v.tensor_tensor(dst, src, bcast(m, D), ALU.subtract))
            L.step(v, v.tensor_tensor(tile, dst, dst, ALU.mult))
            L.step(v, v.tensor_reduce(s, tile, AX.X, ALU.add))
            L.step(v, v.tensor_scalar(s, s, 1.0 / D, EPS, ALU.mult, ALU.add))
            v.sem_inc(sqrt_req, 1)
            v.wait_ge(sqrt_done, n)
            L.step(v, v.reciprocal(s, small[0:NP, 2, 0:NK]))
            L.step(v, v.tensor_tensor(dst, dst, bcast(s, D), ALU.mult))

        sqrt_req = sem("sqrt_req"); sqrt_done = sem("sqrt_done"); sqrts = [0]

        def sqrt_act(a, n, width=NP):
            a.wait_ge(sqrt_req, n)
            a.activation(small[0:NP, 2, 0:NK], small[0:NP, 1, 0:NK], ACT.Sqrt).then_inc(sqrt_done, 1)

        hT = PA[0:D, 0:N]
        zT = PB[0:D, 0:N]
        scratch = PC[0:NP, 0:NK * D].rearrange("p (k f) -> p k f", f=D)
        turn_in = sem("turn_in"); turn_pe = sem("turn_pe"); turn_act = sem("turn_act"); turns = [0]
        mm_pe = sem("mm_pe"); mm_out = sem("mm_out"); mms = [0]

        def turn_nodes(pe, src, t):
            pe.wait_ge(turn_in, t + 1)
            for g in range(7):
                if g >= 2:
                    pe.wait_ge(turn_act, 7 * t + g - 1)
                for k in range(4 * g, min(4 * g + 4, NK)):
                    last = pe.transpose(ps[g % 2][0:D, (k % 4) * NP:(k % 4 + 1) * NP], src[:, k, :], ident[0:NP, 0:NP])
                last.then_inc(turn_pe, 1)

        def turn_copy(a, t):
            for g in range(7):
                w = (min(4 * g + 4, NK) - 4 * g) * NP
                a.wait_ge(turn_pe, 7 * t + g + 1)
                a.copy(hT[:, 4 * g * NP:4 * g * NP + w], ps[g % 2][0:D, 0:w]).then_inc(turn_act, 1)

        ends_rows = sem("ends_rows"); ends_cnt = [0]

        def gather_ends(g):
            for k in range(NK):
                g.indirect_dma_start(gn[:, k, :], None, scan_d[:, :],
                                     bass.IndirectOffsetOnAxis(ap=end_idx[:, k:k + 1], axis=0)).then_inc(ends_rows, 16)
                ends_cnt[0] += 16
            g.wait_ge(ends_rows, ends_cnt[0])

        tab_up = sem("tab_up"); tab_out = sem("tab_out"); tabs = [0]
        gat = sem("gat")

        idx_in = [sem(f"idx_in{j}") for j in range(3)]
        flag_in = [sem(f"flag_in{j}") for j in range(FLAGS)]
        gathered = [sem(f"gathered{j}") for j in range(RING)]
        spread_in = [sem(f"spread_in{j}") for j in range(3)]
        stored = [sem(f"stored{j}") for j in range(4)]
        msg_out = [sem(f"msg_out{j}") for j in range(RING)]
        turned_ = sem("turned_blocks")
        scaled = sem("scaled")
        scanned = sem("scanned")
        heldt = sem("spread_turned")
        held_up = sem("held_up")
        joined = sem("joined")
        relued = sem("relued")
        mixed = sem("mixed")
        backt = sem("turned_back")
        copied = sem("copied")
        progress = (turned_, scaled, scanned, heldt, held_up, joined, relued, mixed, backt, copied)
        sent = {s.num: 0 for s in (*idx_in, *flag_in, *gathered, *spread_in, *stored, *msg_out, *progress)}

        def through(s, i, off):
            return i * BODY + (sent[s.num] + off)

        def landed(s, i, u, n, by=16):
            return i * (BODY // n * by) + (sent[s.num] + (u // n + 1) * by)

        def wait_for(eng, s, value):
            if not isinstance(value, int) or value > sent[s.num]:
                eng.wait_ge(s, value)
                return True
            return False

        def gated(eng, s, value):
            if wait_for(eng, s, value):
                eng.sem_inc(armed, 1)

        def all_blocks(eng, body, side=None):
            side = side or {}
            for u in range(BODY):
                body(0, u, BODY)
            cuts = sorted({1, TURNS, *side})
            for lo, hi in zip(cuts, cuts[1:]):
                if lo in side:
                    side[lo](eng)
                with eng.Fori(lo, hi) as i:
                    for u in range(BODY):
                        body(i, u, BODY)
            for u in range(TAIL):
                body(TURNS, u, TAIL - 1 - u)

        def first(i, u):
            return isinstance(i, int) and i * BODY + u == 0

        def sweep(kind, table, idx_dram, scale=False, side={}):
            spread = kind in ("score", "max")
            W = RW if kind == "score" else D
            width = table.shape[1]
            bank_read = joined if spread else scanned
            flags_read = held_up if kind == "score" else scanned
            n_flags = 32 if kind == "max" else 16
            with nc.Block() as block:
                @block.sync
                def _(sp):
                    def body(i, u, left):
                        b = i * BODY + u
                        if u % GRP == 0:
                            s = gathered[(u - 2 * GRP - 1) % RING]
                            gated(sp, s, landed(s, i, u - 2 * GRP - 1, RING, 16 * CPB))
                            sp.dma_start(idx[:, u // GRP, :], idx_dram[i * (BODY // GRP) + u // GRP]
                                         ).then_inc(idx_in[u // GRP], 16)
                        gated(sp, flags_read, through(flags_read, i, u + 1 - FLAGS))
                        sp.dma_start(hold[0:W, u % FLAGS, :], seg_bcast(hold_d, b, W)).then_inc(flag_in[u % FLAGS], 16)
                        if kind == "max":
                            sp.dma_start(cap[:, u % FLAGS, :], seg_bcast(cap_d, b, D)).then_inc(flag_in[u % FLAGS], 16)
                        if spread:
                            gated(sp, heldt, through(heldt, i, u - 2))
                            sp.dma_start(EX[:, u % 3, :, :], blk(spread_d[0:EP, :])[b]).then_inc(spread_in[u % 3], 16)
                    all_blocks(sp, body, side.get("sync"))
                    for j, s in enumerate(stored):
                        sp.wait_ge(s, sent[s.num] + 16 * len(range(j, NBP, 4)))
                    if kind == "score":
                        for j, s in enumerate(msg_out):
                            sp.wait_ge(s, sent[s.num] + 16 * len(range(j, NBP, RING)))

                @block.gpsimd
                def _(g):
                    def body(i, u, left):
                        if u % GRP == 0:
                            gated(g, idx_in[u // GRP], landed(idx_in[u // GRP], i, u, RING))
                        gated(g, turned_, through(turned_, i, u + 1 - RING))
                        if kind == "score":
                            gated(g, msg_out[u], landed(msg_out[u], i, u - RING, RING))
                        for c in range(CPB):
                            q = (u % GRP) * CPB + c
                            g.indirect_dma_start(G[:, u, c, 0:width], None, table,
                                                 bass.IndirectOffsetOnAxis(ap=idx[:, u // GRP, q:q + 1], axis=0)
                                                 ).then_inc(gathered[u], 16)
                    all_blocks(g, body, side.get("gpsimd"))

                @block.tensor
                def _(pe):
                    def turn_spread(i, u):
                        s = spread_in[u % 3]
                        wait_for(pe, s, landed(s, i, u, 3))
                        gated(pe, held_up, through(held_up, i, u - 1))
                        for c in range(CPB):
                            last = pe.transpose(ps[2 + u % 2][0:W, c:BLK:CPB], EX[:, u % 3, c, 0:W], ident[:, :])
                        last.then_inc(heldt, 1)

                    def turn_gathered(i, u):
                        s = gathered[u % RING]
                        if scale or kind == "score":
                            wait_for(pe, scaled, through(scaled, i, u + 1))
                        wait_for(pe, bank_read, through(bank_read, i, u - 1))
                        gated(pe, s, landed(s, i, u, RING, 16 * CPB))
                        src = GS[:, u % 2, :, 0:D] if scale else G[:, u % RING]
                        cc = slice(D, D + RW) if kind == "score" else slice(0, D)
                        for c in range(CPB):
                            last = pe.transpose(ps[u % 2][0:W, c:BLK:CPB], src[:, c, cc], ident[:, :])
                        last.then_inc(turned_, 1)

                    def turn_back(i, u):
                        wait_for(pe, scanned, through(scanned, i, u + 1))
                        gated(pe, copied, through(copied, i, u - 1))
                        for c in range(CPB):
                            last = pe.transpose(ps[6 + u % 2][:, c * D:(c + 1) * D], run[0:D, u % 2, c:BLK:CPB],
                                                ident[0:D, 0:D])
                        last.then_inc(backt, 1)

                    def body(i, u, left):
                        if kind == "score":
                            if left:
                                turn_spread(i, u + 1)
                            wait_for(pe, joined, through(joined, i, u + 1))
                            gated(pe, copied, through(copied, i, u - 1))
                            pe.matmul(ps[4 + u % 2][0:4, :], w4[:, :], prod[:, u % 2, :], start=True, stop=True
                                      ).then_inc(mixed, 1)
                            if left:
                                turn_gathered(i, u + 1)
                        elif kind == "max":
                            wait_for(pe, relued, through(relued, i, u + 1))
                            gated(pe, scanned, through(scanned, i, u - 1))
                            pe.matmul(ps[4 + u % 2][0:D, :], w3bt[:, :], act_sb[:, u % 2, :], start=True, stop=True
                                      ).then_inc(mixed, 1)
                            if left > 1:
                                turn_spread(i, u + 2)
                                turn_gathered(i, u + 2)
                            if not first(i, u):
                                turn_back(i, u - 1)
                            if not left:
                                turn_back(i, u)
                        else:
                            if left:
                                turn_gathered(i, u + 1)
                            turn_back(i, u)
                    for u in range(2 if kind == "max" else 1):
                        if spread:
                            turn_spread(0, u)
                        turn_gathered(0, u)
                    all_blocks(pe, body, side.get("tensor"))

                @block.vector
                def _(v):
                    def spread_over(i, u):
                        s = flag_in[u % FLAGS]
                        wait_for(v, s, landed(s, i, u, FLAGS, n_flags))
                        wait_for(v, heldt, through(heldt, i, u + 1))
                        wait_for(v, held_up, through(held_up, i, u))
                        wait_for(v, joined, through(joined, i, u - 1))
                        v.tensor_tensor_scan(held[0:W, u % 2, :], hold[0:W, u % FLAGS, :], ps[2 + u % 2][0:W, :],
                                             held[0:W, (u + 1) % 2, BLK - 1:BLK], ALU.mult, ALU.add).then_inc(held_up, 1)

                    def one_hot(i, u):
                        wait_for(v, turned_, through(turned_, i, u + 1 - RING))
                        v.tensor_tensor(G[:, u % RING, :, 2 * D:2 * D + R8], bcast(per_edge(i, u).bitcast(I32), R8),
                                        iota8[:, :].unsqueeze(1).to_broadcast([128, CPB, R8]),
                                        ALU.is_equal).then_inc(scaled, 1)

                    def scale_rows(i, u):
                        s = gathered[u % RING]
                        wait_for(v, s, landed(s, i, u, RING, 16 * CPB))
                        wait_for(v, turned_, through(turned_, i, u - 1))
                        v.tensor_tensor(GS[:, u % 2, :, 0:D], G[:, u % RING, :, 0:D], bcast(per_edge(i, u), D),
                                        ALU.mult).then_inc(scaled, 1)

                    def join(i, u, op):
                        wait_for(v, turned_, through(turned_, i, u + 1))
                        wait_for(v, held_up, through(held_up, i, u + 1))
                        used = mixed if kind == "score" else relued
                        wait_for(v, used, through(used, i, u - 1))
                        v.tensor_tensor(prod[0:W, u % 2, :], ps[u % 2][0:W, :], held[0:W, u % 2, :], op).then_inc(joined, 1)

                    def reduce_runs(i, u):
                        if kind == "max":
                            wait_for(v, mixed, through(mixed, i, u + 1))
                            flag, val, ops = cap[:, u % FLAGS, :], ps[4 + u % 2][0:D, :], (ALU.min, ALU.max)
                        else:
                            wait_for(v, turned_, through(turned_, i, u + 1))
                            s = flag_in[u % FLAGS]
                            wait_for(v, s, landed(s, i, u, FLAGS))
                            flag, val, ops = hold[0:D, u % FLAGS, :], ps[u % 2][0:D, :], (ALU.mult, ALU.add)
                        wait_for(v, scanned, through(scanned, i, u))
                        wait_for(v, backt, through(backt, i, u - 1))
                        v.tensor_tensor_scan(run[0:D, u % 2, :], flag, val, run[0:D, (u + 1) % 2, BLK - 1:BLK],
                                             *ops).then_inc(scanned, 1)

                    def body(i, u, left):
                        if kind == "score":
                            join(i, u, ALU.mult)
                            if left:
                                one_hot(i, u + 1)
                                spread_over(i, u + 1)
                        elif kind == "max":
                            if not first(i, u):
                                reduce_runs(i, u - 1)
                            if left:
                                spread_over(i, u + 1)
                                join(i, u + 1, ALU.add)
                            else:
                                reduce_runs(i, u)
                        else:
                            if scale and left:
                                scale_rows(i, u + 1)
                            reduce_runs(i, u)
                    if kind == "score":
                        one_hot(0, 0)
                    if spread:
                        spread_over(0, 0)
                    if kind == "max":
                        join(0, 0, ALU.add)
                    if scale:
                        scale_rows(0, 0)
                    all_blocks(v, body, side.get("vector"))

                @block.scalar
                def _(a):
                    def relu(i, u):
                        wait_for(a, joined, through(joined, i, u + 1))
                        wait_for(a, mixed, through(mixed, i, u - 1))
                        a.activation(act_sb[:, u % 2, :], prod[0:D, u % 2, :], ACT.Relu).then_inc(relued, 1)

                    def store_runs(i, u):
                        wait_for(a, backt, through(backt, i, u + 1))
                        wait_for(a, stored[u % 4], landed(stored[u % 4], i, u - 4, 4))
                        a.activation(O[:, u % 4, 0, :, :], ps[6 + u % 2][:, 0:CPB * D].rearrange("p (c f) -> p c f", c=CPB),
                                     ACT.Copy).then_inc(copied, 1)
                        gated(a, copied, through(copied, i, u + 1))
                        a.dma_start(blk(scan_d[0:EP, :])[i * BODY + u], O[:, u % 4, 0, :, :]).then_inc(stored[u % 4], 16)

                    def body(i, u, left):
                        b = i * BODY + u
                        if kind == "score":
                            gated(a, gathered[u], landed(gathered[u], i, u, RING, 16 * CPB))
                            a.dma_start(blk(msg_d)[b], G[:, u, :, 0:D]).then_inc(msg_out[u], 16)
                            wait_for(a, mixed, through(mixed, i, u + 1))
                            wait_for(a, stored[u % 4], landed(stored[u % 4], i, u - 4, 4))
                            a.activation(sc_sb[:, u % 4, :], ps[4 + u % 2][0:4, :], ACT.Copy, scale=D ** -0.5
                                         ).then_inc(copied, 1)
                            gated(a, copied, through(copied, i, u + 1))
                            a.dma_start(score_d.rearrange("r (b e) -> b r e", e=BLK)[b], sc_sb[:, u % 4, :]
                                        ).then_inc(stored[u % 4], 16)
                        elif kind == "max":
                            if left:
                                relu(i, u + 1)
                            if not first(i, u):
                                store_runs(i, u - 1)
                            if not left:
                                store_runs(i, u)
                        else:
                            store_runs(i, u)
                    if kind == "max":
                        relu(0, 0)
                    all_blocks(a, body, side.get("scalar"))

            for s, on in ((turned_, True), (scaled, scale or kind == "score"), (scanned, kind != "score"),
                          (heldt, spread), (held_up, spread), (joined, spread), (relued, kind == "max"),
                          (mixed, spread), (backt, kind != "score"), (copied, True)):
                sent[s.num] += NBP * on
            for j, s in enumerate(idx_in):
                sent[s.num] += 16 * len(range(j, -(-NBP // GRP), 3))
            for slots, by in ((flag_in, n_flags), (spread_in, 16 * spread), (gathered, 16 * CPB), (stored, 16),
                              (msg_out, 16 * (kind == "score"))):
                for j, s in enumerate(slots):
                    sent[s.num] += by * len(range(j, NBP, len(slots)))

        def per_edge(i, u):
            return scal[:, bass.ds(i * (BODY * CPB) + u * CPB, CPB)]

        def sweep_messages():
            two_in = gathered_m
            hold2 = hold_d[0:NBP * BLK].rearrange("(h b e) -> b h e", h=2, e=BLK)
            msg2, scan2 = (d[0:NBP * BLK, :].rearrange("(h b p c) f -> b p h c f", h=2, p=128, c=CPB) for d in (msg_d, scan_d))
            with nc.Block() as block:
                @block.sync
                def _(sp):
                    def body(i, u, left):
                        b = i * BODY + u
                        gated(sp, scanned, through(scanned, i, u + 1 - FLAGS))
                        sp.dma_start(hold[:, u % FLAGS, :], hold2[b].unsqueeze(1).to_broadcast([2, D, BLK])
                                     ).then_inc(flag_in[u % FLAGS], 16)
                        gated(sp, scaled, through(scaled, i, u - 3))
                        sp.dma_start(G2[:, u % 4], msg2[b]).then_inc(two_in[u % 4], 16)
                    pair_blocks(sp, body)
                    for j, s in enumerate(stored):
                        sp.wait_ge(s, sent[s.num] + 16 * len(range(j, HALF, 4)))

                @block.tensor
                def _(pe):
                    def turn(i, u):
                        wait_for(pe, scaled, through(scaled, i, u + 1))
                        gated(pe, scanned, through(scanned, i, u - 1))
                        for c in range(CPB):
                            last = pe.transpose(ps[u % 2][:, c:BLK:CPB], GS2[:, u % 2, c, :, :].rearrange("p h f -> p (h f)"),
                                                ident[:, :])
                        last.then_inc(turned_, 1)

                    def body(i, u, left):
                        if left:
                            turn(i, u + 1)
                        wait_for(pe, scanned, through(scanned, i, u + 1))
                        gated(pe, copied, through(copied, i, u - 1))
                        for c in range(CPB):
                            last = pe.transpose(ps[6 + u % 2][:, c * 128:(c + 1) * 128], run[:, u % 2, c:BLK:CPB], ident[:, :])
                        last.then_inc(backt, 1)
                    turn(0, 0)
                    pair_blocks(pe, body)

                @block.vector
                def _(v):
                    L = dve_line
                    L.step(v, v.memset(run[:, :, :], 0.0))

                    def scale_rows(i, u):
                        s = two_in[u % 4]
                        wait_for(v, s, landed(s, i, u, 4))
                        wait_for(v, turned_, through(turned_, i, u - 1))
                        for h in range(2):
                            ins = v.tensor_tensor(GS2[:, u % 2, :, h, :], G2[:, u % 4, h, :, :],
                                                  bcast(scal[:, bass.ds(i * (BODY * CPB) + (u + h * HALF) * CPB, CPB)], D),
                                                  ALU.mult)
                        ins.then_inc(scaled, 1)

                    def body(i, u, left):
                        if left:
                            scale_rows(i, u + 1)
                        wait_for(v, turned_, through(turned_, i, u + 1))
                        s = flag_in[u % FLAGS]
                        wait_for(v, s, landed(s, i, u, FLAGS))
                        wait_for(v, scanned, through(scanned, i, u))
                        wait_for(v, backt, through(backt, i, u - 1))
                        v.tensor_tensor_scan(run[:, u % 2, :], hold[:, u % FLAGS, :], ps[u % 2][:, :],
                                             run[:, (u + 1) % 2, BLK - 1:BLK], ALU.mult, ALU.add).then_inc(scanned, 1)
                    scale_rows(0, 0)
                    pair_blocks(v, body)

                @block.scalar
                def _(a):
                    def body(i, u, left):
                        b = i * BODY + u
                        wait_for(a, backt, through(backt, i, u + 1))
                        wait_for(a, stored[u % 4], landed(stored[u % 4], i, u - 4, 4))
                        a.activation(O[:, u % 4], ps[6 + u % 2][:, :].rearrange("p (c h f) -> p h c f", h=2, f=D), ACT.Copy
                                     ).then_inc(copied, 1)
                        gated(a, copied, through(copied, i, u + 1))
                        a.dma_start(scan2[b], O[:, u % 4]).then_inc(stored[u % 4], 16)
                    pair_blocks(a, body)

            for s in (turned_, scaled, scanned, backt, copied):
                sent[s.num] += HALF
            for slots in (flag_in, two_in, stored):
                for j, s in enumerate(slots):
                    sent[s.num] += 16 * len(range(j, HALF, len(slots)))

        gathered_m = [sem(f"messages_in{j}") for j in range(4)]
        sent.update({s.num: 0 for s in gathered_m})

        def pair_blocks(eng, body):
            for u in range(BODY):
                body(0, u, BODY)
            with eng.Fori(1, HALF // BODY) as i:
                for u in range(BODY):
                    body(i, u, BODY)
            for u in range(HALF % BODY):
                body(HALF // BODY, u, HALF % BODY - 1 - u)

        def blk(d):
            return d.rearrange("(b p c) f -> b p c f", p=128, c=CPB)

        def seg_bcast(d, b, parts):
            return d.rearrange("(b e) -> b e", e=BLK)[b].unsqueeze(0).to_broadcast([parts, BLK])

        def norm_phase():
            sqrts[0] += 1
            n = sqrts[0]
            with nc.Block() as block:
                @block.vector
                def _(v):
                    layer_norm(v, None, xn[:, :, :], hn[:, :, :], sqrt_req, sqrt_done, n, scratch)
                    dve_line.step(v, v.tensor_scalar(hn[:, :, :], hn[:, :, :], 0.0, None, ALU.max))

                @block.scalar
                def _(a):
                    sqrt_act(a, n)

        def store_table(dst_d):
            with nc.Block() as block:
                @block.sync
                def _(sp):
                    sp_line.step(sp, sp.dma_start(node(dst_d), hn[:, :, :]), 16)

        norm_phase()
        store_table(tab_d)
        sweep("sum", tab_d, A["src_it"], side=first_side)

        zin = sem("zin"); zup = sem("zup"); zcp = sem("zcp"); bnr = sem("bnr"); h1b = sem("h1b"); h1c = sem("h1c")
        with nc.Block() as block:
            @block.sync
            def _(sp):
                sp.wait_ge(zfill, n_zfill)

            @block.gpsimd
            def _(g):
                gather_ends(g)

            @block.vector
            def _(v):
                L = dve_line
                v.wait_ge(ends_rows, 16 * NK)
                L.step(v, v.tensor_tensor(gn[:, :, :], gn[:, :, :], hn[:, :, :], ALU.add))
                v.sem_inc(turn_in, 1)
                for c, (a0, w) in enumerate(CHUNKS):
                    v.wait_ge(zcp, c + 1)
                    L.step(v, v.bn_stats(bn[:, c, :], zT[:, a0:a0 + w]))
                L.step(v, v.bn_aggr(bnm[:, :], bn[:, :, :]))
                L.step(v, v.tensor_scalar(bnc[:, 0:1], bnm[:, 1:2], EPS, None, ALU.add))
                v.sem_inc(bnr, 1)
                v.wait_ge(bnr, 2)
                L.step(v, v.reciprocal(bnc[:, 2:3], bnc[:, 1:2]))
                L.step(v, v.tensor_tensor(bnc[:, 2:3], bnc[:, 2:3], cols[:, 1:2], ALU.mult))
                L.step(v, v.tensor_tensor(bnc[:, 3:4], bnm[:, 0:1], bnc[:, 2:3], ALU.mult))
                L.step(v, v.tensor_tensor(bnc[:, 3:4], cols[:, 2:3], bnc[:, 3:4], ALU.subtract))
                v.sem_inc(bnr, 1)

            @block.tensor
            def _(pe):
                turn_nodes(pe, gn, 0)
                pe.wait_ge(turn_act, 7)
                for c, (a0, w) in enumerate(CHUNKS):
                    if c >= 2:
                        pe.wait_ge(zcp, c - 1)
                    pe.matmul(ps[2 + c % 2][0:D, 0:w], w0a[:, :], hT[:, a0:a0 + w], start=True, stop=True).then_inc(zup, 1)
                pe.wait_ge(h1b, 1)
                for k in range(NK):
                    if k and k % 8 == 0:
                        pe.wait_ge(h1c, (k // 8) - 1) if k >= 16 else None
                    last = pe.transpose(ps[4 + (k // 8) % 2][0:NP, (k % 8) * D:(k % 8 + 1) * D], zT[:, k * NP:(k + 1) * NP],
                                        ident[0:D, 0:D])
                    if k % 8 == 7 or k == NK - 1:
                        last.then_inc(h1b, 1)

            @block.scalar
            def _(a):
                turn_copy(a, 0)
                for c, (a0, w) in enumerate(CHUNKS):
                    a.wait_ge(zup, c + 1)
                    a.activation(zT[:, a0:a0 + w], ps[2 + c % 2][0:D, 0:w], ACT.Identity, bias=cols[:, 0:1]).then_inc(zcp, 1)
                a.wait_ge(bnr, 1)
                a.activation(bnc[:, 1:2], bnc[:, 0:1], ACT.Sqrt).then_inc(bnr, 1)
                a.wait_ge(bnr, 3)
                a.activation(zT, zT, ACT.Relu, bias=bnc[:, 3:4], scale=bnc[:, 2:3]).then_inc(h1b, 1)
                for gidx in range(4):
                    w = min(8, NK - 8 * gidx)
                    a.wait_ge(h1b, gidx + 2)
                    a.copy(hn[:, 8 * gidx:8 * gidx + w, :].rearrange("p k f -> p (k f)"), ps[4 + gidx % 2][0:NP, 0:w * D]).then_inc(h1c, 1)

        store_table(tab_d)
        sweep("sum", tab_d, A["src_it"])
        turns[0] = 1

        def node_matmul(pe, rhs, width, lhs=None):
            lhs = hT if lhs is None else lhs
            base = mms[0]
            for k in range(NK):
                if k >= 2:
                    pe.wait_ge(mm_out, base + k - 1)
                pe.matmul(ps[2 + k % 2][0:NP, 0:width], lhs[:, k * NP:(k + 1) * NP], rhs, start=True, stop=True).then_inc(mm_pe, 1)

        def add_ends(v, other):
            v.wait_ge(ends_rows, ends_total[0])
            dve_line.step(v, v.tensor_tensor(gn[:, :, :], gn[:, :, :], other, ALU.add))

        ends_total = [16 * NK]

        ends_total[0] += 16 * NK
        with nc.Block() as block:
            @block.gpsimd
            def _(g):
                gather_ends(g)

            @block.vector
            def _(v):
                add_ends(v, hn[:, :, :])
                v.sem_inc(turn_in, 1)
                dve_line.step(v, v.tensor_tensor(xn[:, :, :], xn[:, :, :],
                                                 rows[:, 0, :].unsqueeze(1).to_broadcast([NP, NK, D]), ALU.add))
                for k in range(NK):
                    v.wait_ge(mm_pe, k + 1)
                    v.tensor_tensor(xn[:, k, :], xn[:, k, :], ps[2 + k % 2][0:NP, 0:D], ALU.add).then_inc(mm_out, 1)
                v.wait_ge(mm_out, NK)

            @block.tensor
            def _(pe):
                turn_nodes(pe, gn, 1)
                pe.wait_ge(turn_act, 14)
                node_matmul(pe, w0b[:, :], D)

            @block.scalar
            def _(a):
                turn_copy(a, 1)
        mms[0] += NK
        turns[0] = 2
        if dbg == 1:
            with nc.Block() as block:
                @block.sync
                def _(sp):
                    sp_line.step(sp, sp.dma_start(node(out), xn[:, :, :]), 16)
            return

        def conv_tables(w, b_row):
            t = turns[0]
            turns[0] += 1
            base = mms[0]
            H4 = [PB[0:NP, :], PC[0:NP, :]]
            v4 = lambda t_: H4[t_ // 2][:, (t_ % 2) * NK * D:(t_ % 2 + 1) * NK * D].rearrange("p (k f) -> p k f", f=D)
            with nc.Block() as block:
                @block.vector
                def _(v):
                    v.sem_inc(turn_in, 1)
                    for k in range(NK):
                        v.wait_ge(mm_pe, base + k + 1)
                        p = ps[2 + k % 2]
                        for h in range(2):
                            o = H4[h][:, 0:2 * NK * D].rearrange("p (t k f) -> p t k f", t=2, f=D)[:, :, k, :]
                            v.tensor_copy(o, p[0:NP, 2 * h * D:2 * (h + 1) * D].rearrange("p (t f) -> p t f", t=2))
                        v.tensor_tensor(rn[:, k, :], p[0:NP, R4 * D:(R4 + 1) * D], rows[:, b_row, :], ALU.add).then_inc(mm_out, 1)
                    v.wait_ge(mm_out, base + NK)
                    v.sem_inc(tab_up, 1)

                @block.tensor
                def _(pe):
                    turn_nodes(pe, hn, t)
                    pe.wait_ge(turn_act, 7 * (t + 1))
                    node_matmul(pe, w[:, :, :].rearrange("d r e -> d (r e)"), (R4 + 1) * D)

                @block.scalar
                def _(a):
                    turn_copy(a, t)

                @block.sync
                def _(sp):
                    tabs[0] += 1
                    sp.wait_ge(tab_up, tabs[0])
                    for t_ in range(R4):
                        sp.dma_start(node(tab4_d[t_ * N:(t_ + 1) * N, :]), v4(t_)).then_inc(tab_out, 16)
                    sp.wait_ge(tab_out, 16 * R4 * tabs[0])
            mms[0] += NK

        def ends_phase(finish):
            ends_total[0] += 16 * NK
            with nc.Block() as block:
                @block.gpsimd
                def _(g):
                    gather_ends(g)

                @block.vector
                def _(v):
                    add_ends(v, rn[:, :, :])
                    finish(v, dve_line)

        norm_phase()
        conv_tables(w1a, 1)
        sweep("sum", tab4_d, idx4_d, scale=True)
        ends_phase(lambda v, L: L.step(v, v.tensor_scalar(hn[:, :, :], gn[:, :, :], 0.0, None, ALU.max)))
        conv_tables(w1b, 2)
        sweep("sum", tab4_d, idx4_d, scale=True)
        ends_phase(lambda v, L: L.step(v, v.tensor_tensor(xn[:, :, :], xn[:, :, :], gn[:, :, :], ALU.add)))
        norm_phase()
        if dbg == 2:
            with nc.Block() as block:
                @block.sync
                def _(sp):
                    sp_line.step(sp, sp.dma_start(node(out), xn[:, :, :]), 16)
            return

        w_rel = sem("w_rel"); w_tr = sem("w_tr"); w_cp = sem("w_cp"); emb_in = sem("emb_in"); q_pe = sem("q_pe"); q_cp = sem("q_cp")
        with nc.Block() as block:
            @block.gpsimd
            def _(g):
                g.indirect_dma_start(emb[:, :], None, A["L2_gnn_rule_emb"],
                                     bass.IndirectOffsetOnAxis(ap=rid[:, 0:1], axis=0)).then_inc(emb_in, 16)
                g.wait_ge(emb_in, 16)

            @block.vector
            def _(v):
                L = dve_line
                L.step(v, v.tensor_reduce(relT[:, :], w2r[:, :, :], AX.X, ALU.add))
                L.step(v, v.tensor_scalar(relT[:, :], relT[:, :], 1.0 / D, None, ALU.mult))
                v.sem_inc(w_rel, 1)
                v.wait_ge(w_tr, 1)
                L.step(v, v.tensor_copy(m2[:, 0:D], ps[0][0:D, 0:D]))
                L.step(v, v.tensor_copy(embT[:, :], ps[0][0:D, D:D + 4]))
                L.step(v, v.tensor_copy(w3t[:, 0, :], ps[0][0:D, 2 * D:3 * D]))
                L.step(v, v.tensor_tensor(w3t[:, 1, :], ps[0][0:D, 3 * D:4 * D], w3t[:, 0, :], ALU.subtract))
                L.step(v, v.tensor_copy(w3bt[:, :], ps[0][0:D, 4 * D:5 * D]))
                v.sem_inc(w_cp, 1)
                v.wait_ge(w_tr, 2)
                L.step(v, v.tensor_scalar(m2[:, D:D + R8], ps[1][0:D, 0:R8], cols[:, 4:5], None, ALU.add))
                L.step(v, v.tensor_copy(m2[:, D + R8:RW], ps[1][0:D, R8:R8 + 4]))

            @block.tensor
            def _(pe):
                pe.wait_ge(emb_in, 16)
                pe.transpose(ps[0][0:D, 0:D], wk[:, 0, :], ident[0:D, 0:D])
                pe.transpose(ps[0][0:D, D:D + 4], emb[:, :], ident[0:4, 0:4])
                pe.transpose(ps[0][0:D, 2 * D:3 * D], w3[:, D:2 * D], ident[0:D, 0:D])
                pe.transpose(ps[0][0:D, 3 * D:4 * D], w3[:, 0:D], ident[0:D, 0:D])
                pe.transpose(ps[0][0:D, 4 * D:5 * D], w3b[:, :], ident[0:D, 0:D]).then_inc(w_tr, 1)
                pe.wait_ge(w_rel, 1)
                pe.wait_ge(w_cp, 1)
                pe.matmul(ps[1][0:D, 0:R8], wk[:, 1, :], relT[:, :], start=True, stop=True)
                pe.matmul(ps[1][0:D, R8:R8 + 4], wk[:, 2, :], embT[:, :], start=True, stop=True).then_inc(w_tr, 1)

        t = turns[0]
        turns[0] += 1
        base = mms[0]
        R_nm = rn
        rrows = PC[0:NP, 0:NK * RW].rearrange("p (k f) -> p k f", f=RW)
        T8 = PC[0:NP, NK * RW:NK * RW + 4 * R8 * 2 * D // 4 * 1]
        t8buf = [PC[0:NP, 2048 + 1024 * s:2048 + 1024 * (s + 1)].rearrange("p (t f) -> p t f", t=R8) for s in range(4)]
        t8_out = [sem(f"t8_out{s}") for s in range(4)]
        spread_out = sem("spread_out"); rr_up = sem("rr_up"); t8_up = sem("t8_up")
        qT = zT

        def scatter_rows(g, n):
            for k in range(NK):
                g.indirect_dma_start(spread_d, bass.IndirectOffsetOnAxis(ap=start_idx[:, k:k + 1], axis=0),
                                     rrows[:, k, :], None).then_inc(spread_out, 16)
            g.wait_ge(spread_out, n)

        with nc.Block() as block:
            @block.vector
            def _(v):
                L = dve_line
                v.sem_inc(turn_in, 1)
                for k in range(NK):
                    v.wait_ge(mm_pe, base + k + 1)
                    v.tensor_copy(rrows[:, k, :], ps[2 + k % 2][0:NP, 0:RW]).then_inc(mm_out, 1)
                v.wait_ge(mm_out, base + NK)
                v.sem_inc(rr_up, 1)
                for k in range(NK):
                    v.wait_ge(mm_pe, base + NK + k + 1)
                    if k >= 4:
                        v.wait_ge(t8_out[k % 4], 16 * (k // 4))
                    v.tensor_copy(t8buf[k % 4][:, :, D:2 * D], hn[:, k, :].unsqueeze(1).to_broadcast([NP, R8, D]))
                    v.tensor_copy(t8buf[k % 4][:, :, 0:D], ps[2 + k % 2][0:NP, :].rearrange("p (t f) -> p t f", t=R8)
                                  ).then_inc(mm_out, 1)

            @block.tensor
            def _(pe):
                turn_nodes(pe, hn, t)
                pe.wait_ge(turn_act, 7 * (t + 1))
                for c, (a0, w) in enumerate(CHUNKS):
                    if c >= 2:
                        pe.wait_ge(q_cp, c - 1)
                    pe.matmul(ps[4 + c % 2][0:D, 0:w], wq[:, :], hT[:, a0:a0 + w], start=True, stop=True).then_inc(q_pe, 1)
                pe.wait_ge(q_cp, len(CHUNKS))
                node_matmul(pe, m2[:, :], RW, qT)
                mms[0] += NK
                pe.wait_ge(mm_out, mms[0])
                node_matmul(pe, w2r[:, :, :].rearrange("d r e -> d (r e)"), R8 * D)
                mms[0] += NK

            @block.scalar
            def _(a):
                turn_copy(a, t)
                for c, (a0, w) in enumerate(CHUNKS):
                    a.wait_ge(q_pe, c + 1)
                    a.activation(qT[:, a0:a0 + w], ps[4 + c % 2][0:D, 0:w], ACT.Identity, bias=cols[:, 3:4]).then_inc(q_cp, 1)

            @block.gpsimd
            def _(g):
                g.wait_ge(rr_up, 1)
                scatter_rows(g, 16 * NK)

            @block.sync
            def _(sp):
                sp_line.step(sp, sp.dma_start(em3(scal[:, :].bitcast(I32)), em(A["t8_it"])), 16)
                tv = tab8_d.rearrange("(t p k) f -> k p t f", t=R8, k=NK)
                for k in range(NK):
                    sp.wait_ge(mm_out, base + NK + k + 1)
                    sp.dma_start(tv[k], t8buf[k % 4]).then_inc(t8_out[k % 4], 16)
                for s in range(4):
                    sp.wait_ge(t8_out[s], 16 * len(range(s, NK, 4)))

        sweep("score", tab8_d, idx8_d)

        s_in = sem("s_in"); exp_req = sem("exp_req"); exp_done = sem("exp_done")
        with nc.Block() as block:
            a_, b_, c_ = (t_[0:PQ, 0:PL] for t_ in (PA, PB, PC))
            capp = c_[:, 0:PL // 2].bitcast(BF16)
            attrow = PB[0:PCS, 0:PL]

            @block.sync
            def _(sp):
                for r in range(4):
                    sp.dma_start(PA[r * PCS:(r + 1) * PCS, 0:PL], score_d[r].rearrange("(i f) -> i f", i=PCS)).then_inc(s_in, 16)

            @block.vector
            def _(v):
                L = dve_line
                v.wait_ge(s_in, 64)
                L.step(v, v.tensor_scalar(b_, same_prev[:, :], 0.5, 2.0, ALU.subtract, ALU.mult))
                L.step(v, v.tensor_scalar(capp, b_, BIG, None, ALU.mult))
                L.step(v, v.tensor_scalar(small[0:PQ, 7, 0:1], small[0:PQ, 6, 3:4], BIG, None, ALU.mult))
                scan_pieces(v, b_, capp, small[0:PQ, 7, 0:1], a_, ALU.min, ALU.max, -BIG, False)
                L.step(v, v.tensor_tensor(b_, b_, last_of_run[:, :], ALU.mult))
                scan_pieces(v, c_, same_next, small[0:PQ, 6, 1:2], b_, ALU.mult, ALU.add, 0.0, True)
                L.step(v, v.tensor_tensor(a_, a_, c_, ALU.subtract))
                v.sem_inc(exp_req, 1)
                v.wait_ge(exp_done, 1)
                scan_pieces(v, b_, same_prev, small[0:PQ, 6, 0:1], a_, ALU.mult, ALU.add, 0.0, False)
                L.step(v, v.tensor_tensor(b_, b_, last_of_run[:, :], ALU.mult))
                scan_pieces(v, c_, same_next, small[0:PQ, 6, 1:2], b_, ALU.mult, ALU.add, 0.0, True)
                L.step(v, v.reciprocal(b_, c_))
                L.step(v, v.tensor_tensor(a_, a_, b_, ALU.mult))
                L.step(v, v.tensor_scalar(a_, a_, 0.25, None, ALU.mult))
                v.sem_inc(kinds_up, 1)
                edge_major_out(v, scal[:, :], 2)

            @block.tensor
            def _(pe):
                for j in range(4):
                    carry_pe(pe, 3 + j, j % 2 == 1)
                fold_pe(pe, pa, attrow, 2)

            @block.scalar
            def _(a):
                a.wait_ge(exp_req, 1)
                a.activation(a_, a_, ACT.Exp).then_inc(exp_done, 1)
                fold_act(a, attrow, 2)

        sweep_messages()

        sqrts[0] += 1
        n_sq = sqrts[0]
        ends_total[0] += 16 * NK
        rb = lambda j: rows[:, j, :].unsqueeze(1).to_broadcast([NP, NK, D])
        seam_in = sem("seam_in")
        with nc.Block() as block:
            @block.sync
            def _(sp):
                sp.dma_start(PC[0:NP, 1600:1600 + D], row_bcast(scan_d[HALF * BLK - 1, :], NP, D)).then_inc(seam_in, 16)
                sp.wait_ge(seam_in, 16)

            @block.gpsimd
            def _(g):
                gather_ends(g)

            @block.vector
            def _(v):
                L = dve_line
                add_ends(v, rb(3))
                v.wait_ge(seam_in, 16)
                seam = PC[0:NP, 1600:1600 + D]
                L.step(v, v.tensor_tensor(rn[:, :, :], seam.unsqueeze(1).to_broadcast([NP, NK, D]),
                                          bcast(straddle[:, :], D), ALU.mult))
                L.step(v, v.tensor_tensor(gn[:, :, :], gn[:, :, :], rn[:, :, :], ALU.add))
                layer_norm(v, None, gn[:, :, :], rn[:, :, :], sqrt_req, sqrt_done, n_sq, scratch)
                L.step(v, v.tensor_tensor(rn[:, :, :], rn[:, :, :], rb(4), ALU.mult))
                L.step(v, v.tensor_tensor(rn[:, :, :], rn[:, :, :], rb(5), ALU.add))
                L.step(v, v.tensor_scalar(rn[:, :, :], rn[:, :, :], 0.0, None, ALU.max))
                L.step(v, v.tensor_tensor(xn[:, :, :], xn[:, :, :], rn[:, :, :], ALU.add))

            @block.scalar
            def _(a):
                sqrt_act(a, n_sq)
        norm_phase()
        if dbg == 3:
            with nc.Block() as block:
                @block.sync
                def _(sp):
                    sp_line.step(sp, sp.dma_start(node(out), xn[:, :, :]), 16)
            return

        t = turns[0]
        turns[0] += 1
        base = mms[0]
        s3_out = sem("s3_out")
        with nc.Block() as block:
            @block.vector
            def _(v):
                L = dve_line
                v.sem_inc(turn_in, 1)
                L.step(v, v.memset(rrows[:, :, D:RW], 0.0))
                for k in range(NK):
                    v.wait_ge(mm_pe, base + k + 1)
                    v.tensor_copy(rn[:, k, :], ps[2 + k % 2][0:NP, 0:D])
                    v.tensor_tensor(rrows[:, k, 0:D], ps[2 + k % 2][0:NP, D:2 * D], rows[:, 6, :], ALU.add).then_inc(mm_out, 1)
                v.wait_ge(mm_out, base + NK)
                v.sem_inc(rr_up, 1)

            @block.tensor
            def _(pe):
                turn_nodes(pe, hn, t)
                pe.wait_ge(turn_act, 7 * (t + 1))
                node_matmul(pe, w3t[:, :, :].rearrange("d r e -> d (r e)"), 2 * D)

            @block.scalar
            def _(a):
                turn_copy(a, t)

            @block.gpsimd
            def _(g):
                g.wait_ge(rr_up, 2)
                scatter_rows(g, 32 * NK)

            @block.sync
            def _(sp):
                sp.wait_ge(rr_up, 2)
                sp.dma_start(node(tab_d), rn[:, :, :]).then_inc(s3_out, 16)
                sp.wait_ge(s3_out, 16)

        sweep("max", tab_d, A["src_it"])

        fin = sem("fin"); fin_out = sem("fin_out")
        with nc.Block() as block:
            @block.gpsimd
            def _(g):
                gather_ends(g)

            @block.vector
            def _(v):
                L = dve_line
                L.step(v, v.tensor_tensor(rn[:, :, :], rb(7), bcast(nonempty[:, :], D), ALU.mult))
                ends_total[0] += 16 * NK
                add_ends(v, rn[:, :, :])
                L.step(v, v.tensor_tensor(xn[:, :, :], xn[:, :, :], gn[:, :, :], ALU.add))
                v.sem_inc(fin, 1)

            @block.sync
            def _(sp):
                sp.wait_ge(fin, 1)
                sp.dma_start(node(out), xn[:, :, :]).then_inc(fin_out, 16)
                sp.wait_ge(fin_out, 16)


_FLOATS = ['x', 'L0_gnn_W1', 'L0_gnn_b1', 'L0_gnn_gamma1', 'L0_gnn_beta1', 'L0_gnn_W2', 'L0_gnn_b2', 'L1_gnn_W1',
           'L1_gnn_root1', 'L1_gnn_b1', 'L1_gnn_W2', 'L1_gnn_root2', 'L1_gnn_b2', 'L2_gnn_W_r', 'L2_gnn_Wq_w',
           'L2_gnn_Wq_bias', 'L2_gnn_Wk_w', 'L2_gnn_Wk_bias', 'L2_gnn_rule_emb', 'L2_gnn_bias', 'L2_gnn_ln_g',
           'L2_gnn_ln_b', 'L3_gnn_W1', 'L3_gnn_b1', 'L3_gnn_W2', 'L3_gnn_b2']
_COLUMNS = ['L0_gnn_b1', 'L0_gnn_gamma1', 'L0_gnn_beta1', 'L2_gnn_Wq_bias', 'L2_gnn_Wk_bias']
DBG = 0


def kernel(**inputs):
    import numpy as _np
    import concourse.bacc as _bacc
    from concourse import mybir as _mybir
    from concourse.bass_utils import run_bass_kernel_spmd as _run

    def padded(name, fill):
        a = _np.asarray(inputs[name])
        return _np.concatenate([a, _np.full(EP - E, fill, a.dtype)])

    def by_group(a):
        return _np.ascontiguousarray(a.reshape(NG, GRP, 128, CPB).transpose(0, 2, 1, 3).reshape(NG, 128, GC))

    host = {n: _np.ascontiguousarray(inputs[n]) for n in _FLOATS}
    for n in _COLUMNS:
        host[n] = host[n].reshape(D, 1)
    dst = padded("dst", N)
    none = _np.full(1, -1, dst.dtype)
    host["dst_ext"] = _np.concatenate([none, dst, none])
    host["dst_rows"] = dst.reshape(HEADS, 128)
    host["dst_heads"] = _np.ascontiguousarray(dst[::128])
    host["src_it"] = by_group(padded("src", 0))
    t4, t8 = padded("edge_type_4", 0), padded("edge_type_8", 0)
    host["t4_nat"] = t4
    host["t4_it"] = by_group(t4)
    host["t8_it"] = by_group(t8)
    host["rule_ids"] = _np.asarray(inputs["L2_gnn_rule_ids"]).reshape(4, 1)

    nc = _bacc.Bacc("TRN2", target_bir_lowering=False, num_devices=1)
    arrays = {f"in_{n}": a for n, a in host.items()}
    A = {n: nc.dram_tensor(f"in_{n}", a.shape, _mybir.dt.from_np(a.dtype), kind="ExternalInput").ap()
         for n, a in host.items()}
    out = nc.dram_tensor("out", (N, D), F32, kind="ExternalOutput").ap()
    build(nc, A, out, DBG)
    r = _run(nc, [arrays], core_ids=[0])
    return r.results[0]["out"]
```

```python
from contextlib import ExitStack

import concourse.bass as bass
from concourse import mybir

F32 = mybir.dt.float32
BF16 = mybir.dt.bfloat16
I32 = mybir.dt.int32
ALU = mybir.AluOpType
ACT = mybir.ActivationFunctionType
AX = mybir.AxisListType

N = 3125
D = 64
NP = 125
NK = N // NP
E = 103125
BLK = 512
CPB = BLK // 128
BODY = 12
NBP = -(-E // BLK)
NBP += NBP % 2
TURNS, TAIL = divmod(NBP, BODY)
BPP = 8
PCS = -(-NBP // BPP)
NB = PCS * BPP
EP = NB * BLK
FLAGS = 6
RING = BODY
GRP = 4
NG = NB // GRP
GC = GRP * CPB
PL = EP // PCS
PQ = 4 * PCS
R4, R8 = 4, 8
RW = D + R8 + 4
ZROW = EP
BIG = 3.3e38
HEADS = EP // 128
HALF = NBP // 2
EPS = 1e-5
QUADS = -(-NK // 4)
GROUPS = ((0, 4), (4, 8), (12, 8), (20, 5))


def slots(j):
    return slice(GROUPS[j][0], sum(GROUPS[j]))


def quads(j):
    return [(k // 4, range(k, min(k + 4, sum(GROUPS[j])))) for k in range(GROUPS[j][0], sum(GROUPS[j]), 4)]


def build(nc, A, out):
    with ExitStack() as ctx:
        def sb(name, shape, dt=F32):
            return ctx.enter_context(nc.sbuf_tensor(name, shape, dt))

        def dram(name, shape, dt=F32):
            return nc.dram_tensor(name, shape, dt, kind="Internal").ap()

        def sem(name):
            return ctx.enter_context(nc.semaphore(name))

        hold_d = dram("hold_d", [EP], BF16)
        cap_d = dram("cap_d", [EP], BF16)
        ends_d = dram("ends_d", [N + 1], F32)
        idx4_d = dram("idx4_d", [NG, 128, GC], I32)
        idx8_d = dram("idx8_d", [NG, 128, GC], I32)
        scan_d = dram("scan_d", [EP + 1, D])
        tab_d = dram("tab_d", [N, D])
        tab4_d = dram("tab4_d", [R4 * N, D])
        tab8_d = dram("tab8_d", [R8 * N, 2 * D])
        spread_d = dram("spread_d", [EP + N, RW])
        msg_d = dram("msg_d", [EP, D])
        score_d = dram("score_d", [4, EP])

        PA = sb("PA", [128, PL])
        PB = sb("PB", [128, PL])
        PC = sb("PC", [128, R4 * NK * D])
        same_prev = sb("same_prev", [PQ, PL], BF16)
        same_next = sb("same_next", [PQ, PL], BF16)
        last_of_run = sb("last_of_run", [PQ, PL], BF16)
        ident = sb("ident", [128, 128])
        iota8 = sb("iota8", [128, R8])
        ones = sb("ones", [128, 4])
        end_idx = sb("end_idx", [NP, NK], I32)
        start_idx = sb("start_idx", [NP, NK], I32)
        nonempty = sb("nonempty", [NP, NK])
        xn = sb("xn", [NP, NK, D])
        hn = sb("hn", [NP, NK, D])
        rn = sb("rn", [NP, NK, D])
        gn = sb("gn", [NP, NK, D])
        small = sb("small", [128, 8, 32])
        straddle = sb("straddle", [NP, NK])
        fold = sb("fold", [PQ, PCS])
        srow = sb("srow", [1, 3, PQ + 1])
        scol = sb("scol", [PQ, 4])
        G = sb("G", [128, RING, CPB, D + RW])
        GS = sb("GS", [128, 2, CPB, 2 * D])
        EX = sb("EX", [128, 3, CPB, RW])
        idx = sb("idx", [128, 3, GC], I32)
        scal = sb("scal", [128, NB * CPB])
        G2 = G[:, :, :, :].rearrange("p r c w -> p (r c w)")[:, 0:4 * CPB * 2 * D].rearrange(
            "p (s h c f) -> p s h c f", s=4, c=CPB, h=2)
        GS2 = GS[:, :, :, :].rearrange("p s c (h f) -> p s c h f", h=2)
        hold = sb("hold", [128, FLAGS, BLK], BF16)
        cap = sb("cap", [D, FLAGS, BLK], BF16)
        held = sb("held", [RW, 2, BLK])
        prod = sb("prod", [RW, 2, BLK])
        act_sb = sb("act_sb", [D, 2, BLK])
        run = sb("run", [128, 2, BLK])
        O = sb("O", [128, 4, 2, CPB, D])
        sc_sb = O[0:4].rearrange("r s h c f -> r s (h c f)")
        w0a = sb("w0a", [D, D]); w0b = sb("w0b", [D, D])
        w1a = sb("w1a", [D, R4 + 1, D]); w1b = sb("w1b", [D, R4 + 1, D])
        w2r = sb("w2r", [D, R8, D])
        wq = sb("wq", [D, D]); wk = sb("wk", [D, 3, D]); m2 = sb("m2", [D, RW])
        w3 = sb("w3", [D, 2 * D]); w3t = sb("w3t", [D, 2, D]); w3b = sb("w3b", [D, D]); w3bt = sb("w3bt", [D, D])
        emb = sb("emb", [4, D]); embT = sb("embT", [D, 4]); relT = sb("relT", [D, R8]); rid = sb("rid", [4, 1], I32)
        cols = sb("cols", [D, 8])
        rows = sb("rows", [NP, 8, D])
        w4 = sb("w4", [RW, 4])
        bn = sb("bn", [D, QUADS, 6]); bnm = sb("bnm", [D, 2]); bnc = sb("bnc", [D, 4])

        ps = [ctx.enter_context(nc.psum_tensor(f"ps{i}", [128, 512], F32)) for i in range(8)]

        armed = sem("armed")

        class Line:
            def __init__(self, name):
                self.s, self.n = sem(name), 0

            def step(self, eng, ins, by=1):
                self.n += by
                ins.then_inc(self.s, by)
                eng.wait_ge(self.s, self.n)

        dve_line, pool_line = Line("dve_line"), Line("pool_line")

        def bcast(ap, n):
            return ap.unsqueeze(len(ap.shape)).to_broadcast(list(ap.shape) + [n])

        def row_bcast(v, parts, n):
            return bass.AP(tensor=v.tensor, offset=v.offset, ap=[[0, parts], [1, n]])

        node = lambda d: d.rearrange("(p k) f -> p k f", p=NP)
        P_ = lambda t: t[:, :]

        zeros = PC[:, PL:]

        carry_req = sem("carry_req"); carry_row = sem("carry_row"); carry_back = sem("carry_back"); carry_col = sem("carry_col")
        carries = [0]

        def scan_pieces(v, dst, flag, flag_min, val, op0, op1, rest, back):
            L = dve_line
            w = slice(None, None, -1) if back else slice(None)
            far = 0 if back else PL - 1
            L.step(v, v.tensor_tensor_scan(dst[:, w], flag[:, w], val[:, w], rest, op0, op1))
            L.step(v, v.tensor_copy(scol[:, 0:1], dst[:, far:far + 1]))
            L.step(v, v.tensor_copy(scol[:, 1:2], flag_min))
            c = carries[0] = carries[0] + 1
            v.sem_inc(carry_req, 1)
            v.wait_ge(carry_row, c)
            L.step(v, v.tensor_copy(srow[:, 0, 0:PQ], ps[2][0:1, 0:PQ]))
            L.step(v, v.tensor_copy(srow[:, 1, 0:PQ], ps[2][0:1, PQ:2 * PQ]))
            L.step(v, v.memset(srow[:, 2, :], rest))
            if back:
                L.step(v, v.tensor_tensor_scan(srow[:, 2, 0:PQ][:, ::-1], srow[:, 1, 0:PQ][:, ::-1],
                                               srow[:, 0, 0:PQ][:, ::-1], rest, op0, op1))
            else:
                L.step(v, v.tensor_tensor_scan(srow[:, 2, 1:PQ + 1], srow[:, 1, 0:PQ], srow[:, 0, 0:PQ],
                                               rest, op0, op1))
            v.sem_inc(carry_back, 1)
            v.wait_ge(carry_col, c)
            L.step(v, v.tensor_copy(scol[:, 2:3], ps[3][0:PQ, 0:1]))
            L.step(v, v.tensor_tensor_scan(dst[:, w], flag[:, w], val[:, w], scol[:, 2:3], op0, op1))

        def carry_pe(pe, c, back):
            pe.wait_ge(carry_req, c)
            pe.matmul(ps[2][0:1, 0:PQ], scol[:, 0:1], ident[0:PQ, 0:PQ], start=True, stop=True)
            pe.matmul(ps[2][0:1, PQ:2 * PQ], scol[:, 1:2], ident[0:PQ, 0:PQ], start=True, stop=True).then_inc(carry_row, 1)
            pe.wait_ge(carry_back, c)
            init = srow[:, 2, 1:PQ + 1] if back else srow[:, 2, 0:PQ]
            pe.matmul(ps[3][0:PQ, 0:1], init, ones[0:1, 0:1], start=True, stop=True).then_inc(carry_col, 1)

        kinds_up = sem("kinds_up"); folded = sem("folded"); fold_out = sem("fold_out"); edge_major = sem("edge_major")
        FC = PL // 512
        TB = BPP * CPB // 2

        def fold_pe(pe, src, rowt, n):
            pe.wait_ge(kinds_up, n)
            for j in range(FC):
                if j >= 2:
                    pe.wait_ge(fold_out, (n - 1) * FC + j - 1)
                pe.matmul(ps[2 + j % 2][0:PCS, :], fold[:, :], src[:, 512 * j:512 * (j + 1)], start=True, stop=True
                          ).then_inc(folded, 1)
            pe.wait_ge(fold_out, n * FC)
            for j in range(2 * TB):
                b, c = divmod(j, CPB)
                last = pe.transpose(ps[4 + j // TB][:, (j % TB) * PCS:(j % TB + 1) * PCS],
                                    rowt[:, 512 * b + c:512 * (b + 1):CPB], ident[0:PCS, 0:PCS])
            last.then_inc(edge_major, 1)

        def fold_act(a, rowt, n, scale=1.0):
            for j in range(FC):
                a.wait_ge(folded, (n - 1) * FC + j + 1)
                a.activation(rowt[:, 512 * j:512 * (j + 1)], ps[2 + j % 2][0:PCS, :], ACT.Copy, scale=scale).then_inc(fold_out, 1)

        def edge_major_out(v, dst, n):
            v.wait_ge(edge_major, n)
            for h in range(2):
                dve_line.step(v, v.tensor_copy(dst.rearrange("p (i j) -> p j i", i=PCS)[:, TB * h:TB * h + TB, :],
                                               ps[4 + h][:, 0:TB * PCS].rearrange("p (j i) -> p j i", i=PCS)))

        srcs = PA[:, 0:HEADS].bitcast(I32)
        t4s = PA[:, HEADS:2 * HEADS].bitcast(I32)
        t8s = PA[:, 2 * HEADS:3 * HEADS].bitcast(I32)
        heads_i = PA[0:NP, 3 * HEADS:4 * HEADS].bitcast(I32)
        nid_i = PA[0:NP, 4 * HEADS:4 * HEADS + NK].bitcast(I32)
        em = lambda d: d.rearrange("g p c -> p g c")
        em3 = lambda t: t.rearrange("p (g c) -> p g c", c=GC)
        types_in = sem("types_in"); idx_up = sem("idx_up"); idx_out = sem("idx_out"); nid_up = sem("nid_up")
        rows_at = sem("rows_at"); rows_in = sem("rows_in"); ends_up = sem("ends_up"); ends_out = sem("ends_out")
        ends_in = sem("ends_in"); pieces_in = sem("pieces_in"); onehot_at = sem("onehot_at"); kinds_in = sem("kinds_in")
        zfill = sem("zfill")
        nid, cnt, rowc, end, start, tmp = (small[0:NP, j, 0:NK] for j in (0, 1, 2, 3, 4, 6))
        rowc_i = small[0:NP, 5, 0:NK].bitcast(I32)
        drows = PC[0:NP, 0:NK * 128].bitcast(I32).rearrange("p (k c) -> p k c", c=128)
        pa, pb, pc = (t[0:PQ, 0:PL] for t in (PA, PB, PC))

        def load_types(sp):
            for dst, src in ((em3(srcs), em(A["src_it"])), (em3(t4s), em(A["t4_it"])), (em3(t8s), em(A["t8_it"])),
                             (heads_i, row_bcast(A["dst_heads"], NP, HEADS))):
                sp.dma_start(dst, src).then_inc(types_in, 16)

        wide = zeros.shape[1]
        whole, rest = divmod((EP + N) * RW, 128 * wide)
        cuts = [(j * 128 * wide, 128, wide) for j in range(whole)]
        cuts += [(whole * 128 * wide, 128, rest // 128), ((EP + N) * RW - rest % 128, 1, rest % 128)]
        cuts = [c for c in cuts if c[2]]
        FILL = -(-len(cuts) // (TURNS - 1))
        n_zfill = 16 * (len(cuts) + 3 + NB - NBP)

        def zero_fill(turn):
            def fill(a):
                flat = spread_d.rearrange("a b -> (a b)")
                for at_, p, w in cuts[(turn - 1) * FILL:turn * FILL]:
                    a.dma_start(flat[at_:at_ + p * w].rearrange("(p f) -> p f", p=p), zeros[0:p, 0:w]).then_inc(zfill, 16)
                if turn > 1:
                    return
                a.dma_start(ends_d[0:1].rearrange("(p f) -> p f", p=1), zeros[0:1, 0:1]).then_inc(zfill, 16)
                a.dma_start(scan_d[ZROW:ZROW + 1, :], zeros[0:1, 0:D]).then_inc(zfill, 16)
                a.dma_start(scan_d[NBP * BLK:EP, :].rearrange("(p r) f -> p (r f)", p=128),
                            zeros[:, 0:(NB - NBP) * CPB * D]).then_inc(zfill, 16)
                for b in range(NBP, NB):
                    a.dma_start(score_d[:, b * BLK:(b + 1) * BLK], zeros[0:4, 0:BLK]).then_inc(zfill, 16)
            return fill

        def node_numbers(g):
            pool_line.step(g, g.iota(nid_i, [[1, NK]], base=0, channel_multiplier=NK))
            g.sem_inc(nid_up, 1)

        def count_rows(v):
            L = dve_line
            v.wait_ge(types_in, 64)
            for t in (t4s, t8s):
                L.step(v, v.tensor_scalar(PB[:, 0:HEADS], t, float(N), None, ALU.mult))
                L.step(v, v.tensor_tensor(t, PB[:, 0:HEADS], srcs, ALU.add))
            v.sem_inc(idx_up, 1)
            v.wait_ge(nid_up, 1)
            L.step(v, v.tensor_copy(nid, nid_i))
            heads = PB[0:NP, HEADS:2 * HEADS]
            L.step(v, v.tensor_copy(heads, heads_i))
            for k in range(NK):
                L.step(v, v.tensor_scalar(PB[0:NP, 0:HEADS], heads, nid[:, k:k + 1], 0.0, ALU.is_le, ALU.add,
                                          accum_out=cnt[:, k:k + 1]))
            L.step(v, v.tensor_scalar(rowc, cnt, -1.0, 0.0, ALU.add, ALU.max))
            L.step(v, v.tensor_copy(rowc_i, rowc))
            v.sem_inc(rows_at, 1)

        def store_indices(sp):
            sp.wait_ge(idx_up, 1)
            sp.dma_start(em(idx4_d), em3(t4s)).then_inc(idx_out, 16)
            sp.dma_start(em(idx8_d), em3(t8s)).then_inc(idx_out, 16)

        def gather_rows(g):
            g.wait_ge(rows_at, 1)
            for k in range(NK):
                g.indirect_dma_start(drows[:, k, :], None, A["dst_rows"],
                                     bass.IndirectOffsetOnAxis(ap=rowc_i[:, k:k + 1], axis=0)).then_inc(rows_in, 16)

        def find_ends(v):
            L = dve_line
            v.wait_ge(rows_in, 16 * NK)
            le = PB[0:NP, 0:NK * 128].rearrange("p (k c) -> p k c", c=128)
            L.step(v, v.tensor_tensor(le, drows, bcast(nid, 128), ALU.is_le))
            L.step(v, v.tensor_reduce(cnt, le, AX.X, ALU.add))
            L.step(v, v.scalar_tensor_tensor(end, rowc, 128.0, cnt, ALU.mult, ALU.add))
            v.sem_inc(ends_up, 1)

        def exchange_ends(sp):
            sp.wait_ge(ends_up, 1)
            sp.wait_ge(idx_out, 32)
            sp.dma_start(ends_d[1:N + 1].rearrange("(p k) -> p k", p=NP), end).then_inc(ends_out, 16)
            dx = A["dst_ext"]
            for t in range(4):
                q = slice(t * PCS, (t + 1) * PCS)
                for j, tile in ((1, PA), (0, PB), (2, PC)):
                    sp.dma_start(tile[q, 0:PL].bitcast(I32), dx[j:j + EP].rearrange("(i f) -> i f", i=PCS)
                                 ).then_inc(pieces_in, 16)
            sp.wait_ge(ends_out, 16)
            sp.dma_start(start, ends_d[0:N].rearrange("(p k) -> p k", p=NP)).then_inc(ends_in, 16)

        def index_runs(v):
            L = dve_line
            v.wait_ge(ends_in, 16)
            L.step(v, v.tensor_tensor(nonempty[:, :], end, start, ALU.is_gt))
            L.step(v, v.tensor_scalar(straddle[:, :], start, float(HALF * BLK), None, ALU.is_lt))
            L.step(v, v.tensor_scalar(tmp, end, float(HALF * BLK), None, ALU.is_gt))
            L.step(v, v.tensor_tensor(straddle[:, :], straddle[:, :], tmp, ALU.mult))
            L.step(v, v.tensor_scalar(tmp, end, -1.0 - ZROW, None, ALU.add))
            L.step(v, v.tensor_tensor(tmp, tmp, nonempty[:, :], ALU.mult))
            L.step(v, v.tensor_scalar(tmp, tmp, float(ZROW), None, ALU.add))
            L.step(v, v.tensor_copy(end_idx[:, :], tmp))
            L.step(v, v.tensor_scalar(tmp, nid, float(EP), None, ALU.add))
            L.step(v, v.tensor_tensor(start, start, tmp, ALU.subtract))
            L.step(v, v.tensor_tensor(start, start, nonempty[:, :], ALU.mult))
            L.step(v, v.tensor_tensor(start, start, tmp, ALU.add))
            L.step(v, v.tensor_copy(start_idx[:, :], start))

        def piece_flags(v):
            L = dve_line
            v.wait_ge(pieces_in, 16 * 12)
            L.step(v, v.tensor_tensor(same_prev[:, :], pa.bitcast(I32), pb.bitcast(I32), ALU.is_equal))
            v.sem_inc(onehot_at, 1)
            L.step(v, v.tensor_tensor(same_next[:, :], pa.bitcast(I32), pc.bitcast(I32), ALU.is_equal))
            L.step(v, v.tensor_scalar(last_of_run[:, :], same_next[:, :], -1.0, 1.0, ALU.mult, ALU.add))
            L.step(v, v.tensor_reduce(small[0:PQ, 6, 0:1], same_prev[:, :], AX.X, ALU.min))
            L.step(v, v.tensor_reduce(small[0:PQ, 6, 1:2], same_next[:, :], AX.X, ALU.min))
            L.step(v, v.tensor_scalar(small[0:PQ, 6, 3:4], small[0:PQ, 6, 0:1], 0.5, 2.0, ALU.subtract, ALU.mult))
            L.step(v, v.tensor_reduce(small[0:PQ, 7, 0:4], ident[0:PQ, 0:PQ].rearrange("q (t i) -> q t i", i=PCS),
                                      AX.X, ALU.add))
            L.step(v, v.tensor_tensor(small[0:PQ, 7, 4:8], small[0:PQ, 7, 0:4], iota8[0:PQ, 0:4], ALU.mult))
            L.step(v, v.tensor_reduce(small[0:PQ, 6, 2:3], small[0:PQ, 7, 4:8], AX.X, ALU.add))

        def load_kinds(sp):
            sp.wait_ge(onehot_at, 1)
            for t in range(4):
                q = slice(t * PCS, (t + 1) * PCS)
                sp.dma_start(PB[q, 0:PL].bitcast(I32), A["t4_nat"].rearrange("(i f) -> i f", i=PCS)).then_inc(kinds_in, 16)

        def count_kinds(v):
            v.wait_ge(kinds_in, 64)
            dve_line.step(v, v.tensor_scalar(pa, pb.bitcast(I32), small[0:PQ, 6, 2:3], None, ALU.is_equal))
            scan_pieces(v, pb, same_prev, small[0:PQ, 6, 0:1], pa, ALU.mult, ALU.add, 0.0, False)

        def spread_counts(v):
            L = dve_line
            L.step(v, v.tensor_tensor(pb, pb, last_of_run[:, :], ALU.mult))
            scan_pieces(v, pc, same_next, small[0:PQ, 6, 1:2], pb, ALU.mult, ALU.add, 0.0, True)
            L.step(v, v.tensor_tensor(pc, pc, pa, ALU.mult))
            v.sem_inc(kinds_up, 1)

        def norms(v):
            L = dve_line
            edge_major_out(v, PB[:, 0:HEADS], 1)
            L.step(v, v.tensor_scalar(PB[:, 0:HEADS], PB[:, 0:HEADS], 1.0, None, ALU.max))
            L.step(v, v.reciprocal(scal[:, :], PB[:, 0:HEADS]))

        first_side = {
            "sync": {1: load_types, 4: store_indices, 7: exchange_ends, 9: load_kinds},
            "scalar": {t: zero_fill(t) for t in range(1, TURNS)} | {
                14: lambda a: (zero_fill(14)(a), fold_act(a, PA[0:PCS, 0:PL], 1))},
            "gpsimd": {1: node_numbers, 4: gather_rows},
            "tensor": {10: lambda pe: carry_pe(pe, 1, False), 12: lambda pe: carry_pe(pe, 2, True),
                       14: lambda pe: fold_pe(pe, pc, PA[0:PCS, 0:PL], 1)},
            "vector": {2: count_rows, 6: find_ends, 8: lambda v: (index_runs(v), piece_flags(v)), 10: count_kinds,
                       12: spread_counts, 15: norms},
        }

        end_rows = [sem(f"end_rows{j}") for j in range(len(GROUPS))]
        turn_in = sem("turn_in")
        turn_pe = sem("turn_pe")
        turn_act = sem("turn_act")
        mm_pe = sem("mm_pe")
        mm_dve = sem("mm_dve")
        mm_act = sem("mm_act")
        group_up = sem("group_up")
        tab_out = sem("tab_out")
        sent = {}

        def at(s, n):
            return sent.get(s.num, 0) + n

        def add_sent(*pairs):
            for s, n in pairs:
                sent[s.num] = sent.get(s.num, 0) + n

        sqrt_req = sem("sqrt_req")
        sqrt_done = sem("sqrt_done")
        hT = PA[0:D, 0:N]
        zT = PB[0:D, 0:N]
        squares = PA[0:NP, 3200:3200 + 8 * D].rearrange("p (k f) -> p k f", f=D)
        tables4 = PC[0:NP, 0:R4 * NK * D].rearrange("p (t k f) -> p t k f", t=R4, f=D)
        rrows = PC[0:NP, 0:NK * RW].rearrange("p (k f) -> p k f", f=RW)
        over = lambda ap, j: ap.unsqueeze(1).to_broadcast([NP, GROUPS[j][1], D])

        def gather_ends(g):
            for j, (k0, n) in enumerate(GROUPS):
                for k in range(k0, k0 + n):
                    g.indirect_dma_start(gn[:, k, :], None, scan_d[:, :],
                                         bass.IndirectOffsetOnAxis(ap=end_idx[:, k:k + 1], axis=0)).then_inc(end_rows[j], 16)

        def ends_gathered(v, j):
            v.wait_ge(end_rows[j], at(end_rows[j], 16 * GROUPS[j][1]))

        def layer_norm(v, src, dst, j, n):
            L, sl = dve_line, slots(j)
            m, s = small[0:NP, 0, sl], small[0:NP, 1, sl]
            src, dst, sq = src[:, sl, :], dst[:, sl, :], squares[:, 0:GROUPS[j][1], :]
            L.step(v, v.tensor_reduce(m, src, AX.X, ALU.add))
            L.step(v, v.tensor_scalar(m, m, 1.0 / D, None, ALU.mult))
            L.step(v, v.tensor_tensor(dst, src, bcast(m, D), ALU.subtract))
            L.step(v, v.tensor_tensor(sq, dst, dst, ALU.mult))
            L.step(v, v.tensor_reduce(s, sq, AX.X, ALU.add))
            L.step(v, v.tensor_scalar(s, s, 1.0 / D, EPS, ALU.mult, ALU.add))
            v.sem_inc(sqrt_req, 1)
            v.wait_ge(sqrt_done, at(sqrt_done, n))
            L.step(v, v.reciprocal(s, small[0:NP, 2, sl]))
            L.step(v, v.tensor_tensor(dst, dst, bcast(s, D), ALU.mult))

        def norm_group(v, j, n=None):
            layer_norm(v, xn, hn, j, j + 1 if n is None else n)
            dve_line.step(v, v.tensor_scalar(hn[:, slots(j), :], hn[:, slots(j), :], 0.0, None, ALU.max))

        def sqrt_group(a, j, n=None):
            n = j + 1 if n is None else n
            a.wait_ge(sqrt_req, at(sqrt_req, n))
            a.activation(small[0:NP, 2, slots(j)], small[0:NP, 1, slots(j)], ACT.Sqrt).then_inc(sqrt_done, 1)

        def turn_group(pe, src, j, before=None, gate=True):
            first_q = quads(j)[0][0]
            if gate:
                pe.wait_ge(turn_in, at(turn_in, j + 1))
            for q, ks in quads(j):
                t = at(turn_pe, q if before is None else before + q - first_q)
                if t >= 2:
                    pe.wait_ge(turn_act, t - 1)
                for k in ks:
                    last = pe.transpose(ps[t % 2][0:D, (k % 4) * NP:(k % 4 + 1) * NP], src[:, k, :], ident[0:NP, 0:NP])
                last.then_inc(turn_pe, 1)

        def copy_turned(a, dst, j, before=None):
            first_q = quads(j)[0][0]
            for q, ks in quads(j):
                t = at(turn_pe, q if before is None else before + q - first_q)
                a.wait_ge(turn_pe, t + 1)
                a.copy(dst[:, 4 * q * NP:(4 * q + len(ks)) * NP], ps[t % 2][0:D, 0:len(ks) * NP]).then_inc(turn_act, 1)

        def table_products(pe, w, j):
            for k in range(GROUPS[j][0], sum(GROUPS[j])):
                m = at(mm_pe, k)
                if m >= 4:
                    pe.wait_ge(mm_act, m - 3)
                pe.matmul(ps[4 + m % 4][0:NP, 0:(R4 + 1) * D], hT[:, k * NP:(k + 1) * NP],
                          w[:, :, :].rearrange("d r e -> d (r e)"), start=True, stop=True).then_inc(mm_pe, 1)

        def copy_tables(a, j, halfway=None):
            for k in range(GROUPS[j][0], sum(GROUPS[j])):
                if halfway and k == GROUPS[j][0] + GROUPS[j][1] // 2:
                    halfway()
                m = at(mm_pe, k)
                a.wait_ge(mm_pe, m + 1)
                a.copy(rn[:, k, :], ps[4 + m % 4][0:NP, R4 * D:(R4 + 1) * D])
                a.copy(tables4[:, :, k, :], ps[4 + m % 4][0:NP, 0:R4 * D].rearrange("p (t f) -> p t f", t=R4)).then_inc(mm_act, 1)

        def store_tables4(sp):
            for j in range(len(GROUPS)):
                sp.wait_ge(mm_act, at(mm_act, sum(GROUPS[j])))
                sp.dma_start(tab4_d.rearrange("(t p k) f -> p t k f", t=R4, k=NK)[:, :, slots(j), :], tables4[:, :, slots(j), :]
                             ).then_inc(tab_out, 16)
            sp.wait_ge(tab_out, at(tab_out, 16 * len(GROUPS)))

        def add_to_roots(v, b_row):
            dve_line.step(v, v.tensor_tensor(rn[:, :, :], rn[:, :, :],
                                             rows[:, b_row, :].unsqueeze(1).to_broadcast([NP, NK, D]), ALU.add))

        def store_groups(sp, dst, src):
            for j in range(len(GROUPS)):
                sp.wait_ge(group_up, at(group_up, j + 1))
                sp.dma_start(node(dst)[:, slots(j), :], src[:, slots(j), :]).then_inc(tab_out, 16)
            sp.wait_ge(tab_out, at(tab_out, 16 * len(GROUPS)))

        all_ends = [(s, 16 * n) for s, (_, n) in zip(end_rows, GROUPS)]

        idx_in = [sem(f"idx_in{j}") for j in range(3)]
        flag_in = [sem(f"flag_in{j}") for j in range(FLAGS)]
        gathered = [sem(f"gathered{j}") for j in range(RING)]
        spread_in = [sem(f"spread_in{j}") for j in range(3)]
        stored = [sem(f"stored{j}") for j in range(4)]
        msg_out = [sem(f"msg_out{j}") for j in range(RING)]
        messages_in = [sem(f"messages_in{j}") for j in range(4)]
        turned_ = sem("turned_blocks")
        scaled = sem("scaled")
        scanned = sem("scanned")
        heldt = sem("spread_turned")
        held_up = sem("held_up")
        joined = sem("joined")
        relued = sem("relued")
        mixed = sem("mixed")
        backt = sem("turned_back")
        copied = sem("copied")
        progress = (turned_, scaled, scanned, heldt, held_up, joined, relued, mixed, backt, copied)
        sent.update({s.num: 0 for s in (*idx_in, *flag_in, *gathered, *spread_in, *stored, *msg_out, *messages_in, *progress)})

        def through(s, i, off):
            return i * BODY + (sent[s.num] + off)

        def landed(s, i, u, n, by=16):
            return i * (BODY // n * by) + (sent[s.num] + (u // n + 1) * by)

        def wait_for(eng, s, value):
            if not isinstance(value, int) or value > sent[s.num]:
                eng.wait_ge(s, value)
                return True
            return False

        def gated(eng, s, value):
            if wait_for(eng, s, value):
                eng.sem_inc(armed, 1)

        def all_blocks(eng, body, side=None):
            side = side or {}
            for u in range(BODY):
                body(0, u, BODY)
            cuts = sorted({1, TURNS, *side})
            for lo, hi in zip(cuts, cuts[1:]):
                if lo in side:
                    side[lo](eng)
                with eng.Fori(lo, hi) as i:
                    for u in range(BODY):
                        body(i, u, BODY)
            for u in range(TAIL):
                body(TURNS, u, TAIL - 1 - u)

        def first(i, u):
            return isinstance(i, int) and i * BODY + u == 0

        def first_indices(sp, idx_dram):
            for g in range(BODY // GRP):
                sp.dma_start(idx[:, g, :], idx_dram[g]).then_inc(idx_in[g], 16)

        def sweep(kind, table, idx_dram, scale=False, side={}):
            spread = kind in ("score", "max")
            W = RW if kind == "score" else D
            width = table.shape[1]
            bank_read = joined if spread else scanned
            flags_read = held_up if kind == "score" else scanned
            n_flags = 32 if kind == "max" else 16
            with nc.Block() as block:
                @block.sync
                def _(sp):
                    def body(i, u, left):
                        b = i * BODY + u
                        if u % GRP == 0 and not first(i, 0):
                            s = gathered[(u - 2 * GRP - 1) % RING]
                            gated(sp, s, landed(s, i, u - 2 * GRP - 1, RING, 16 * CPB))
                            sp.dma_start(idx[:, u // GRP, :], idx_dram[i * (BODY // GRP) + u // GRP]
                                         ).then_inc(idx_in[u // GRP], 16)
                        gated(sp, flags_read, through(flags_read, i, u + 1 - FLAGS))
                        sp.dma_start(hold[0:W, u % FLAGS, :], seg_bcast(hold_d, b, W)).then_inc(flag_in[u % FLAGS], 16)
                        if kind == "max":
                            sp.dma_start(cap[:, u % FLAGS, :], seg_bcast(cap_d, b, D)).then_inc(flag_in[u % FLAGS], 16)
                        if spread:
                            gated(sp, heldt, through(heldt, i, u - 2))
                            sp.dma_start(EX[:, u % 3, :, :], blk(spread_d[0:EP, :])[b]).then_inc(spread_in[u % 3], 16)
                    all_blocks(sp, body, side.get("sync"))
                    for j, s in enumerate(stored):
                        sp.wait_ge(s, sent[s.num] + 16 * len(range(j, NBP, 4)))
                    if kind == "score":
                        for j, s in enumerate(msg_out):
                            sp.wait_ge(s, sent[s.num] + 16 * len(range(j, NBP, RING)))

                @block.gpsimd
                def _(g):
                    def body(i, u, left):
                        if u % GRP == 0:
                            gated(g, idx_in[u // GRP], landed(idx_in[u // GRP], i, u, RING))
                        gated(g, turned_, through(turned_, i, u + 1 - RING))
                        if kind == "score":
                            gated(g, msg_out[u], landed(msg_out[u], i, u - RING, RING))
                        for c in range(CPB):
                            q = (u % GRP) * CPB + c
                            g.indirect_dma_start(G[:, u, c, 0:width], None, table,
                                                 bass.IndirectOffsetOnAxis(ap=idx[:, u // GRP, q:q + 1], axis=0)
                                                 ).then_inc(gathered[u], 16)
                    all_blocks(g, body, side.get("gpsimd"))

                @block.tensor
                def _(pe):
                    def turn_spread(i, u):
                        s = spread_in[u % 3]
                        wait_for(pe, s, landed(s, i, u, 3))
                        gated(pe, held_up, through(held_up, i, u - 1))
                        for c in range(CPB):
                            last = pe.transpose(ps[2 + u % 2][0:W, c:BLK:CPB], EX[:, u % 3, c, 0:W], ident[:, :])
                        last.then_inc(heldt, 1)

                    def turn_gathered(i, u):
                        s = gathered[u % RING]
                        if scale or kind == "score":
                            wait_for(pe, scaled, through(scaled, i, u + 1))
                        wait_for(pe, bank_read, through(bank_read, i, u - 1))
                        gated(pe, s, landed(s, i, u, RING, 16 * CPB))
                        src = GS[:, u % 2, :, 0:D] if scale else G[:, u % RING]
                        cc = slice(D, D + RW) if kind == "score" else slice(0, D)
                        for c in range(CPB):
                            last = pe.transpose(ps[u % 2][0:W, c:BLK:CPB], src[:, c, cc], ident[:, :])
                        last.then_inc(turned_, 1)

                    def turn_back(i, u):
                        wait_for(pe, scanned, through(scanned, i, u + 1))
                        gated(pe, copied, through(copied, i, u - 1))
                        for c in range(CPB):
                            last = pe.transpose(ps[6 + u % 2][:, c * D:(c + 1) * D], run[0:D, u % 2, c:BLK:CPB],
                                                ident[0:D, 0:D])
                        last.then_inc(backt, 1)

                    def body(i, u, left):
                        if kind == "score":
                            if left:
                                turn_spread(i, u + 1)
                            wait_for(pe, joined, through(joined, i, u + 1))
                            gated(pe, copied, through(copied, i, u - 1))
                            pe.matmul(ps[4 + u % 2][0:4, :], w4[:, :], prod[:, u % 2, :], start=True, stop=True
                                      ).then_inc(mixed, 1)
                            if left:
                                turn_gathered(i, u + 1)
                        elif kind == "max":
                            wait_for(pe, relued, through(relued, i, u + 1))
                            gated(pe, scanned, through(scanned, i, u - 1))
                            pe.matmul(ps[4 + u % 2][0:D, :], w3bt[:, :], act_sb[:, u % 2, :], start=True, stop=True
                                      ).then_inc(mixed, 1)
                            if left > 1:
                                turn_spread(i, u + 2)
                                turn_gathered(i, u + 2)
                            if not first(i, u):
                                turn_back(i, u - 1)
                            if not left:
                                turn_back(i, u)
                        else:
                            if left:
                                turn_gathered(i, u + 1)
                            turn_back(i, u)
                    for u in range(2 if kind == "max" else 1):
                        if spread:
                            turn_spread(0, u)
                        turn_gathered(0, u)
                    all_blocks(pe, body, side.get("tensor"))

                @block.vector
                def _(v):
                    def spread_over(i, u):
                        s = flag_in[u % FLAGS]
                        wait_for(v, s, landed(s, i, u, FLAGS, n_flags))
                        wait_for(v, heldt, through(heldt, i, u + 1))
                        wait_for(v, held_up, through(held_up, i, u))
                        wait_for(v, joined, through(joined, i, u - 1))
                        v.tensor_tensor_scan(held[0:W, u % 2, :], hold[0:W, u % FLAGS, :], ps[2 + u % 2][0:W, :],
                                             held[0:W, (u + 1) % 2, BLK - 1:BLK], ALU.mult, ALU.add).then_inc(held_up, 1)

                    def one_hot(i, u):
                        wait_for(v, turned_, through(turned_, i, u + 1 - RING))
                        v.tensor_tensor(G[:, u % RING, :, 2 * D:2 * D + R8], bcast(per_edge(i, u).bitcast(I32), R8),
                                        iota8[:, :].unsqueeze(1).to_broadcast([128, CPB, R8]),
                                        ALU.is_equal).then_inc(scaled, 1)

                    def scale_rows(i, u):
                        s = gathered[u % RING]
                        wait_for(v, s, landed(s, i, u, RING, 16 * CPB))
                        wait_for(v, turned_, through(turned_, i, u - 1))
                        v.tensor_tensor(GS[:, u % 2, :, 0:D], G[:, u % RING, :, 0:D], bcast(per_edge(i, u), D),
                                        ALU.mult).then_inc(scaled, 1)

                    def join(i, u, op):
                        wait_for(v, turned_, through(turned_, i, u + 1))
                        wait_for(v, held_up, through(held_up, i, u + 1))
                        used = mixed if kind == "score" else relued
                        wait_for(v, used, through(used, i, u - 1))
                        v.tensor_tensor(prod[0:W, u % 2, :], ps[u % 2][0:W, :], held[0:W, u % 2, :], op).then_inc(joined, 1)

                    def reduce_runs(i, u):
                        if kind == "max":
                            wait_for(v, mixed, through(mixed, i, u + 1))
                            flag, val, ops = cap[:, u % FLAGS, :], ps[4 + u % 2][0:D, :], (ALU.min, ALU.max)
                        else:
                            wait_for(v, turned_, through(turned_, i, u + 1))
                            s = flag_in[u % FLAGS]
                            wait_for(v, s, landed(s, i, u, FLAGS))
                            flag, val, ops = hold[0:D, u % FLAGS, :], ps[u % 2][0:D, :], (ALU.mult, ALU.add)
                        wait_for(v, scanned, through(scanned, i, u))
                        wait_for(v, backt, through(backt, i, u - 1))
                        v.tensor_tensor_scan(run[0:D, u % 2, :], flag, val, run[0:D, (u + 1) % 2, BLK - 1:BLK],
                                             *ops).then_inc(scanned, 1)

                    def body(i, u, left):
                        if kind == "score":
                            join(i, u, ALU.mult)
                            if left:
                                one_hot(i, u + 1)
                                spread_over(i, u + 1)
                        elif kind == "max":
                            if not first(i, u):
                                reduce_runs(i, u - 1)
                            if left:
                                spread_over(i, u + 1)
                                join(i, u + 1, ALU.add)
                            else:
                                reduce_runs(i, u)
                        else:
                            if scale and left:
                                scale_rows(i, u + 1)
                            reduce_runs(i, u)
                    if kind == "score":
                        one_hot(0, 0)
                    if spread:
                        spread_over(0, 0)
                    if kind == "max":
                        join(0, 0, ALU.add)
                    if scale:
                        scale_rows(0, 0)
                    all_blocks(v, body, side.get("vector"))

                @block.scalar
                def _(a):
                    def relu(i, u):
                        wait_for(a, joined, through(joined, i, u + 1))
                        wait_for(a, mixed, through(mixed, i, u - 1))
                        a.activation(act_sb[:, u % 2, :], prod[0:D, u % 2, :], ACT.Relu).then_inc(relued, 1)

                    def store_runs(i, u):
                        wait_for(a, backt, through(backt, i, u + 1))
                        wait_for(a, stored[u % 4], landed(stored[u % 4], i, u - 4, 4))
                        a.activation(O[:, u % 4, 0, :, :], ps[6 + u % 2][:, 0:CPB * D].rearrange("p (c f) -> p c f", c=CPB),
                                     ACT.Copy).then_inc(copied, 1)
                        gated(a, copied, through(copied, i, u + 1))
                        a.dma_start(blk(scan_d[0:EP, :])[i * BODY + u], O[:, u % 4, 0, :, :]).then_inc(stored[u % 4], 16)

                    def body(i, u, left):
                        b = i * BODY + u
                        if kind == "score":
                            gated(a, gathered[u], landed(gathered[u], i, u, RING, 16 * CPB))
                            a.dma_start(blk(msg_d)[b], G[:, u, :, 0:D]).then_inc(msg_out[u], 16)
                            wait_for(a, mixed, through(mixed, i, u + 1))
                            wait_for(a, stored[u % 4], landed(stored[u % 4], i, u - 4, 4))
                            a.activation(sc_sb[:, u % 4, :], ps[4 + u % 2][0:4, :], ACT.Copy, scale=D ** -0.5
                                         ).then_inc(copied, 1)
                            gated(a, copied, through(copied, i, u + 1))
                            a.dma_start(score_d.rearrange("r (b e) -> b r e", e=BLK)[b], sc_sb[:, u % 4, :]
                                        ).then_inc(stored[u % 4], 16)
                        elif kind == "max":
                            if left:
                                relu(i, u + 1)
                            if not first(i, u):
                                store_runs(i, u - 1)
                            if not left:
                                store_runs(i, u)
                        else:
                            store_runs(i, u)
                    if kind == "max":
                        relu(0, 0)
                    all_blocks(a, body, side.get("scalar"))

            for s, on in ((turned_, True), (scaled, scale or kind == "score"), (scanned, kind != "score"),
                          (heldt, spread), (held_up, spread), (joined, spread), (relued, kind == "max"),
                          (mixed, spread), (backt, kind != "score"), (copied, True)):
                sent[s.num] += NBP * on
            for j, s in enumerate(idx_in):
                sent[s.num] += 16 * len(range(j, -(-NBP // GRP), 3))
            for ring, by in ((flag_in, n_flags), (spread_in, 16 * spread), (gathered, 16 * CPB), (stored, 16),
                              (msg_out, 16 * (kind == "score"))):
                for j, s in enumerate(ring):
                    sent[s.num] += by * len(range(j, NBP, len(ring)))

        def per_edge(i, u):
            return scal[:, bass.ds(i * (BODY * CPB) + u * CPB, CPB)]

        def sweep_messages():
            hold2 = hold_d[0:NBP * BLK].rearrange("(h b e) -> b h e", h=2, e=BLK)
            msg2, scan2 = (d[0:NBP * BLK, :].rearrange("(h b p c) f -> b p h c f", h=2, p=128, c=CPB) for d in (msg_d, scan_d))
            with nc.Block() as block:
                @block.sync
                def _(sp):
                    def body(i, u, left):
                        b = i * BODY + u
                        gated(sp, scanned, through(scanned, i, u + 1 - FLAGS))
                        sp.dma_start(hold[:, u % FLAGS, :], hold2[b].unsqueeze(1).to_broadcast([2, D, BLK])
                                     ).then_inc(flag_in[u % FLAGS], 16)
                        gated(sp, scaled, through(scaled, i, u - 3))
                        sp.dma_start(G2[:, u % 4], msg2[b]).then_inc(messages_in[u % 4], 16)
                    pair_blocks(sp, body)
                    for j, s in enumerate(stored):
                        sp.wait_ge(s, sent[s.num] + 16 * len(range(j, HALF, 4)))

                @block.tensor
                def _(pe):
                    def turn(i, u):
                        wait_for(pe, scaled, through(scaled, i, u + 1))
                        gated(pe, scanned, through(scanned, i, u - 1))
                        for c in range(CPB):
                            last = pe.transpose(ps[u % 2][:, c:BLK:CPB], GS2[:, u % 2, c, :, :].rearrange("p h f -> p (h f)"),
                                                ident[:, :])
                        last.then_inc(turned_, 1)

                    def body(i, u, left):
                        if left:
                            turn(i, u + 1)
                        wait_for(pe, scanned, through(scanned, i, u + 1))
                        gated(pe, copied, through(copied, i, u - 1))
                        for c in range(CPB):
                            last = pe.transpose(ps[6 + u % 2][:, c * 128:(c + 1) * 128], run[:, u % 2, c:BLK:CPB], ident[:, :])
                        last.then_inc(backt, 1)
                    turn(0, 0)
                    pair_blocks(pe, body)

                @block.vector
                def _(v):
                    L = dve_line
                    L.step(v, v.memset(run[:, :, :], 0.0))

                    def scale_rows(i, u):
                        s = messages_in[u % 4]
                        wait_for(v, s, landed(s, i, u, 4))
                        wait_for(v, turned_, through(turned_, i, u - 1))
                        for h in range(2):
                            ins = v.tensor_tensor(GS2[:, u % 2, :, h, :], G2[:, u % 4, h, :, :],
                                                  bcast(scal[:, bass.ds(i * (BODY * CPB) + (u + h * HALF) * CPB, CPB)], D),
                                                  ALU.mult)
                        ins.then_inc(scaled, 1)

                    def body(i, u, left):
                        if left:
                            scale_rows(i, u + 1)
                        wait_for(v, turned_, through(turned_, i, u + 1))
                        s = flag_in[u % FLAGS]
                        wait_for(v, s, landed(s, i, u, FLAGS))
                        wait_for(v, scanned, through(scanned, i, u))
                        wait_for(v, backt, through(backt, i, u - 1))
                        v.tensor_tensor_scan(run[:, u % 2, :], hold[:, u % FLAGS, :], ps[u % 2][:, :],
                                             run[:, (u + 1) % 2, BLK - 1:BLK], ALU.mult, ALU.add).then_inc(scanned, 1)
                    scale_rows(0, 0)
                    pair_blocks(v, body)

                @block.scalar
                def _(a):
                    def body(i, u, left):
                        b = i * BODY + u
                        wait_for(a, backt, through(backt, i, u + 1))
                        wait_for(a, stored[u % 4], landed(stored[u % 4], i, u - 4, 4))
                        a.activation(O[:, u % 4], ps[6 + u % 2][:, :].rearrange("p (c h f) -> p h c f", h=2, f=D), ACT.Copy
                                     ).then_inc(copied, 1)
                        gated(a, copied, through(copied, i, u + 1))
                        a.dma_start(scan2[b], O[:, u % 4]).then_inc(stored[u % 4], 16)
                    pair_blocks(a, body)

            for s in (turned_, scaled, scanned, backt, copied):
                sent[s.num] += HALF
            for ring in (flag_in, messages_in, stored):
                for j, s in enumerate(ring):
                    sent[s.num] += 16 * len(range(j, HALF, len(ring)))

        def pair_blocks(eng, body):
            for u in range(BODY):
                body(0, u, BODY)
            with eng.Fori(1, HALF // BODY) as i:
                for u in range(BODY):
                    body(i, u, BODY)
            for u in range(HALF % BODY):
                body(HALF // BODY, u, HALF % BODY - 1 - u)

        def blk(d):
            return d.rearrange("(b p c) f -> b p c f", p=128, c=CPB)

        def seg_bcast(d, b, parts):
            return d.rearrange("(b e) -> b e", e=BLK)[b].unsqueeze(0).to_broadcast([parts, BLK])

        ALL = range(len(GROUPS))

        x_in = sem("x_in"); edge_in = sem("edge_in"); loaded = sem("loaded"); numbers = sem("numbers")
        flags_up = sem("flags_up"); flags_out = sem("flags_out")
        n_loads = [0]
        cur = PA[:, 0:HEADS].bitcast(I32)
        prv = PA[:, HEADS:2 * HEADS].bitcast(I32)
        hold_b = PB[:, 0:HEADS // 2].bitcast(BF16)
        cap_b = PB[:, HEADS // 2:HEADS].bitcast(BF16)
        counting = PC[:, 0:128].bitcast(I32)
        part_no = PC[:, 128:129].bitcast(I32)
        with nc.Block() as block:
            @block.sync
            def _(sp):
                def ld(dst, src):
                    sp.dma_start(dst, src).then_inc(loaded, 16)
                    n_loads[0] += 16
                sp.dma_start(xn[:, :, :], node(A["x"])).then_inc(x_in, 16)
                first_indices(sp, A["src_it"])
                dx = A["dst_ext"]
                sp.dma_start(cur, dx[1:EP + 1].rearrange("(p f) -> p f", p=128)).then_inc(edge_in, 16)
                sp.dma_start(prv, dx[0:EP].rearrange("(p f) -> p f", p=128)).then_inc(edge_in, 16)
                ld(P_(w0a), A["L0_gnn_W1"]); ld(P_(w0b), A["L0_gnn_W2"])
                for w, nm, rt in ((w1a, "L1_gnn_W1", "L1_gnn_root1"), (w1b, "L1_gnn_W2", "L1_gnn_root2")):
                    ld(w[:, 0:R4, :], A[nm].rearrange("r d e -> d r e"))
                    ld(w[:, R4, :], A[rt])
                ld(w2r[:, :, :], A["L2_gnn_W_r"].rearrange("r d e -> d r e"))
                ld(P_(wq), A["L2_gnn_Wq_w"])
                ld(wk[:, :, :], A["L2_gnn_Wk_w"].rearrange("(a d) e -> d a e", a=3))
                ld(P_(w3), A["L3_gnn_W1"]); ld(P_(w3b), A["L3_gnn_W2"])
                ld(P_(rid), A["rule_ids"])
                for j, nm in enumerate(("L0_gnn_b1", "L0_gnn_gamma1", "L0_gnn_beta1", "L2_gnn_Wq_bias", "L2_gnn_Wk_bias")):
                    ld(cols[:, j:j + 1], A[nm])
                for j, nm in enumerate(("L0_gnn_b2", "L1_gnn_b1", "L1_gnn_b2", "L2_gnn_bias", "L2_gnn_ln_g", "L2_gnn_ln_b", "L3_gnn_b1", "L3_gnn_b2")):
                    ld(rows[:, j, :], row_bcast(A[nm], NP, D))
                sp.wait_ge(flags_up, 1)
                sp.dma_start(hold_d.rearrange("(p f) -> p f", p=128), hold_b).then_inc(flags_out, 16)
                sp.dma_start(cap_d.rearrange("(p f) -> p f", p=128), cap_b).then_inc(flags_out, 16)
                store_groups(sp, tab_d, hn)
                sp.wait_ge(flags_out, 32)
                sp.wait_ge(loaded, n_loads[0])

            @block.gpsimd
            def _(g):
                pool_line.step(g, g.iota(counting, [[1, 128]], base=0, channel_multiplier=0))
                pool_line.step(g, g.iota(part_no, [[0, 1]], base=0, channel_multiplier=1))
                g.sem_inc(numbers, 1)

            @block.scalar
            def _(a):
                for j in ALL:
                    sqrt_group(a, j)

            @block.vector
            def _(v):
                L = dve_line
                v.wait_ge(edge_in, 32)
                same = PB[:, HEADS:2 * HEADS]
                L.step(v, v.tensor_tensor(same, cur, prv, ALU.is_equal))
                L.step(v, v.tensor_copy(hold_b, same))
                L.step(v, v.tensor_scalar(same, same, 0.5, 2.0, ALU.subtract, ALU.mult))
                L.step(v, v.tensor_scalar(cap_b, same, BIG, None, ALU.mult))
                v.sem_inc(flags_up, 1)
                v.wait_ge(x_in, 16)
                for j in ALL:
                    norm_group(v, j)
                    v.sem_inc(group_up, 1)
                v.wait_ge(numbers, 1)
                L.step(v, v.tensor_copy(PB[:, 2048:2177], PC[:, 0:129].bitcast(I32)))
                L.step(v, v.tensor_scalar(ident[:, :], PB[:, 2048:2176], PB[:, 2176:2177], None, ALU.is_equal))
                L.step(v, v.tensor_copy(P_(iota8), PB[:, 2048:2048 + R8]))
                L.step(v, v.memset(P_(ones), 1.0))
                L.step(v, v.tensor_copy(fold[:, :], ident[0:PQ, 0:PCS]))
                for t in range(1, 4):
                    L.step(v, v.tensor_tensor(fold[:, :], fold[:, :], ident[0:PQ, t * PCS:(t + 1) * PCS], ALU.add))
                L.step(v, v.memset(w4[0:D, :], 1.0))
                L.step(v, v.tensor_copy(w4[D:RW, :], ident[D:RW, D + R8:RW]))
                L.step(v, v.tensor_reduce(small[D:RW, 7, 0:1], ident[D:RW, D:D + R8], AX.X, ALU.add))
                L.step(v, v.tensor_tensor(w4[D:RW, :], w4[D:RW, :], small[D:RW, 7, 0:1].to_broadcast([RW - D, 4]), ALU.add))
                L.step(v, v.memset(G[:, :, :, 2 * D + R8:], 1.0))
                L.step(v, v.memset(run[:, :, :], 0.0))
                L.step(v, v.memset(held[:, :, :], 0.0))
                L.step(v, v.memset(zeros, 0.0))
        add_sent((sqrt_req, len(GROUPS)), (sqrt_done, len(GROUPS)), (group_up, len(GROUPS)), (tab_out, 16 * len(GROUPS)))

        sweep("sum", tab_d, A["src_it"], side=first_side)

        zup = sem("zup"); zcp = sem("zcp"); bn_req = sem("bn_req"); bn_act = sem("bn_act")
        z_relu = sem("z_relu"); z_back = sem("z_back")
        BACK = 8
        backs = [range(k, min(k + BACK, NK)) for k in range(0, NK, BACK)]
        with nc.Block() as block:
            @block.gpsimd
            def _(g):
                gather_ends(g)

            @block.vector
            def _(v):
                L = dve_line
                for j in ALL:
                    ends_gathered(v, j)
                    L.step(v, v.tensor_tensor(gn[:, slots(j), :], gn[:, slots(j), :], hn[:, slots(j), :], ALU.add))
                    v.sem_inc(turn_in, 1)
                    for q, ks in quads(j):
                        v.wait_ge(zcp, q + 1)
                        L.step(v, v.bn_stats(bn[:, q, :], zT[:, 4 * q * NP:(4 * q + len(ks)) * NP]))
                L.step(v, v.bn_aggr(bnm[:, :], bn[:, :, :]))
                L.step(v, v.tensor_scalar(bnc[:, 0:1], bnm[:, 1:2], EPS, None, ALU.add))
                v.sem_inc(bn_req, 1)
                v.wait_ge(bn_act, 1)
                L.step(v, v.reciprocal(bnc[:, 2:3], bnc[:, 1:2]))
                L.step(v, v.tensor_tensor(bnc[:, 2:3], bnc[:, 2:3], cols[:, 1:2], ALU.mult))
                L.step(v, v.tensor_tensor(bnc[:, 3:4], bnm[:, 0:1], bnc[:, 2:3], ALU.mult))
                L.step(v, v.tensor_tensor(bnc[:, 3:4], cols[:, 2:3], bnc[:, 3:4], ALU.subtract))
                v.sem_inc(bn_req, 1)
                for c, ks in enumerate(backs):
                    v.wait_ge(z_back, c + 1)
                    L.step(v, v.tensor_copy(hn[:, ks[0]:ks[-1] + 1, :],
                                            ps[4 + c][0:NP, 0:len(ks) * D].rearrange("p (k f) -> p k f", f=D)))
                    v.sem_inc(group_up, 1)

            @block.tensor
            def _(pe):
                for j in ALL:
                    turn_group(pe, gn, j)
                    for q, ks in quads(j):
                        pe.wait_ge(turn_act, at(turn_act, q + 1))
                        if q >= 2:
                            pe.wait_ge(zcp, q - 1)
                        pe.matmul(ps[2 + q % 2][0:D, 0:len(ks) * NP], w0a[:, :], hT[:, 4 * q * NP:(4 * q + len(ks)) * NP],
                                  start=True, stop=True).then_inc(zup, 1)
                for c, ks in enumerate(backs):
                    pe.wait_ge(z_relu, c + 1)
                    for k in ks:
                        last = pe.transpose(ps[4 + c][0:NP, (k % BACK) * D:(k % BACK + 1) * D], zT[:, k * NP:(k + 1) * NP],
                                            ident[0:D, 0:D])
                    last.then_inc(z_back, 1)

            @block.scalar
            def _(a):
                for j in ALL:
                    copy_turned(a, hT, j)
                    for q, ks in quads(j):
                        w = len(ks) * NP
                        a.wait_ge(zup, q + 1)
                        a.activation(zT[:, 4 * q * NP:4 * q * NP + w], ps[2 + q % 2][0:D, 0:w], ACT.Identity,
                                     bias=cols[:, 0:1]).then_inc(zcp, 1)
                a.wait_ge(bn_req, 1)
                a.activation(bnc[:, 1:2], bnc[:, 0:1], ACT.Sqrt).then_inc(bn_act, 1)
                a.wait_ge(bn_req, 2)
                for ks in backs:
                    z = zT[:, ks[0] * NP:(ks[-1] + 1) * NP]
                    a.activation(z, z, ACT.Relu, bias=bnc[:, 3:4], scale=bnc[:, 2:3]).then_inc(z_relu, 1)

            @block.sync
            def _(sp):
                first_indices(sp, A["src_it"])
                sp.wait_ge(zfill, n_zfill)
                for c, ks in enumerate(backs):
                    sp.wait_ge(group_up, at(group_up, c + 1))
                    sp.dma_start(node(tab_d)[:, ks[0]:ks[-1] + 1, :], hn[:, ks[0]:ks[-1] + 1, :]).then_inc(tab_out, 16)
                sp.wait_ge(tab_out, at(tab_out, 16 * len(backs)))
        add_sent(*all_ends, (turn_in, len(GROUPS)), (turn_pe, QUADS), (turn_act, QUADS), (group_up, len(backs)),
                 (tab_out, 16 * len(backs)))

        emb_in = sem("emb_in"); w_rel = sem("w_rel"); w_tr = sem("w_tr"); w_cp = sem("w_cp")

        def gather_rules(g):
            g.indirect_dma_start(emb[:, :], None, A["L2_gnn_rule_emb"],
                                 bass.IndirectOffsetOnAxis(ap=rid[:, 0:1], axis=0)).then_inc(emb_in, 16)

        def relation_means(v):
            L = dve_line
            L.step(v, v.tensor_reduce(relT[:, :], w2r[:, :, :], AX.X, ALU.add))
            L.step(v, v.tensor_scalar(relT[:, :], relT[:, :], 1.0 / D, None, ALU.mult))
            v.sem_inc(w_rel, 1)

        def turn_weights(pe):
            pe.wait_ge(emb_in, 16)
            pe.transpose(ps[4][0:D, 0:D], wk[:, 0, :], ident[0:D, 0:D])
            pe.transpose(ps[4][0:D, D:D + 4], emb[:, :], ident[0:4, 0:4])
            pe.transpose(ps[4][0:D, 2 * D:3 * D], w3[:, D:2 * D], ident[0:D, 0:D])
            pe.transpose(ps[4][0:D, 3 * D:4 * D], w3[:, 0:D], ident[0:D, 0:D])
            pe.transpose(ps[4][0:D, 4 * D:5 * D], w3b[:, :], ident[0:D, 0:D]).then_inc(w_tr, 1)

        def copy_weights(v):
            L = dve_line
            v.wait_ge(w_tr, 1)
            L.step(v, v.tensor_copy(m2[:, 0:D], ps[4][0:D, 0:D]))
            L.step(v, v.tensor_copy(embT[:, :], ps[4][0:D, D:D + 4]))
            L.step(v, v.tensor_copy(w3t[:, 0, :], ps[4][0:D, 2 * D:3 * D]))
            L.step(v, v.tensor_tensor(w3t[:, 1, :], ps[4][0:D, 3 * D:4 * D], w3t[:, 0, :], ALU.subtract))
            L.step(v, v.tensor_copy(w3bt[:, :], ps[4][0:D, 4 * D:5 * D]))
            v.sem_inc(w_cp, 1)

        def multiply_weights(pe):
            pe.wait_ge(w_rel, 1)
            pe.wait_ge(w_cp, 1)
            pe.matmul(ps[5][0:D, 0:R8], wk[:, 1, :], relT[:, :], start=True, stop=True)
            pe.matmul(ps[5][0:D, R8:R8 + 4], wk[:, 2, :], embT[:, :], start=True, stop=True).then_inc(w_tr, 1)

        def copy_products(v):
            L = dve_line
            v.wait_ge(w_tr, 2)
            L.step(v, v.tensor_scalar(m2[:, D:D + R8], ps[5][0:D, 0:R8], cols[:, 4:5], None, ALU.add))
            L.step(v, v.tensor_copy(m2[:, D + R8:RW], ps[5][0:D, R8:R8 + 4]))

        sweep("sum", tab_d, A["src_it"], side={
            "gpsimd": {1: gather_rules}, "tensor": {2: turn_weights, 4: multiply_weights},
            "vector": {1: relation_means, 3: copy_weights, 5: copy_products}})

        agg_up = sem("agg_up"); w2_pe = sem("w2_pe"); w2_dve = sem("w2_dve")
        aggT = zT
        nq = [len(quads(j)) for j in ALL]
        before_w2 = [sum(nq[:j]) + sum(nq[:max(j - 1, 0)]) for j in ALL]
        before_tab = [sum(nq[:j + 2]) + sum(nq[:j]) for j in ALL]
        with nc.Block() as block:
            @block.gpsimd
            def _(g):
                gather_ends(g)

            @block.vector
            def _(v):
                L = dve_line
                L.step(v, v.tensor_tensor(xn[:, :, :], xn[:, :, :], rows[:, 0, :].unsqueeze(1).to_broadcast([NP, NK, D]), ALU.add))

                def aggregate(j):
                    sl = slots(j)
                    ends_gathered(v, j)
                    L.step(v, v.tensor_tensor(gn[:, sl, :], gn[:, sl, :], hn[:, sl, :], ALU.add))
                    v.sem_inc(agg_up, 1)
                aggregate(0)
                for j in ALL:
                    sl, n = slots(j), GROUPS[j][1]
                    if j + 1 in ALL:
                        aggregate(j + 1)
                    v.wait_ge(w2_pe, j + 1)
                    v.tensor_tensor(xn[:, sl, :], xn[:, sl, :],
                                    ps[2 + j % 2][0:NP, 0:n * D].rearrange("p (k f) -> p k f", f=D), ALU.add).then_inc(w2_dve, 1)
                    v.wait_ge(w2_dve, j + 1)
                    norm_group(v, j)
                    v.sem_inc(turn_in, 1)

            @block.tensor
            def _(pe):
                def products_w2(j):
                    pe.wait_ge(agg_up, j + 1)
                    turn_group(pe, gn, j, before_w2[j], gate=False)
                    pe.wait_ge(turn_act, at(turn_act, before_w2[j] + nq[j]))
                    if j >= 2:
                        pe.wait_ge(w2_dve, j - 1)
                    for k in range(GROUPS[j][0], sum(GROUPS[j])):
                        i = k - GROUPS[j][0]
                        last = pe.matmul(ps[2 + j % 2][0:NP, i * D:(i + 1) * D], aggT[:, k * NP:(k + 1) * NP],
                                         w0b[:, :], start=True, stop=True)
                    last.then_inc(w2_pe, 1)
                products_w2(0)
                for j in ALL:
                    if j + 1 in ALL:
                        products_w2(j + 1)
                    if j:
                        pe.wait_ge(turn_act, at(turn_act, before_tab[j - 1] + nq[j - 1]))
                        table_products(pe, w1a, j - 1)
                    turn_group(pe, hn, j, before_tab[j])
                pe.wait_ge(turn_act, at(turn_act, before_tab[-1] + nq[-1]))
                table_products(pe, w1a, ALL[-1])

            @block.scalar
            def _(a):
                copy_turned(a, aggT, 0, before_w2[0])
                for j in ALL:
                    if j + 1 in ALL:
                        copy_turned(a, aggT, j + 1, before_w2[j + 1])
                    if j:
                        copy_tables(a, j - 1, lambda: sqrt_group(a, j))
                    else:
                        sqrt_group(a, j)
                    copy_turned(a, hT, j, before_tab[j])
                copy_tables(a, ALL[-1])

            @block.sync
            def _(sp):
                first_indices(sp, idx4_d)
                store_tables4(sp)
        add_sent(*all_ends, (turn_in, len(GROUPS)), (turn_pe, 2 * QUADS), (turn_act, 2 * QUADS),
                 (mm_pe, NK), (mm_act, NK), (tab_out, 16 * len(GROUPS)), (sqrt_req, len(GROUPS)), (sqrt_done, len(GROUPS)))

        sweep("sum", tab4_d, idx4_d, scale=True)

        with nc.Block() as block:
            @block.gpsimd
            def _(g):
                gather_ends(g)

            @block.vector
            def _(v):
                L = dve_line
                add_to_roots(v, 1)
                for j in ALL:
                    sl = slots(j)
                    ends_gathered(v, j)
                    L.step(v, v.tensor_tensor(gn[:, sl, :], gn[:, sl, :], rn[:, sl, :], ALU.add))
                    L.step(v, v.tensor_scalar(hn[:, sl, :], gn[:, sl, :], 0.0, None, ALU.max))
                    v.sem_inc(turn_in, 1)

            @block.tensor
            def _(pe):
                for j in ALL:
                    turn_group(pe, hn, j)
                    pe.wait_ge(turn_act, at(turn_act, quads(j)[-1][0] + 1))
                    table_products(pe, w1b, j)

            @block.scalar
            def _(a):
                for j in ALL:
                    copy_turned(a, hT, j)
                    copy_tables(a, j)

            @block.sync
            def _(sp):
                first_indices(sp, idx4_d)
                store_tables4(sp)
        add_sent(*all_ends, (turn_in, len(GROUPS)), (turn_pe, QUADS), (turn_act, QUADS),
                 (mm_pe, NK), (mm_act, NK), (tab_out, 16 * len(GROUPS)))

        sweep("sum", tab4_d, idx4_d, scale=True)

        q_pe = sem("q_pe"); q_act = sem("q_act"); rr_pe = sem("rr_pe"); rr_up = sem("rr_up")
        t8_pe = sem("t8_pe"); t8_act = sem("t8_act"); t8_h = sem("t8_h")
        t8_out = [sem(f"t8_out{s}") for s in range(4)]
        spread_out = sem("spread_out")
        t8buf = [PC[0:NP, 2048 + 1024 * s:2048 + 1024 * (s + 1)].rearrange("p (t f) -> p t f", t=R8) for s in range(4)]
        t8_in = sem("t8_in")
        qT = zT

        def scatter_rows(g):
            for q in range(QUADS):
                g.wait_ge(rr_up, at(rr_up, q + 1))
                for k in range(4 * q, min(4 * q + 4, NK)):
                    g.indirect_dma_start(spread_d, bass.IndirectOffsetOnAxis(ap=start_idx[:, k:k + 1], axis=0),
                                         rrows[:, k, :], None).then_inc(spread_out, 16)
            g.wait_ge(spread_out, at(spread_out, 16 * NK))

        with nc.Block() as block:
            @block.gpsimd
            def _(g):
                gather_ends(g)
                scatter_rows(g)

            @block.vector
            def _(v):
                L = dve_line

                def spread_and_copy(j):
                    for q, ks in quads(j):
                        v.wait_ge(rr_pe, q + 1)
                        v.tensor_copy(rrows[:, ks[0]:ks[-1] + 1, :],
                                      ps[4][0:NP, 0:len(ks) * RW].rearrange("p (k f) -> p k f", f=RW)).then_inc(rr_up, 1)
                        for k in ks:
                            if k >= 4:
                                v.wait_ge(t8_out[k % 4], 16 * (k // 4))
                            v.tensor_copy(t8buf[k % 4][:, :, D:2 * D], hn[:, k, :].unsqueeze(1).to_broadcast([NP, R8, D])
                                          ).then_inc(t8_h, 1)
                add_to_roots(v, 2)
                for j in ALL:
                    sl = slots(j)
                    ends_gathered(v, j)
                    L.step(v, v.tensor_tensor(gn[:, sl, :], gn[:, sl, :], rn[:, sl, :], ALU.add))
                    L.step(v, v.tensor_tensor(xn[:, sl, :], xn[:, sl, :], gn[:, sl, :], ALU.add))
                    if j:
                        spread_and_copy(j - 1)
                    norm_group(v, j)
                    v.sem_inc(turn_in, 1)
                spread_and_copy(ALL[-1])

            @block.tensor
            def _(pe):
                for j in ALL:
                    turn_group(pe, hn, j)
                    for q, ks in quads(j):
                        w = slice(4 * q * NP, (4 * q + len(ks)) * NP)
                        pe.wait_ge(turn_act, at(turn_act, q + 1))
                        pe.matmul(ps[3][0:D, 0:len(ks) * NP], wq[:, :], hT[:, w], start=True, stop=True).then_inc(q_pe, 1)
                        pe.wait_ge(q_act, q + 1)
                        if q:
                            pe.wait_ge(rr_up, q)
                        for k in ks:
                            last = pe.matmul(ps[4][0:NP, (k % 4) * RW:(k % 4 + 1) * RW], qT[:, k * NP:(k + 1) * NP], m2[:, :],
                                             start=True, stop=True)
                        last.then_inc(rr_pe, 1)
                        for k in ks:
                            if k >= 3:
                                pe.wait_ge(t8_act, k - 2)
                            pe.matmul(ps[5 + k % 3][0:NP, :], hT[:, k * NP:(k + 1) * NP],
                                      w2r[:, :, :].rearrange("d r e -> d (r e)"), start=True, stop=True).then_inc(t8_pe, 1)

            @block.scalar
            def _(a):
                for j in ALL:
                    sqrt_group(a, j)
                    copy_turned(a, hT, j)
                    for q, ks in quads(j):
                        w = slice(4 * q * NP, (4 * q + len(ks)) * NP)
                        a.wait_ge(q_pe, q + 1)
                        a.activation(qT[:, w], ps[3][0:D, 0:len(ks) * NP], ACT.Identity, bias=cols[:, 3:4]).then_inc(q_act, 1)
                        for k in ks:
                            if k >= 4:
                                a.wait_ge(t8_out[k % 4], 16 * (k // 4))
                            a.wait_ge(t8_pe, k + 1)
                            a.copy(t8buf[k % 4][:, :, 0:D], ps[5 + k % 3][0:NP, :].rearrange("p (t f) -> p t f", t=R8)
                                   ).then_inc(t8_act, 1)

            @block.sync
            def _(sp):
                first_indices(sp, idx8_d)
                sp.dma_start(em3(scal[:, :].bitcast(I32)), em(A["t8_it"])).then_inc(t8_in, 16)
                tv = tab8_d.rearrange("(t p k) f -> k p t f", t=R8, k=NK)
                for k in range(NK):
                    sp.wait_ge(t8_act, k + 1)
                    sp.wait_ge(t8_h, k + 1)
                    sp.dma_start(tv[k], t8buf[k % 4]).then_inc(t8_out[k % 4], 16)
                for s in range(4):
                    sp.wait_ge(t8_out[s], 16 * len(range(s, NK, 4)))
                sp.wait_ge(t8_in, 16)
        add_sent(*all_ends, (turn_in, len(GROUPS)), (turn_pe, QUADS), (turn_act, QUADS), (rr_up, QUADS),
                 (spread_out, 16 * NK), (sqrt_req, len(GROUPS)), (sqrt_done, len(GROUPS)))

        capp = PC[0:PQ, 0:PL // 2].bitcast(BF16)

        def piece_caps(v):
            L = dve_line
            L.step(v, v.tensor_scalar(pb, same_prev[:, :], 0.5, 2.0, ALU.subtract, ALU.mult))
            L.step(v, v.tensor_scalar(capp, pb, BIG, None, ALU.mult))
            L.step(v, v.tensor_scalar(small[0:PQ, 7, 0:1], small[0:PQ, 6, 3:4], BIG, None, ALU.mult))

        sweep("score", tab8_d, idx8_d, side={"vector": {1: piece_caps}})

        s_in = sem("s_in"); exp_req = sem("exp_req"); exp_done = sem("exp_done")
        with nc.Block() as block:
            a_, b_, c_ = (t_[0:PQ, 0:PL] for t_ in (PA, PB, PC))
            attrow = PB[0:PCS, 0:PL]

            @block.sync
            def _(sp):
                for r in range(4):
                    sp.dma_start(PA[r * PCS:(r + 1) * PCS, 0:PL], score_d[r].rearrange("(i f) -> i f", i=PCS)).then_inc(s_in, 16)

            @block.vector
            def _(v):
                L = dve_line
                v.wait_ge(s_in, 64)
                scan_pieces(v, b_, capp, small[0:PQ, 7, 0:1], a_, ALU.min, ALU.max, -BIG, False)
                L.step(v, v.tensor_tensor(b_, b_, last_of_run[:, :], ALU.mult))
                scan_pieces(v, c_, same_next, small[0:PQ, 6, 1:2], b_, ALU.mult, ALU.add, 0.0, True)
                L.step(v, v.tensor_tensor(a_, a_, c_, ALU.subtract))
                v.sem_inc(exp_req, 1)
                v.wait_ge(exp_done, 1)
                scan_pieces(v, b_, same_prev, small[0:PQ, 6, 0:1], a_, ALU.mult, ALU.add, 0.0, False)
                L.step(v, v.tensor_tensor(b_, b_, last_of_run[:, :], ALU.mult))
                scan_pieces(v, c_, same_next, small[0:PQ, 6, 1:2], b_, ALU.mult, ALU.add, 0.0, True)
                L.step(v, v.reciprocal(b_, c_))
                L.step(v, v.tensor_tensor(a_, a_, b_, ALU.mult))
                v.sem_inc(kinds_up, 1)
                edge_major_out(v, scal[:, :], 2)

            @block.tensor
            def _(pe):
                for j in range(4):
                    carry_pe(pe, 3 + j, j % 2 == 1)
                fold_pe(pe, pa, attrow, 2)

            @block.scalar
            def _(a):
                a.wait_ge(exp_req, 1)
                a.activation(a_, a_, ACT.Exp).then_inc(exp_done, 1)
                fold_act(a, attrow, 2, 0.25)

        sweep_messages()

        seam_in = sem("seam_in")
        seam = PC[0:NP, 2000:2000 + D]
        with nc.Block() as block:
            @block.gpsimd
            def _(g):
                gather_ends(g)
                scatter_rows(g)

            @block.vector
            def _(v):
                L = dve_line
                L.step(v, v.memset(rrows[:, :, D:RW], 0.0))

                def add_bias(j):
                    for q, ks in quads(j):
                        v.wait_ge(mm_act, at(mm_act, q + 1))
                        v.tensor_tensor(rrows[:, ks[0]:ks[-1] + 1, 0:D],
                                        ps[2 + q % 6][0:NP, 0:len(ks) * 2 * D].rearrange("p (k f) -> p k f", f=2 * D)[:, :, D:],
                                        rows[:, 6, :].unsqueeze(1).to_broadcast([NP, len(ks), D]), ALU.add).then_inc(mm_dve, 1)
                        v.wait_ge(mm_dve, q + 1)
                        v.sem_inc(rr_up, 1)
                for j in ALL:
                    sl = slots(j)
                    x, g, o = xn[:, sl, :], gn[:, sl, :], rn[:, sl, :]
                    if j == 0:
                        v.wait_ge(seam_in, 16)
                    L.step(v, v.tensor_tensor(o, over(seam, j), bcast(straddle[:, sl], D), ALU.mult))
                    L.step(v, v.tensor_tensor(o, o, over(rows[:, 3, :], j), ALU.add))
                    ends_gathered(v, j)
                    L.step(v, v.tensor_tensor(g, g, o, ALU.add))
                    layer_norm(v, gn, rn, j, 2 * j + 1)
                    L.step(v, v.tensor_tensor(o, o, over(rows[:, 4, :], j), ALU.mult))
                    L.step(v, v.tensor_tensor(o, o, over(rows[:, 5, :], j), ALU.add))
                    L.step(v, v.scalar_tensor_tensor(x, o, 0.0, x, ALU.max, ALU.add))
                    norm_group(v, j, 2 * j + 2)
                    v.sem_inc(turn_in, 1)
                    if j:
                        add_bias(j - 1)
                add_bias(ALL[-1])

            @block.tensor
            def _(pe):
                for j in ALL:
                    turn_group(pe, hn, j)
                    for q, ks in quads(j):
                        pe.wait_ge(turn_act, at(turn_act, q + 1))
                        if q == 6:
                            pe.wait_ge(mm_dve, 1)
                        for k in ks:
                            last = pe.matmul(ps[2 + q % 6][0:NP, (k % 4) * 2 * D:(k % 4 + 1) * 2 * D],
                                             hT[:, k * NP:(k + 1) * NP], w3t[:, :, :].rearrange("d r e -> d (r e)"),
                                             start=True, stop=True)
                        last.then_inc(mm_pe, 1)

            @block.scalar
            def _(a):
                for j in ALL:
                    sqrt_group(a, j, 2 * j + 1)
                    sqrt_group(a, j, 2 * j + 2)
                    copy_turned(a, hT, j)
                    for q, ks in quads(j):
                        a.wait_ge(mm_pe, at(mm_pe, q + 1))
                        a.copy(rn[:, ks[0]:ks[-1] + 1, :],
                               ps[2 + q % 6][0:NP, 0:len(ks) * 2 * D].rearrange("p (k f) -> p k f", f=2 * D)[:, :, 0:D]
                               ).then_inc(mm_act, 1)

            @block.sync
            def _(sp):
                first_indices(sp, A["src_it"])
                sp.dma_start(seam, row_bcast(scan_d[HALF * BLK - 1, :], NP, D)).then_inc(seam_in, 16)
                for j in ALL:
                    sp.wait_ge(mm_act, at(mm_act, quads(j)[-1][0] + 1))
                    sp.dma_start(node(tab_d)[:, slots(j), :], rn[:, slots(j), :]).then_inc(tab_out, 16)
                sp.wait_ge(tab_out, at(tab_out, 16 * len(GROUPS)))
        add_sent(*all_ends, (turn_in, len(GROUPS)), (turn_pe, QUADS), (turn_act, QUADS), (rr_up, QUADS),
                 (mm_pe, QUADS), (mm_dve, QUADS), (mm_act, QUADS), (tab_out, 16 * len(GROUPS)),
                 (spread_out, 16 * NK), (sqrt_req, 2 * len(GROUPS)), (sqrt_done, 2 * len(GROUPS)))

        sweep("max", tab_d, A["src_it"])

        with nc.Block() as block:
            @block.gpsimd
            def _(g):
                gather_ends(g)

            @block.vector
            def _(v):
                L = dve_line
                L.step(v, v.tensor_tensor(rn[:, :, :], rows[:, 7, :].unsqueeze(1).to_broadcast([NP, NK, D]),
                                          bcast(nonempty[:, :], D), ALU.mult))
                L.step(v, v.tensor_tensor(xn[:, :, :], xn[:, :, :], rn[:, :, :], ALU.add))
                for j in ALL:
                    sl = slots(j)
                    ends_gathered(v, j)
                    L.step(v, v.tensor_tensor(xn[:, sl, :], xn[:, sl, :], gn[:, sl, :], ALU.add))
                    v.sem_inc(group_up, 1)

            @block.sync
            def _(sp):
                store_groups(sp, out, xn)


_FLOATS = ['x', 'L0_gnn_W1', 'L0_gnn_b1', 'L0_gnn_gamma1', 'L0_gnn_beta1', 'L0_gnn_W2', 'L0_gnn_b2', 'L1_gnn_W1',
           'L1_gnn_root1', 'L1_gnn_b1', 'L1_gnn_W2', 'L1_gnn_root2', 'L1_gnn_b2', 'L2_gnn_W_r', 'L2_gnn_Wq_w',
           'L2_gnn_Wq_bias', 'L2_gnn_Wk_w', 'L2_gnn_Wk_bias', 'L2_gnn_rule_emb', 'L2_gnn_bias', 'L2_gnn_ln_g',
           'L2_gnn_ln_b', 'L3_gnn_W1', 'L3_gnn_b1', 'L3_gnn_W2', 'L3_gnn_b2']
_COLUMNS = ['L0_gnn_b1', 'L0_gnn_gamma1', 'L0_gnn_beta1', 'L2_gnn_Wq_bias', 'L2_gnn_Wk_bias']


def kernel(**inputs):
    import numpy as _np
    import concourse.bacc as _bacc
    from concourse import mybir as _mybir
    from concourse.bass_utils import run_bass_kernel_spmd as _run

    def padded(name, fill):
        a = _np.asarray(inputs[name])
        return _np.concatenate([a, _np.full(EP - E, fill, a.dtype)])

    def by_group(a):
        return _np.ascontiguousarray(a.reshape(NG, GRP, 128, CPB).transpose(0, 2, 1, 3).reshape(NG, 128, GC))

    host = {n: _np.ascontiguousarray(inputs[n]) for n in _FLOATS}
    for n in _COLUMNS:
        host[n] = host[n].reshape(D, 1)
    dst = padded("dst", N)
    none = _np.full(1, -1, dst.dtype)
    host["dst_ext"] = _np.concatenate([none, dst, none])
    host["dst_rows"] = dst.reshape(HEADS, 128)
    host["dst_heads"] = _np.ascontiguousarray(dst[::128])
    host["src_it"] = by_group(padded("src", 0))
    t4, t8 = padded("edge_type_4", 0), padded("edge_type_8", 0)
    host["t4_nat"] = t4
    host["t4_it"] = by_group(t4)
    host["t8_it"] = by_group(t8)
    host["rule_ids"] = _np.asarray(inputs["L2_gnn_rule_ids"]).reshape(4, 1)

    nc = _bacc.Bacc("TRN2", target_bir_lowering=False, num_devices=1)
    arrays = {f"in_{n}": a for n, a in host.items()}
    A = {n: nc.dram_tensor(f"in_{n}", a.shape, _mybir.dt.from_np(a.dtype), kind="ExternalInput").ap()
         for n, a in host.items()}
    out = nc.dram_tensor("out", (N, D), F32, kind="ExternalOutput").ap()
    build(nc, A, out)
    r = _run(nc, [arrays], core_ids=[0])
    return r.results[0]["out"]
```
